# Optimizing a Trainium2 kernel written in Bass

```python
import numpy as np
import jax
import jax.numpy as jnp

def _softmax(x, axis=-1):
    return jax.nn.softmax(x, axis=axis)

def _gelu(x):
    return jax.nn.gelu(x, approximate=True)

def _silu(x):
    return jax.nn.silu(x)

def _sigmoid(x):
    return jax.nn.sigmoid(x)

def _layernorm(x, axis=-1, eps=1e-05):
    m = jnp.mean(x, axis=axis, keepdims=True)
    v = jnp.var(x, axis=axis, keepdims=True)
    return (x - m) / jnp.sqrt(v + eps)

def _scatter_add(tgt, idx, src, axis=0):
    return tgt.at[idx].add(src)

def _segment_sum(src, seg, n):
    return jax.ops.segment_sum(src, seg, n)
kernel_name = 'mk_flamingo_gated_d4_seqx_r8_9c19eb'

def setup_inputs(seed: int=0):
    np.random.seed(seed)
    _w = jnp.asarray

    def _rec_inputs():
        import jax
        import jax.numpy as jnp
        _rk = jax.random.key(seed)
        x = -0.0002928 + 1 * jax.random.normal(jax.random.fold_in(_rk, 1), (8, 128, 128), jnp.float32)
        _lenS = 128 - jax.random.randint(jax.random.fold_in(_rk, 7), (8,), 0, max(1, 128 // 4) + 1, jnp.int32)
        _lenS2 = 77 - jax.random.randint(jax.random.fold_in(_rk, 8), (8,), 0, max(1, 77 // 4) + 1, jnp.int32)
        _ctx_1024P = jax.random.normal(jax.random.fold_in(_rk, 11), (8, 16, 128), jnp.float32)
        _ctx_1024c = jax.random.dirichlet(jax.random.fold_in(_rk, 511), 0.3 * jnp.ones((16,), jnp.float32), (8, 77))
        _ctx_1024t = jnp.einsum('bsk,bkd->bsd', _ctx_1024c, _ctx_1024P)
        _ctx_1024t = _ctx_1024t * jax.lax.rsqrt(jnp.mean(jnp.square(_ctx_1024t)) + 1e-12) * 0.953939
        ctx_1024 = -1.39393e-06 + 0.999914 * (_ctx_1024t + 0.3 * jax.random.normal(jax.random.fold_in(_rk, 611), (8, 77, 128), jnp.float32))
        fside_Bx16xSxS2_0 = 9.80324e-06 + 0.100009 * jax.random.normal(jax.random.fold_in(_rk, 12), (8, 16, 128, 77), jnp.float32)
        fside_SxS2_0 = -2.64403e-05 + 0.100002 * jax.random.normal(jax.random.fold_in(_rk, 14), (128, 77), jnp.float32)
        _validS = jnp.arange(128)[None, :] < _lenS[:, None]
        _validS2 = jnp.arange(77)[None, :] < _lenS2[:, None]
        _causal = jnp.tril(jnp.ones((128, 128), dtype=bool))
        mask_BxS2_bf0 = jnp.logical_not(jnp.ones((8, 77), dtype=bool))
        mask_BxS2_bk1 = jnp.broadcast_to(_validS2[:, :], (8, 77))
        _g = jax.random.normal(jax.random.fold_in(_rk, 9001), (2, 4), jnp.float32)
        _g = jnp.sign(_g) * jnp.maximum(jnp.abs(_g), 1.0) + (_g == 0) * 1.0
        g_xattn = _g[0]
        g_ffn = _g[1]
        return (x, ctx_1024, fside_Bx16xSxS2_0, fside_SxS2_0, mask_BxS2_bf0, mask_BxS2_bk1, g_xattn, g_ffn)
    x, ctx_1024, fside_Bx16xSxS2_0, fside_SxS2_0, mask_BxS2_bf0, mask_BxS2_bk1, g_xattn, g_ffn = _rec_inputs()

    def _L0_xattn_setup():
        import jax, jax.numpy as jnp
        import numpy as np
        D_MODEL = 128
        N_HEADS = 16
        HEAD_DIM = D_MODEL // N_HEADS

        def sparsemax(x):
            x = x - jnp.max(x, axis=-1, keepdims=True)
            zs = -jnp.sort(-x, axis=-1)
            L = x.shape[-1]
            rho = jnp.arange(1, L + 1, dtype=x.dtype)
            cssv = jnp.cumsum(zs, axis=-1) - 1.0
            support = zs > cssv / rho
            k = jnp.maximum(jnp.sum(support, axis=-1, keepdims=True), 1)
            tau = jnp.take_along_axis(cssv, k - 1, axis=-1) / k.astype(x.dtype)
            return jnp.clip(x - tau, 0.0)

        def _split_heads(x):
            B, L, _ = x.shape
            return x.reshape(B, L, N_HEADS, HEAD_DIM).transpose(0, 2, 1, 3)
        key = jax.random.key(seed)
        ks = jax.random.split(key, 11)
        B, L = (2, 256)
        s = 0.02
        inp = {'q': jax.random.normal(ks[0], (B, L, D_MODEL), jnp.float32), 'k': jax.random.normal(ks[1], (B, L, D_MODEL), jnp.float32), 'v': jax.random.normal(ks[2], (B, L, D_MODEL), jnp.float32), 'Wq': jax.random.normal(ks[3], (D_MODEL, D_MODEL), jnp.float32) * s, 'bq': jnp.zeros((D_MODEL,), jnp.float32), 'Wk': jax.random.normal(ks[4], (D_MODEL, D_MODEL), jnp.float32) * s, 'bk': jnp.zeros((D_MODEL,), jnp.float32), 'Wv': jax.random.normal(ks[5], (D_MODEL, D_MODEL), jnp.float32) * s, 'bv': jnp.zeros((D_MODEL,), jnp.float32), 'Wo': jax.random.normal(ks[6], (D_MODEL, D_MODEL), jnp.float32) * s, 'bo': jnp.zeros((D_MODEL,), jnp.float32)}
        return inp
    _L0_xattn_all = _L0_xattn_setup()
    _L0_xattn_in = {k: v for k, v in _L0_xattn_all.items() if k in ('Wq', 'bq', 'Wk', 'bk', 'Wv', 'bv', 'Wo', 'bo')}
    del _L0_xattn_all

    def _L0_ffn_setup():
        import jax, jax.numpy as jnp
        import numpy as np
        B, S, H, I = (2, 256, 128, 352)
        NUM_EXPERTS = 8
        NUM_SHARED = 1
        E_ROUTED = NUM_EXPERTS - NUM_SHARED
        TOP_K = 2

        def _mlp(x, gate_w, up_w, down_w):
            return jax.nn.silu(x @ gate_w) * (x @ up_w) @ down_w
        key = jax.random.key(seed)
        ks = jax.random.split(key, 9)
        scale = 0.02
        return {'x': jax.random.normal(ks[0], (B, S, H), jnp.float32), 'router_w': jax.random.normal(ks[1], (H, E_ROUTED), jnp.float32) * scale, 'routing_bias': jnp.zeros((E_ROUTED,), jnp.float32), 'shared_gate': jax.random.normal(ks[2], (H, I), jnp.float32) * scale, 'shared_up': jax.random.normal(ks[3], (H, I), jnp.float32) * scale, 'shared_down': jax.random.normal(ks[4], (I, H), jnp.float32) * scale, 'routed_gate': jax.random.normal(ks[5], (E_ROUTED, H, I), jnp.float32) * scale, 'routed_up': jax.random.normal(ks[6], (E_ROUTED, H, I), jnp.float32) * scale, 'routed_down': jax.random.normal(ks[7], (E_ROUTED, I, H), jnp.float32) * scale}
    _L0_ffn_all = _L0_ffn_setup()
    _L0_ffn_in = {k: v for k, v in _L0_ffn_all.items() if k in ('router_w', 'routing_bias', 'shared_gate', 'shared_up', 'shared_down', 'routed_gate', 'routed_up', 'routed_down')}
    del _L0_ffn_all

    def _L1_xattn_setup():
        import jax, jax.numpy as jnp
        import numpy as np
        E = 128
        H = 16
        D = E // H
        key = jax.random.key(seed)
        ks = jax.random.split(key, 12)
        B, T, S = (2, 256, 256)
        inp = {'query': jax.random.normal(ks[0], (B, T, E), jnp.float32), 'key': jax.random.normal(ks[1], (B, S, E), jnp.float32), 'value': jax.random.normal(ks[2], (B, S, E), jnp.float32), 'spatial_bias': jax.random.normal(ks[3], (B, H, T, S), jnp.float32) * 0.1, 'directional_bias': jax.random.normal(ks[4], (B, H, T, S), jnp.float32) * 0.1, 'key_padding_mask': jnp.zeros((B, S), dtype=bool), 'attn_mask': jax.random.normal(ks[5], (T, S), jnp.float32) * 0.1, 'Wq': jax.random.normal(ks[6], (E, E), jnp.float32) / np.sqrt(E), 'bq': jnp.zeros((E,), jnp.float32), 'Wk': jax.random.normal(ks[7], (E, E), jnp.float32) / np.sqrt(E), 'bk': jnp.zeros((E,), jnp.float32), 'Wv': jax.random.normal(ks[8], (E, E), jnp.float32) / np.sqrt(E), 'bv': jnp.zeros((E,), jnp.float32), 'Wo': jax.random.normal(ks[9], (E, E), jnp.float32) / np.sqrt(E), 'bo': jnp.zeros((E,), jnp.float32)}
        return inp
    _L1_xattn_all = _L1_xattn_setup()
    _L1_xattn_in = {k: v for k, v in _L1_xattn_all.items() if k in ('Wq', 'bq', 'Wk', 'bk', 'Wv', 'bv', 'Wo', 'bo')}
    del _L1_xattn_all

    def _L1_ffn_setup():
        import jax, jax.numpy as jnp
        import numpy as np
        ALPHA = 2.0
        TOP_K = 2
        key = jax.random.key(seed)
        ks = jax.random.split(key, 8)
        B, S, D, H, E = (2, 256, 128, 512, 8)
        Er = E - 1
        s_in = 1.0 / np.sqrt(D)
        s_hid = 1.0 / np.sqrt(H)
        return {'x': jax.random.normal(ks[0], (B, S, D), dtype=jnp.float32), 'router_w': jax.random.normal(ks[1], (D, E), dtype=jnp.float32) * s_in, 'up_w': jax.random.normal(ks[2], (Er, D, H), dtype=jnp.float32) * s_in, 'gate_w': jax.random.normal(ks[3], (Er, D, H), dtype=jnp.float32) * s_in, 'down_w': jax.random.normal(ks[4], (Er, H, D), dtype=jnp.float32) * s_hid * 0.1, 'shared_up_w': jax.random.normal(ks[5], (D, H), dtype=jnp.float32) * s_in, 'shared_gate_w': jax.random.normal(ks[6], (D, H), dtype=jnp.float32) * s_in, 'shared_down_w': jax.random.normal(ks[7], (H, D), dtype=jnp.float32) * s_hid * 0.1}
    _L1_ffn_all = _L1_ffn_setup()
    _L1_ffn_in = {k: v for k, v in _L1_ffn_all.items() if k in ('router_w', 'up_w', 'gate_w', 'down_w', 'shared_up_w', 'shared_gate_w', 'shared_down_w')}
    del _L1_ffn_all

    def _L2_xattn_setup():
        import jax, jax.numpy as jnp
        import numpy as np
        DIM = 128
        NUM_HEADS = 16
        DIM_HEAD = 64
        INNER = NUM_HEADS * DIM_HEAD
        SCALE = DIM_HEAD ** (-0.5)

        def _layernorm(x, gamma, beta, eps=1e-05):
            mu = jnp.mean(x, axis=-1, keepdims=True)
            var = jnp.mean(jnp.square(x - mu), axis=-1, keepdims=True)
            return (x - mu) * jax.lax.rsqrt(var + eps) * gamma + beta
        key = jax.random.key(seed)
        ks = jax.random.split(key, 8)
        B, SQ, SK = (2, 256, 512)
        x = jax.random.normal(ks[0], (B, SQ, DIM), dtype=jnp.float32)
        context = jax.random.normal(ks[1], (B, SK, DIM), dtype=jnp.float32)
        ln_gamma = jnp.ones((DIM,), jnp.float32)
        ln_beta = jnp.zeros((DIM,), jnp.float32)
        w_q = jax.random.normal(ks[2], (DIM, INNER), dtype=jnp.float32) / np.sqrt(DIM)
        w_kv = jax.random.normal(ks[3], (DIM, 2 * INNER), dtype=jnp.float32) / np.sqrt(DIM)
        w_out = jax.random.normal(ks[4], (INNER, DIM), dtype=jnp.float32) / np.sqrt(INNER)
        b_out = jnp.zeros((DIM,), jnp.float32)
        gate = jnp.array([0.5], jnp.float32)
        return {'x': x, 'context': context, 'ln_gamma': ln_gamma, 'ln_beta': ln_beta, 'w_q': w_q, 'w_kv': w_kv, 'w_out': w_out, 'b_out': b_out, 'gate': gate}
    _L2_xattn_all = _L2_xattn_setup()
    _L2_xattn_in = {k: v for k, v in _L2_xattn_all.items() if k in ('ln_gamma', 'ln_beta', 'w_q', 'w_kv', 'w_out', 'b_out', 'gate')}
    del _L2_xattn_all

    def _L2_ffn_setup():
        import jax, jax.numpy as jnp
        import numpy as np
        D_MODEL, D_FF, N_EXPERTS, TOP_K = (128, 256, 8, 2)
        B, S = (2, 256)
        key = jax.random.key(seed)
        ks = jax.random.split(key, 6)
        sd = 1.0 / np.sqrt(D_MODEL)
        sf = 1.0 / np.sqrt(D_FF)
        return {'x': jax.random.normal(ks[0], (B, S, D_MODEL), jnp.float32), 'router_w': jax.random.normal(ks[1], (N_EXPERTS, D_MODEL), jnp.float32) * sd, 'gate_w': jax.random.normal(ks[2], (N_EXPERTS, D_MODEL, D_FF), jnp.float32) * sd, 'gate_b': jnp.zeros((N_EXPERTS, D_FF), jnp.float32), 'up_w': jax.random.normal(ks[3], (N_EXPERTS, D_MODEL, D_FF), jnp.float32) * sd, 'up_b': jnp.zeros((N_EXPERTS, D_FF), jnp.float32), 'down_w': jax.random.normal(ks[4], (N_EXPERTS, D_FF, D_MODEL), jnp.float32) * sf, 'down_b': jnp.zeros((N_EXPERTS, D_MODEL), jnp.float32)}
    _L2_ffn_all = _L2_ffn_setup()
    _L2_ffn_in = {k: v for k, v in _L2_ffn_all.items() if k in ('router_w', 'gate_w', 'gate_b', 'up_w', 'up_b', 'down_w', 'down_b')}
    del _L2_ffn_all

    def _L3_xattn_setup():
        import jax, jax.numpy as jnp
        import numpy as np
        DIM = 128
        DIM_HEAD = 64
        HEADS = 8
        INNER = DIM_HEAD * HEADS
        EPS = 1e-05

        def layernorm(x, g, b):
            mu = jnp.mean(x, axis=-1, keepdims=True)
            var = jnp.var(x, axis=-1, keepdims=True)
            return (x - mu) * jax.lax.rsqrt(var + EPS) * g + b
        key = jax.random.key(seed)
        ks = jax.random.split(key, 8)
        b, n, m = (8, 512, 64)
        x = jax.random.normal(ks[0], (b, n, DIM), dtype=jnp.float32)
        latents = jax.random.normal(ks[1], (b, m, DIM), dtype=jnp.float32)
        mask = jax.random.bernoulli(ks[2], 0.9, (b, n))
        s = DIM ** (-0.5)
        Wq = jax.random.normal(ks[3], (DIM, INNER), dtype=jnp.float32) * s
        Wkv = jax.random.normal(ks[4], (DIM, 2 * INNER), dtype=jnp.float32) * s
        Wo = jax.random.normal(ks[5], (INNER, DIM), dtype=jnp.float32) * INNER ** (-0.5)
        ln_x_g = jnp.ones((DIM,), jnp.float32)
        ln_x_b = jnp.zeros((DIM,), jnp.float32)
        ln_l_g = jnp.ones((DIM,), jnp.float32)
        ln_l_b = jnp.zeros((DIM,), jnp.float32)
        ln_o_g = jnp.ones((DIM,), jnp.float32)
        ln_o_b = jnp.zeros((DIM,), jnp.float32)
        return {'x': x, 'latents': latents, 'mask': mask, 'Wq': Wq, 'Wkv': Wkv, 'Wo': Wo, 'ln_x_g': ln_x_g, 'ln_x_b': ln_x_b, 'ln_l_g': ln_l_g, 'ln_l_b': ln_l_b, 'ln_o_g': ln_o_g, 'ln_o_b': ln_o_b}
    _L3_xattn_all = _L3_xattn_setup()
    _L3_xattn_in = {k: v for k, v in _L3_xattn_all.items() if k in ('Wq', 'Wkv', 'Wo', 'ln_x_g', 'ln_x_b', 'ln_l_g', 'ln_l_b', 'ln_o_g', 'ln_o_b')}
    del _L3_xattn_all

    def _L3_ffn_setup():
        import jax, jax.numpy as jnp
        import numpy as np
        N_EMBD = 128
        NUM_EXPERTS = 8
        TOP_K = 2
        D_FF = 4 * N_EMBD
        B, S = (4, 256)
        key = jax.random.key(seed)
        ks = jax.random.split(key, 7)
        scale = lambda fan_in: 1.0 / np.sqrt(fan_in)
        x = jax.random.normal(ks[0], (B, S, N_EMBD), dtype=jnp.float32)
        W_router = jax.random.normal(ks[1], (N_EMBD, NUM_EXPERTS), dtype=jnp.float32) * scale(N_EMBD)
        b_router = jnp.zeros((NUM_EXPERTS,), dtype=jnp.float32)
        W1 = jax.random.normal(ks[2], (NUM_EXPERTS, N_EMBD, D_FF), dtype=jnp.float32) * scale(N_EMBD)
        b1 = jnp.zeros((NUM_EXPERTS, D_FF), dtype=jnp.float32)
        W2 = jax.random.normal(ks[3], (NUM_EXPERTS, D_FF, N_EMBD), dtype=jnp.float32) * scale(D_FF)
        b2 = jnpp = jnp.zeros((NUM_EXPERTS, N_EMBD), dtype=jnp.float32)
        return {'x': x, 'W_router': W_router, 'b_router': b_router, 'W1': W1, 'b1': b1, 'W2': W2, 'b2': b2}
    _L3_ffn_all = _L3_ffn_setup()
    _L3_ffn_in = {k: v for k, v in _L3_ffn_all.items() if k in ('W_router', 'b_router', 'W1', 'b1', 'W2', 'b2')}
    del _L3_ffn_all
    return {'x': x, 'ctx_1024': ctx_1024, 'fside_Bx16xSxS2_0': fside_Bx16xSxS2_0, 'fside_SxS2_0': fside_SxS2_0, 'mask_BxS2_bf0': mask_BxS2_bf0, 'mask_BxS2_bk1': mask_BxS2_bk1, 'g_xattn': g_xattn, 'g_ffn': g_ffn, 'L0_xattn_Wq': _L0_xattn_in['Wq'], 'L0_xattn_bq': _L0_xattn_in['bq'], 'L0_xattn_Wk': _L0_xattn_in['Wk'], 'L0_xattn_bk': _L0_xattn_in['bk'], 'L0_xattn_Wv': _L0_xattn_in['Wv'], 'L0_xattn_bv': _L0_xattn_in['bv'], 'L0_xattn_Wo': _L0_xattn_in['Wo'], 'L0_xattn_bo': _L0_xattn_in['bo'], 'L0_ffn_router_w': _L0_ffn_in['router_w'], 'L0_ffn_routing_bias': _L0_ffn_in['routing_bias'], 'L0_ffn_shared_gate': _L0_ffn_in['shared_gate'], 'L0_ffn_shared_up': _L0_ffn_in['shared_up'], 'L0_ffn_shared_down': _L0_ffn_in['shared_down'], 'L0_ffn_routed_gate': _L0_ffn_in['routed_gate'], 'L0_ffn_routed_up': _L0_ffn_in['routed_up'], 'L0_ffn_routed_down': _L0_ffn_in['routed_down'], 'L1_xattn_Wq': _L1_xattn_in['Wq'], 'L1_xattn_bq': _L1_xattn_in['bq'], 'L1_xattn_Wk': _L1_xattn_in['Wk'], 'L1_xattn_bk': _L1_xattn_in['bk'], 'L1_xattn_Wv': _L1_xattn_in['Wv'], 'L1_xattn_bv': _L1_xattn_in['bv'], 'L1_xattn_Wo': _L1_xattn_in['Wo'], 'L1_xattn_bo': _L1_xattn_in['bo'], 'L1_ffn_router_w': _L1_ffn_in['router_w'], 'L1_ffn_up_w': _L1_ffn_in['up_w'], 'L1_ffn_gate_w': _L1_ffn_in['gate_w'], 'L1_ffn_down_w': _L1_ffn_in['down_w'], 'L1_ffn_shared_up_w': _L1_ffn_in['shared_up_w'], 'L1_ffn_shared_gate_w': _L1_ffn_in['shared_gate_w'], 'L1_ffn_shared_down_w': _L1_ffn_in['shared_down_w'], 'L2_xattn_ln_gamma': _L2_xattn_in['ln_gamma'], 'L2_xattn_ln_beta': _L2_xattn_in['ln_beta'], 'L2_xattn_w_q': _L2_xattn_in['w_q'], 'L2_xattn_w_kv': _L2_xattn_in['w_kv'], 'L2_xattn_w_out': _L2_xattn_in['w_out'], 'L2_xattn_b_out': _L2_xattn_in['b_out'], 'L2_xattn_gate': _L2_xattn_in['gate'], 'L2_ffn_router_w': _L2_ffn_in['router_w'], 'L2_ffn_gate_w': _L2_ffn_in['gate_w'], 'L2_ffn_gate_b': _L2_ffn_in['gate_b'], 'L2_ffn_up_w': _L2_ffn_in['up_w'], 'L2_ffn_up_b': _L2_ffn_in['up_b'], 'L2_ffn_down_w': _L2_ffn_in['down_w'], 'L2_ffn_down_b': _L2_ffn_in['down_b'], 'L3_xattn_Wq': _L3_xattn_in['Wq'], 'L3_xattn_Wkv': _L3_xattn_in['Wkv'], 'L3_xattn_Wo': _L3_xattn_in['Wo'], 'L3_xattn_ln_x_g': _L3_xattn_in['ln_x_g'], 'L3_xattn_ln_x_b': _L3_xattn_in['ln_x_b'], 'L3_xattn_ln_l_g': _L3_xattn_in['ln_l_g'], 'L3_xattn_ln_l_b': _L3_xattn_in['ln_l_b'], 'L3_xattn_ln_o_g': _L3_xattn_in['ln_o_g'], 'L3_xattn_ln_o_b': _L3_xattn_in['ln_o_b'], 'L3_ffn_W_router': _L3_ffn_in['W_router'], 'L3_ffn_b_router': _L3_ffn_in['b_router'], 'L3_ffn_W1': _L3_ffn_in['W1'], 'L3_ffn_b1': _L3_ffn_in['b1'], 'L3_ffn_W2': _L3_ffn_in['W2'], 'L3_ffn_b2': _L3_ffn_in['b2']}

def reference(x, ctx_1024, fside_Bx16xSxS2_0, fside_SxS2_0, mask_BxS2_bf0, mask_BxS2_bk1, g_xattn, g_ffn, L0_xattn_Wq, L0_xattn_bq, L0_xattn_Wk, L0_xattn_bk, L0_xattn_Wv, L0_xattn_bv, L0_xattn_Wo, L0_xattn_bo, L0_ffn_router_w, L0_ffn_routing_bias, L0_ffn_shared_gate, L0_ffn_shared_up, L0_ffn_shared_down, L0_ffn_routed_gate, L0_ffn_routed_up, L0_ffn_routed_down, L1_xattn_Wq, L1_xattn_bq, L1_xattn_Wk, L1_xattn_bk, L1_xattn_Wv, L1_xattn_bv, L1_xattn_Wo, L1_xattn_bo, L1_ffn_router_w, L1_ffn_up_w, L1_ffn_gate_w, L1_ffn_down_w, L1_ffn_shared_up_w, L1_ffn_shared_gate_w, L1_ffn_shared_down_w, L2_xattn_ln_gamma, L2_xattn_ln_beta, L2_xattn_w_q, L2_xattn_w_kv, L2_xattn_w_out, L2_xattn_b_out, L2_xattn_gate, L2_ffn_router_w, L2_ffn_gate_w, L2_ffn_gate_b, L2_ffn_up_w, L2_ffn_up_b, L2_ffn_down_w, L2_ffn_down_b, L3_xattn_Wq, L3_xattn_Wkv, L3_xattn_Wo, L3_xattn_ln_x_g, L3_xattn_ln_x_b, L3_xattn_ln_l_g, L3_xattn_ln_l_b, L3_xattn_ln_o_g, L3_xattn_ln_o_b, L3_ffn_W_router, L3_ffn_b_router, L3_ffn_W1, L3_ffn_b1, L3_ffn_W2, L3_ffn_b2):
    import jax
    import jax.numpy as jnp

    def _L0_xattn_ref(q, k, v, Wq, bq, Wk, bk, Wv, bv, Wo, bo):
        import jax, jax.numpy as jnp
        import numpy as np
        D_MODEL = 128
        N_HEADS = 16
        HEAD_DIM = D_MODEL // N_HEADS

        def sparsemax(x):
            x = x - jnp.max(x, axis=-1, keepdims=True)
            zs = -jnp.sort(-x, axis=-1)
            L = x.shape[-1]
            rho = jnp.arange(1, L + 1, dtype=x.dtype)
            cssv = jnp.cumsum(zs, axis=-1) - 1.0
            support = zs > cssv / rho
            k = jnp.maximum(jnp.sum(support, axis=-1, keepdims=True), 1)
            tau = jnp.take_along_axis(cssv, k - 1, axis=-1) / k.astype(x.dtype)
            return jnp.clip(x - tau, 0.0)

        def _split_heads(x):
            B, L, _ = x.shape
            return x.reshape(B, L, N_HEADS, HEAD_DIM).transpose(0, 2, 1, 3)
        qh = _split_heads(q @ Wq + bq)
        kh = _split_heads(k @ Wk + bk)
        vh = _split_heads(v @ Wv + bv)
        scale = HEAD_DIM ** (-0.5)
        scores = jnp.einsum('bhqd,bhkd->bhqk', qh, kh) * scale
        attn = sparsemax(scores)
        out = jnp.einsum('bhqk,bhkd->bhqd', attn, vh)
        B, L = (q.shape[0], q.shape[1])
        out = out.transpose(0, 2, 1, 3).reshape(B, L, D_MODEL)
        return out @ Wo + bo

    def _L0_ffn_ref(x, router_w, routing_bias, shared_gate, shared_up, shared_down, routed_gate, routed_up, routed_down):
        import jax, jax.numpy as jnp
        import numpy as np
        B, S, H, I = (2, 256, 128, 352)
        NUM_EXPERTS = 8
        NUM_SHARED = 1
        E_ROUTED = NUM_EXPERTS - NUM_SHARED
        TOP_K = 2

        def _mlp(x, gate_w, up_w, down_w):
            return jax.nn.silu(x @ gate_w) * (x @ up_w) @ down_w
        e_routed = routed_gate.shape[0]
        shared_out = _mlp(x, shared_gate, shared_up, shared_down)
        routing_logits = x @ router_w + routing_bias
        routing_probs = jax.nn.sigmoid(routing_logits)
        scores, indices = jax.lax.top_k(routing_probs, TOP_K)
        scores = scores / scores.sum(axis=-1, keepdims=True)
        onehot = jax.nn.one_hot(indices, e_routed, dtype=x.dtype)
        combine = jnp.einsum('bsk,bske->bse', scores, onehot)
        out = shared_out
        for e in range(e_routed):
            expert_out = _mlp(x, routed_gate[e], routed_up[e], routed_down[e])
            out = out + combine[..., e:e + 1] * expert_out
        return out

    def _L1_xattn_ref(query, key, value, spatial_bias, directional_bias, key_padding_mask, attn_mask, Wq, bq, Wk, bk, Wv, bv, Wo, bo):
        import jax, jax.numpy as jnp
        import numpy as np
        E = 128
        H = 16
        D = E // H
        B, T, _ = query.shape
        S = key.shape[1]
        scale = D ** (-0.5)
        q = (query @ Wq.T + bq).reshape(B, T, H, D).transpose(0, 2, 1, 3)
        k = (key @ Wk.T + bk).reshape(B, S, H, D).transpose(0, 2, 1, 3)
        v = (value @ Wv.T + bv).reshape(B, S, H, D).transpose(0, 2, 1, 3)
        scores = jnp.einsum('bhtd,bhsd->bhts', q, k) * scale
        scores = scores + attn_mask[None, None, :, :]
        pad = key_padding_mask[:, None, None, :]
        scores = jnp.where(pad, -jnp.inf, scores)
        if T == S:
            scores = scores + spatial_bias + directional_bias
        probs = jax.nn.softmax(scores, axis=-1)
        out = jnp.einsum('bhts,bhsd->bhtd', probs, v)
        out = out.transpose(0, 2, 1, 3).reshape(B, T, E)
        return out @ Wo.T + bo

    def _L1_ffn_ref(x, router_w, up_w, gate_w, down_w, shared_up_w, shared_gate_w, shared_down_w):
        import jax, jax.numpy as jnp
        import numpy as np
        ALPHA = 2.0
        TOP_K = 2
        logits = jnp.einsum('bsd,de->bse', x, router_w)
        probs = jax.nn.softmax(logits, axis=-1)
        topk_vals, topk_idx = jax.lax.top_k(probs, TOP_K)
        top1_val = topk_vals[..., 0]
        top1_idx = topk_idx[..., 0]
        hid = jnp.einsum('bsd,edh->ebsh', x, up_w) * jax.nn.silu(jnp.einsum('bsd,edh->ebsh', x, gate_w))
        Er = up_w.shape[0]
        mask = (top1_idx[None, :, :] == jnp.arange(Er)[:, None, None]).astype(x.dtype)
        routed = jnp.einsum('ebsh,ehd,ebs->bsd', hid, down_w, mask)
        shid = jnp.einsum('bsd,dh->bsh', x, shared_up_w) * jax.nn.silu(jnp.einsum('bsd,dh->bsh', x, shared_gate_w))
        shared = jnp.einsum('bsh,hd->bsd', shid, shared_down_w)
        return ALPHA * top1_val[..., None] * routed + shared

    def _L2_xattn_ref(x, context, ln_gamma, ln_beta, w_q, w_kv, w_out, b_out, gate):
        import jax, jax.numpy as jnp
        import numpy as np
        DIM = 128
        NUM_HEADS = 16
        DIM_HEAD = 64
        INNER = NUM_HEADS * DIM_HEAD
        SCALE = DIM_HEAD ** (-0.5)

        def _layernorm(x, gamma, beta, eps=1e-05):
            mu = jnp.mean(x, axis=-1, keepdims=True)
            var = jnp.mean(jnp.square(x - mu), axis=-1, keepdims=True)
            return (x - mu) * jax.lax.rsqrt(var + eps) * gamma + beta
        B, SQ, _ = x.shape
        SK = context.shape[1]
        xn = _layernorm(x, ln_gamma, ln_beta)
        q = (xn @ w_q).reshape(B, SQ, NUM_HEADS, DIM_HEAD)
        kv = context @ w_kv
        k, v = jnp.split(kv, 2, axis=-1)
        k = k.reshape(B, SK, NUM_HEADS, DIM_HEAD)
        v = v.reshape(B, SK, NUM_HEADS, DIM_HEAD)
        scores = jnp.einsum('bqhd,bkhd->bhqk', q * SCALE, k)
        attn = jax.nn.softmax(scores, axis=-1)
        out = jnp.einsum('bhqk,bkhd->bqhd', attn, v).reshape(B, SQ, INNER)
        out = out @ w_out + b_out
        return out * jnp.tanh(gate[0])

    def _L2_ffn_ref(x, router_w, gate_w, gate_b, up_w, up_b, down_w, down_b):
        import jax, jax.numpy as jnp
        import numpy as np
        D_MODEL, D_FF, N_EXPERTS, TOP_K = (128, 256, 8, 2)
        B, S = (2, 256)
        b, s, d = x.shape
        xf = x.reshape(b * s, d)
        n = xf.shape[0]
        router_logits = xf @ router_w.T
        probs = jax.nn.softmax(router_logits, axis=-1)
        topv, topi = jax.lax.top_k(probs, TOP_K)
        mask = jnp.zeros_like(probs).at[jnp.arange(n)[:, None], topi].set(1.0)
        probs = probs * mask
        probs = probs / (probs.sum(axis=-1, keepdims=True) + 1e-09)
        g = jnp.einsum('nd,edf->nef', xf, gate_w) + gate_b
        u = jnp.einsum('nd,edf->nef', xf, up_w) + up_b
        h = jax.nn.silu(g) * u
        expert_out = jnp.einsum('nef,efd->ned', h, down_w) + down_b
        y = jnp.einsum('ne,ned->nd', probs, expert_out)
        return y.reshape(b, s, d)

    def _L3_xattn_ref(x, latents, mask, Wq, Wkv, Wo, ln_x_g, ln_x_b, ln_l_g, ln_l_b, ln_o_g, ln_o_b):
        import jax, jax.numpy as jnp
        import numpy as np
        DIM = 128
        DIM_HEAD = 64
        HEADS = 8
        INNER = DIM_HEAD * HEADS
        EPS = 1e-05

        def layernorm(x, g, b):
            mu = jnp.mean(x, axis=-1, keepdims=True)
            var = jnp.var(x, axis=-1, keepdims=True)
            return (x - mu) * jax.lax.rsqrt(var + EPS) * g + b
        scale = DIM_HEAD ** (-0.5)
        b, m = (latents.shape[0], latents.shape[1])
        xn = layernorm(x, ln_x_g, ln_x_b)
        ln = layernorm(latents, ln_l_g, ln_l_b)
        q = ln @ Wq
        kv_in = jnp.concatenate([xn, ln], axis=1)
        kv = kv_in @ Wkv
        k, v = jnp.split(kv, 2, axis=-1)
        q = q.reshape(b, m, HEADS, DIM_HEAD).transpose(0, 2, 1, 3)
        k = k.reshape(b, k.shape[1], HEADS, DIM_HEAD).transpose(0, 2, 1, 3)
        v = v.reshape(b, v.shape[1], HEADS, DIM_HEAD).transpose(0, 2, 1, 3)
        sim = jnp.einsum('bhid,bhjd->bhij', q * scale, k) * scale
        full_mask = jnp.concatenate([mask, jnp.ones((b, m), dtype=bool)], axis=1)
        max_neg = -jnp.finfo(sim.dtype).max
        sim = jnp.where(full_mask[:, None, None, :], sim, max_neg)
        attn = jax.nn.softmax(sim.astype(jnp.float32), axis=-1).astype(sim.dtype)
        out = jnp.einsum('bhij,bhjd->bhid', attn, v)
        out = out.transpose(0, 2, 1, 3).reshape(b, m, INNER)
        out = out @ Wo
        return layernorm(out, ln_o_g, ln_o_b)

    def _L3_ffn_ref(x, W_router, b_router, W1, b1, W2, b2):
        import jax, jax.numpy as jnp
        import numpy as np
        N_EMBD = 128
        NUM_EXPERTS = 8
        TOP_K = 2
        D_FF = 4 * N_EMBD
        B, S = (4, 256)
        Bv, Sv, D = x.shape
        flat_x = x.reshape(-1, D)
        T = flat_x.shape[0]
        logits = flat_x @ W_router + b_router
        top_vals, top_idx = jax.lax.top_k(logits, TOP_K)
        neg_inf = jnp.full_like(logits, -jnp.inf)
        sparse_logits = neg_inf.at[jnp.arange(T)[:, None], top_idx].set(top_vals)
        router_weights = jax.nn.softmax(sparse_logits, axis=-1)
        final_output = jnp.zeros_like(flat_x)
        for e in range(NUM_EXPERTS):
            expert_mask = jnp.any(top_idx == e, axis=-1)
            h = jax.nn.relu(flat_x @ W1[e] + b1[e])
            y = h @ W2[e] + b2[e]
            w = router_weights[:, e] * expert_mask.astype(x.dtype)
            final_output = final_output + y * w[:, None]
        return final_output.reshape(Bv, Sv, D)
    x = x + jnp.tanh(g_xattn[0]) * _L0_xattn_ref(_layernorm(x, axis=-1), ctx_1024, ctx_1024, L0_xattn_Wq, L0_xattn_bq, L0_xattn_Wk, L0_xattn_bk, L0_xattn_Wv, L0_xattn_bv, L0_xattn_Wo, L0_xattn_bo)
    x = x + jnp.tanh(g_ffn[0]) * _L0_ffn_ref(_layernorm(x, axis=-1), L0_ffn_router_w, L0_ffn_routing_bias, L0_ffn_shared_gate, L0_ffn_shared_up, L0_ffn_shared_down, L0_ffn_routed_gate, L0_ffn_routed_up, L0_ffn_routed_down)
    x = x + jnp.tanh(g_xattn[1]) * _L1_xattn_ref(_layernorm(x, axis=-1), ctx_1024, ctx_1024, fside_Bx16xSxS2_0, fside_Bx16xSxS2_0, mask_BxS2_bf0, fside_SxS2_0, L1_xattn_Wq, L1_xattn_bq, L1_xattn_Wk, L1_xattn_bk, L1_xattn_Wv, L1_xattn_bv, L1_xattn_Wo, L1_xattn_bo)
    x = x + jnp.tanh(g_ffn[1]) * _L1_ffn_ref(_layernorm(x, axis=-1), L1_ffn_router_w, L1_ffn_up_w, L1_ffn_gate_w, L1_ffn_down_w, L1_ffn_shared_up_w, L1_ffn_shared_gate_w, L1_ffn_shared_down_w)
    x = x + jnp.tanh(g_xattn[2]) * _L2_xattn_ref(_layernorm(x, axis=-1), ctx_1024, L2_xattn_ln_gamma, L2_xattn_ln_beta, L2_xattn_w_q, L2_xattn_w_kv, L2_xattn_w_out, L2_xattn_b_out, L2_xattn_gate)
    x = x + jnp.tanh(g_ffn[2]) * _L2_ffn_ref(_layernorm(x, axis=-1), L2_ffn_router_w, L2_ffn_gate_w, L2_ffn_gate_b, L2_ffn_up_w, L2_ffn_up_b, L2_ffn_down_w, L2_ffn_down_b)
    x = x + jnp.tanh(g_xattn[3]) * _L3_xattn_ref(ctx_1024, _layernorm(x, axis=-1), mask_BxS2_bk1, L3_xattn_Wq, L3_xattn_Wkv, L3_xattn_Wo, L3_xattn_ln_x_g, L3_xattn_ln_x_b, L3_xattn_ln_l_g, L3_xattn_ln_l_b, L3_xattn_ln_o_g, L3_xattn_ln_o_b)
    x = x + jnp.tanh(g_ffn[3]) * _L3_ffn_ref(_layernorm(x, axis=-1), L3_ffn_W_router, L3_ffn_b_router, L3_ffn_W1, L3_ffn_b1, L3_ffn_W2, L3_ffn_b2)
    return x

_drawn_inputs = setup_inputs


def setup_inputs(seed=0):
    import zlib

    import numpy as np

    out = dict(_drawn_inputs(seed))
    spreads = {'L0_xattn_bq': (0.0, 0.1),
     'L0_xattn_bk': (0.0, 2.0),
     'L0_xattn_bv': (0.0, 0.1),
     'L0_xattn_bo': (0.0, 0.1),
     'L0_ffn_routing_bias': (0.0, 0.719),
     'L1_xattn_bq': (0.0, 0.1),
     'L1_xattn_bk': (0.0, 2.0),
     'L1_xattn_bv': (0.0, 0.1),
     'L1_xattn_bo': (0.0, 0.1),
     'L2_xattn_ln_gamma': (1.0, 0.2),
     'L2_xattn_ln_beta': (0.0, 0.1),
     'L2_xattn_b_out': (0.0, 0.1),
     'L2_ffn_gate_b': (0.0, 0.1),
     'L2_ffn_up_b': (0.0, 0.1),
     'L2_ffn_down_b': (0.0, 0.1),
     'L3_xattn_ln_x_g': (1.0, 0.2),
     'L3_xattn_ln_x_b': (0.0, 0.1),
     'L3_xattn_ln_l_g': (1.0, 0.2),
     'L3_xattn_ln_l_b': (0.0, 0.1),
     'L3_xattn_ln_o_g': (1.0, 0.2),
     'L3_xattn_ln_o_b': (0.0, 0.1),
     'L3_ffn_b_router': (0.0, 0.1),
     'L3_ffn_b1': (0.0, 0.1),
     'L3_ffn_b2': (0.0, 0.1)}
    factors = {'g_ffn': 28.512,
     'L0_ffn_router_w': 4.021,
     'L0_ffn_routed_gate': 3.115,
     'L0_ffn_routed_up': 3.425,
     'L0_ffn_routed_down': 3.587}
    for name, (base, spread) in spreads.items():
        noise = np.random.default_rng([zlib.crc32(name.encode()), seed]).standard_normal(out[name].shape)
        drawn = base * np.exp(spread * noise) if base else spread * noise
        out[name] = jnp.asarray(drawn.astype(out[name].dtype))
    for name, factor in factors.items():
        out[name] = (out[name] * factor).astype(out[name].dtype)
    return out
```

```python
from contextlib import ExitStack

import concourse.bass as bass
from concourse import mybir

F32 = mybir.dt.float32
BF16 = mybir.dt.bfloat16
U8 = mybir.dt.uint8
ACT = mybir.ActivationFunctionType
ALU = mybir.AluOpType
AX = mybir.AxisListType

B, S, D, SK = 8, 128, 128, 77
T = B * S
HALF = T // 2
E = 8
NEG = -1.0e30

HEADS = (16, 16, 16, 8)
HD = (8, 8, 64, 64)
KEYS = (SK, SK, SK, SK + S)
QSCALE = (1.0, 1.0, 64 ** -0.5, 1.0 / 64)
QC = tuple(max(1, h * d // D) for h, d in zip(HEADS, HD))
NC = (3, 4, 2, 4)
GATED = (True, True, True, False)

(BQ0, BK0, BV0, BO0, BQ1, BK1, BV1, BO1, G2, B2, BO2, XG3, XB3, LG3, LB3, OG3, OB3) = range(17)
GB2 = 17
UB2 = GB2 + E * NC[2]
B13 = UB2 + E * NC[2]
NVEC = B13 + E * NC[3]
GX, GF, GATE2, RB0, RB3 = 0, 4, 8, 9, 17
NROW = 25
IDENT, CENTER, MEAN, HMASK, REV = 0, 128, 256, 384, 400
ONES = 408
NCONST = 409
SHORT, LONG = 4, 20
RESIDUAL = 2.0e-6
GUESS = (-0.034, 1.02)


def build(nc, a, out):
    ctx = ExitStack()
    with ctx:
        def sb(name, shape, dt=F32):
            return ctx.enter_context(nc.sbuf_tensor(name, shape, dt))

        def sem(name):
            return ctx.enter_context(nc.semaphore(name))

        x = sb("x", [D, T])
        xn = sb("xn", [D, T])
        y = sb("y", [D, T])
        cx = sb("cx", [D, B, SK])
        cxn = sb("cxn", [D, B, SK])
        const = sb("const", [128, NCONST])
        vec = sb("vec", [128, NVEC])
        row = sb("row", [128, NROW])
        tg = sb("tg", [128, NROW])
        bad = sb("bad", [128, 1])
        bad_i = sb("bad_i", [1, 1], mybir.dt.int32)
        eps = sb("eps", [128, 1])
        rw = sb("rw", [D, 4, E])
        bd = sb("bd", [E, 4, D])
        fside = sb("fside", [S, SK])
        pad = sb("pad", [128, B, SK], U8)
        keep = sb("keep", [128, B, SK], U8)
        bias1 = sb("bias1", [128, B, KEYS[1]])
        bias3 = sb("bias3", [128, B, KEYS[3]])
        wa = [sb(f"wa{i}", [D, n]) for i, n in enumerate((512, 512, 4096, 2048))]
        sq = sb("sq", [128, 2, HALF])
        lnv = sb("lnv", [128, 2, HALF])
        rstd = sb("rstd", [128, 2, HALF])
        st = sb("st", [D, SK + S])
        q_sb = sb("q_sb", [128, 1024])
        k_sb = sb("k_sb", [128, SK])
        km = sb("km", [128, 1640])
        v_all = sb("v_all", [128, B, 1024])
        sc = sb("sc", [128, 1640])
        pr = sb("pr", [128, 1640])
        pt = sb("pt", [128, 2048])
        ind = sb("ind", [128, 16 * SK], BF16)
        col = sb("col", [128, 6, 16])
        o_sb = sb("o_sb", [128, 1024])
        ot_sb = sb("ot_sb", [128, 1024])
        W = [sb(f"W{i}", [128, 1536]) for i in range(2)]
        cT = sb("cT", [E, T])
        cB = v_all
        gs = sb("gs", [128, 2, HALF])
        tu = sb("tu", [128, 2, HALF])
        hb = sb("hb", [128, 2, HALF])
        rt = sb("rt", [128, 10, B, E])
        rc = sb("rc", [128, 6, B])

        ps = ctx.enter_context(nc.psum_tensor("ps", [128, 8, 512], F32))

        ident = const[:, IDENT:IDENT + 128]
        center = const[:, CENTER:CENTER + 128]
        mean = const[:, MEAN:MEAN + 128]
        ones = const[:, ONES:ONES + 1]
        hmask = const[:, HMASK:HMASK + 16]
        rev = const[:, REV:REV + E]

        def v1(i):
            return vec[:, i:i + 1]

        ld_x, ld_c, ld_cx, ld_t = sem("ld_x"), sem("ld_c"), sem("ld_cx"), sem("ld_t")
        ld_wa = [sem(f"ld_wa{i}") for i in range(4)]
        ld_w = [sem(f"ld_w{p}") for p in range(2)]
        init_v, init_g, tanh_s = sem("init_v"), sem("init_g"), sem("tanh_s")
        bias_s = sem("bias_s")
        x_rdy = sem("x_rdy")
        c_ps, sq_s, var_ps, ln_s, rs_s, xn_s, aff_s = (sem(n) for n in ("c_ps", "sq_s", "var_ps", "ln_s", "rs_s", "xn_s", "aff_s"))
        (stg, q_ps, q_s, k_ps, k_s, km_s, v_ps, v_s, s_ps, s_free, t_s, e_s, p_s, pt_ps, pt_s, pv_ps, o_s, ot_ps, ot_s, out_ps,
         y_s, kz) = (sem(n) for n in (
             "stg", "q_ps", "q_s", "k_ps", "k_s", "km_s", "v_ps", "v_s", "s_ps", "s_free", "t_s", "e_s", "p_s", "pt_ps", "pt_s",
             "pv_ps", "o_s", "ot_ps", "ot_s", "out_ps", "y_s", "kz"))
        dev_s, dev2_s, bad_s, bad_ps = sem("dev_s"), sem("dev2_s"), sem("bad_s"), sem("bad_ps")
        dch = sem("dch")
        lg_ps, rx_in, rx_s, comb_s, ct_ps, ct_s, cb_ps, cb_s, gu_ps, g_s, tu_s, h_s, dn_ps = (sem(n) for n in (
            "lg_ps", "rx_in", "rx_s", "comb_s", "ct_ps", "ct_s", "cb_ps", "cb_s", "gu_ps", "g_s", "tu_s", "h_s", "dn_ps"))
        out_s = sem("out_s")
        passed = sem("passed")

        UNITS = [E * 2 * n for n in NC]
        U0 = [sum(UNITS[:i]) for i in range(4)]
        LN = []
        cxf, cxnf = cx[:].rearrange("p b s -> p (b s)"), cxn[:].rearrange("p b s -> p (b s)")
        CXH = B * SK // 2
        for i in range(2):
            LN.append((cxf[:, i * CXH:(i + 1) * CXH], cxnf[:, i * CXH:(i + 1) * CXH], CXH, XG3, XB3))

        def ln_pair(src, dst, g=None, b=None):
            at = len(LN)
            for i in range(2):
                LN.append((src[:, i * HALF:(i + 1) * HALF], dst[:, i * HALF:(i + 1) * HALF], HALF, g, b))
            return at

        LN_A, LN_A2, LN_F, LN_Y = [], {}, [], None
        for l in range(4):
            LN_A.append(ln_pair(x, xn))
            if l == 2:
                LN_A2[l] = ln_pair(xn, xn, G2, B2)
            if l == 3:
                LN_A2[l] = ln_pair(xn, xn, LG3, LB3)
                LN_Y = ln_pair(y, y, OG3, OB3)
            LN_F.append(ln_pair(x, xn))
        AFF = [sum(1 for u in LN[:i] if u[3] is not None) for i in range(len(LN) + 1)]

        def ln_done(eng, u):
            if LN[u][3] is None:
                eng.wait_ge(xn_s, u + 1)
            else:
                eng.wait_ge(aff_s, AFF[u + 1])

        def settled(eng):
            eng.sem_inc(passed, 1)

        block = ctx.enter_context(nc.Block())

        @block.sync
        def _(sp):
            sp.dma_start(const[:], a["const"]).then_inc(ld_c, 16)
            sp.dma_start(cx[:], a["cx"]).then_inc(ld_cx, 16)
            sp.dma_start(x[:], a["x"]).then_inc(ld_x, 16)
            for dst, name in ((vec, "vec"), (row, "row"), (rw, "rw"), (bd, "bd"), (fside, "fside"), (pad, "pad"), (keep, "keep")):
                sp.dma_start(dst[:], a[name]).then_inc(ld_t, 16)
            for l in range(4):
                sp.dma_start(wa[l][:], a[f"wa{l}"]).then_inc(ld_wa[l], 16)
            for l in range(4):
                w = a[f"w{l}"]
                n = w.shape[2]
                per = 2 * NC[l]
                if l:
                    sp.wait_ge(dn_ps, U0[l] + 2)
                for p in range(2):
                    sp.dma_start(W[p][:, 0:n], w[p]).then_inc(ld_w[p], 16)
                with sp.Fori(0, E // 2 - 1) as j:
                    for p in range(2):
                        sp.wait_ge(dn_ps, j * (2 * per) + (U0[l] + (p + 1) * per + 2))
                        sp.dma_start(W[p][:, 0:n], w[bass.ds(2 * j + (2 + p), 1)].rearrange("a p n -> (a p) n")).then_inc(ld_w[p], 16)
            for h in range(2):
                sp.wait_ge(x_rdy, 15 + h)
                sp.dma_start(out[:, h * HALF:(h + 1) * HALF], x[:, h * HALF:(h + 1) * HALF]).then_inc(out_s, 16)
            sp.wait_ge(out_s, 32)

        @block.tensor
        def _(pe):
            def layernorm(u0):
                for u in (u0, u0 + 1):
                    src, _, n, _, _ = LN[u]
                    pe.matmul(ps[:, u % 2, 0:n], center, src, start=True, stop=True).then_inc(c_ps, 1)
                for u in (u0, u0 + 1):
                    n = LN[u][2]
                    pe.wait_ge(sq_s, u + 1)
                    pe.matmul(ps[:, 2 + u % 2, 0:n], mean, sq[:, u % 2, 0:n], start=True, stop=True).then_inc(var_ps, 1)

            def front(l, n):
                C, nk, w = QC[l], KEYS[l], wa[l]
                pe.wait_ge(stg, n + 1)
                pe.wait_ge(y_s, n + (0 if not isinstance(n, int) or n > 0 else 1))
                if not isinstance(n, int) or n > 0:
                    pe.wait_ge(v_s, n)
                for c in range(C):
                    m = pe.matmul(ps[:, 4 + c // 4, c % 4 * 128:c % 4 * 128 + 128], w[:, c * 128:c * 128 + 128],
                                  st[:, SK:SK + S], start=True, stop=True)
                m.then_inc(q_ps, 1)
                K0 = C * 128
                per = 4 if l == 2 else 2
                for c in range(C):
                    m = pe.matmul(ps[:, 6 + c // per, c % per * nk:c % per * nk + nk], w[:, K0 + c * 128:K0 + c * 128 + 128],
                                  st[:, 0:nk], start=True, stop=True)
                m.then_inc(k_ps, 1)
                pe.wait_ge(q_s, n + 1)
                V0 = 2 * C * 128
                if l < 2:
                    m = pe.matmul(ps[0:SK, 4, 0:128], st[:, 0:SK], w[:, V0:V0 + 128], start=True, stop=True)
                elif l == 2:
                    for c in range(2):
                        m = pe.matmul(ps[0:SK, 4 + c, :], st[:, 0:SK], w[:, V0 + c * 512:V0 + c * 512 + 512], start=True, stop=True)
                else:
                    pe.matmul(ps[0:SK, 4, :], st[:, 0:SK], w[:, V0:V0 + 512], start=True, stop=True)
                    m = pe.matmul(ps[:, 5, :], st[:, SK:SK + S], w[:, V0:V0 + 512], start=True, stop=True)
                m.then_inc(v_ps, 1)
                pe.wait_ge(km_s, n + 1)
                if not isinstance(n, int) or n > 0:
                    pe.wait_ge(s_free, n)
                for t in range(4):
                    if l < 2:
                        m = pe.matmul(ps[:, t, 0:308], q_sb[:, 0:128], km[:, t * 308:t * 308 + 308], start=True, stop=True)
                    elif l == 2:
                        for c in (2 * t, 2 * t + 1):
                            m = pe.matmul(ps[:, t, c % 2 * 154:c % 2 * 154 + 154], q_sb[:, c * 128:c * 128 + 128],
                                          km[:, c * 154:c * 154 + 154], start=True, stop=True)
                    else:
                        m = pe.matmul(ps[:, t, 0:410], q_sb[:, t * 128:t * 128 + 128], km[:, t * 410:t * 410 + 410], start=True, stop=True)
                m.then_inc(s_ps, 1)

            def back(l, n, b, last):
                C, w = QC[l], wa[l]
                if l == 0:
                    pe.wait_ge(bad_s, n + 1)
                    pe.matmul(ps[0:1, 6, 0:1], bad[:], ones[:, 0:1], start=True, stop=True).then_inc(bad_ps, 1)
                pe.wait_ge(p_s, n + 1)
                for g in range(4):
                    if g >= 2:
                        pe.wait_ge(pt_s, n * 4 + (g - 1))
                    for i in range(4):
                        if l < 3:
                            h = 4 * g + i
                            m = pe.transpose(ps[0:SK, 6 + g % 2, i * 128:i * 128 + 128], pr[:, h * SK:h * SK + SK], ident)
                        elif i < 2:
                            h = 2 * g + i
                            m = pe.transpose(ps[0:SK, 6 + g % 2, i * 128:i * 128 + 128], pr[:, h * 205:h * 205 + SK], ident)
                        else:
                            h = 2 * g + i - 2
                            m = pe.transpose(ps[:, 6 + g % 2, i * 128:i * 128 + 128], pr[:, h * 205 + SK:h * 205 + 205], ident)
                    m.then_inc(pt_ps, 1)
                pe.wait_ge(v_s, n + (1 if last else 2))
                pe.wait_ge(pt_s, n * 4 + 4)
                for h in range(HEADS[l]):
                    d = HD[l]
                    o = ps[:, 4 + h * d // 512, h * d % 512:h * d % 512 + d]
                    if l < 3:
                        m = pe.matmul(o, pt[0:SK, h * 128:h * 128 + 128], v_at(b)[0:SK, h * d:h * d + d], start=True, stop=True)
                    else:
                        c0 = h // 2 * 512 + h % 2 * 128
                        pe.matmul(o, pt[0:SK, c0:c0 + 128], v_at(b)[0:SK, h * d:h * d + d], start=True, stop=False)
                        m = pe.matmul(o, pt[:, c0 + 256:c0 + 384], v_at(b)[:, 512 + h * d:512 + h * d + d], start=False, stop=True)
                m.then_inc(pv_ps, 1)
                pe.wait_ge(o_s, n + 1)
                for c in range(C):
                    m = pe.transpose(ps[:, 6 + c // 4, c % 4 * 128:c % 4 * 128 + 128], o_sb[:, c * 128:c * 128 + 128], ident)
                m.then_inc(ot_ps, 1)
                pe.wait_ge(ot_s, n + 1)
                O0 = {0: 384, 1: 384, 2: 3072, 3: 1536}[l]
                for c in range(C):
                    m = pe.matmul(ps[:, 4, 0:128], w[:, O0 + c * 128:O0 + c * 128 + 128], ot_sb[:, c * 128:c * 128 + 128],
                                  start=(c == 0), stop=(c == C - 1))
                m.then_inc(out_ps, 1)

            def v_at(b):
                return v_all[:, b, :] if isinstance(b, int) else v_all[:, bass.ds(b, 1), :].rearrange("p a n -> p (a n)")

            def attention(l):
                pe.wait_ge(ld_wa[l], 16)
                n0 = B * l
                front(l, n0)
                with pe.Fori(0, B - 1) as b:
                    front(l, b + (n0 + 1))
                    back(l, b + n0, b, False)
                back(l, n0 + B - 1, B - 1, True)

            def experts(l):
                n, H = NC[l], NC[l] * 128
                up, down = H, (2 * H if GATED[l] else H)
                ln_done(pe, LN_F[l])
                ln_done(pe, LN_F[l] + 1)
                for t in range(B):
                    m = pe.matmul(ps[:, 7, t * E:t * E + E], xn[:, t * S:t * S + S], rw[:, l, :], start=True, stop=True)
                m.then_inc(lg_ps, 1)
                pe.wait_ge(comb_s, l + 1)
                for t in range(B):
                    m = pe.transpose(ps[0:E, 6 + t // 4, t % 4 * 128:t % 4 * 128 + 128], rt[:, 9, t, :], ident)
                m.then_inc(ct_ps, 1)
                pe.wait_ge(ct_s, l + 1)
                for h in range(2):
                    pe.matmul(ps[:, 4 + h, :], bd[:, l, :], cT[:, h * HALF:h * HALF + HALF], start=True, stop=False, skip_group_check=True)
                for i in range(2 * E):
                    e, h = i // 2, i % 2
                    if i >= 4:
                        pe.wait_ge(cb_s, 2 * E * l + i - 3)
                    pe.matmul(ps[:, i % 4, :], ident[0:E, e:e + 1].to_broadcast([E, 128]), cT[:, h * HALF:h * HALF + HALF],
                              start=True, stop=True).then_inc(cb_ps, 1)
                pe.wait_ge(cb_s, 2 * E * (l + 1))

                def place(i):
                    return i // (2 * n), i // n % 2, i % n

                def gate_up(u, i):
                    p, h, c = place(i)
                    pe.wait_ge(h_s, u + 1)
                    xs = xn[:, h * HALF:h * HALF + HALF]
                    m = pe.matmul(ps[:, i % 2, :], W[p][:, c * 128:c * 128 + 128], xs, start=True, stop=True)
                    if GATED[l]:
                        m = pe.matmul(ps[:, 2 + i % 2, :], W[p][:, up + c * 128:up + c * 128 + 128], xs, start=True, stop=True)
                    m.then_inc(gu_ps, 1)

                def down_(u, i):
                    p, h, c = place(i)
                    pe.wait_ge(h_s, u + 3)
                    pe.matmul(ps[:, 4 + h, :], W[p][:, down + c * 128:down + c * 128 + 128], hb[:, i % 2, :],
                              start=False, stop=False, skip_group_check=True).then_inc(dn_ps, 1)

                NU = 4 * n

                def pair(j, last):
                    for i in range(NU):
                        u = j * NU + (U0[l] + i)
                        if i + 1 < NU:
                            if (i + 1) == 2 * n:
                                pe.wait_ge(ld_w[1], (j + (4 * l + 1)) * 16)
                            gate_up(u + 1, i + 1)
                        elif not last:
                            pe.wait_ge(ld_w[0], (j + (4 * l + 2)) * 16)
                            gate_up(u + 1, 0)
                        down_(u, i)

                pe.wait_ge(ld_w[0], 16 * (4 * l + 1))
                gate_up(U0[l], 0)
                with pe.Fori(0, E // 2 - 1) as j:
                    pair(j, False)
                pair(E // 2 - 1, True)

            pe.wait_ge(ld_c, 16)
            pe.wait_ge(ld_cx, 16)
            layernorm(0)
            pe.wait_ge(ld_x, 16)
            pe.wait_ge(ld_t, 16 * 7)
            ln_done(pe, 1)
            for l in range(4):
                if l:
                    pe.wait_ge(x_rdy, 4 * l)
                layernorm(LN_A[l])
                if l in LN_A2:
                    ln_done(pe, LN_A[l])
                    ln_done(pe, LN_A[l] + 1)
                    layernorm(LN_A2[l])
                    ln_done(pe, LN_A2[l] + 1)
                else:
                    ln_done(pe, LN_A[l] + 1)
                attention(l)
                if l == 3:
                    pe.wait_ge(y_s, B * 4 + 1)
                    layernorm(LN_Y)
                pe.wait_ge(x_rdy, 4 * l + 2)
                layernorm(LN_F[l])
                experts(l)

        @block.scalar
        def _(act):
            def layernorm(u0):
                for u in (u0, u0 + 1):
                    n = LN[u][2]
                    act.wait_ge(c_ps, u + 1)
                    act.activation(sq[:, u % 2, 0:n], ps[:, u % 2, 0:n], ACT.Square).then_inc(sq_s, 1)
                for u in (u0, u0 + 1):
                    n = LN[u][2]
                    act.wait_ge(var_ps, u + 1)
                    act.activation(lnv[:, u % 2, 0:n], ps[:, 2 + u % 2, 0:n], ACT.Ln, bias=eps[:, 0:1]).then_inc(ln_s, 1)
                for u in (u0, u0 + 1):
                    n = LN[u][2]
                    act.wait_ge(ln_s, u + 1)
                    act.activation(rstd[:, u % 2, 0:n], lnv[:, u % 2, 0:n], ACT.Exp, scale=-0.5).then_inc(rs_s, 1)

            def front(l, n, b):
                C, nk = QC[l], KEYS[l]
                act.wait_ge(q_ps, n + 1)
                if not isinstance(n, int) or n > 0:
                    act.wait_ge(s_ps, n)
                if l < 2:
                    act.activation(q_sb[:, 0:128], ps[:, 4, 0:128], ACT.Identity, bias=v1((BQ0, BQ1)[l])).then_inc(q_s, 1)
                else:
                    act.activation(q_sb[:, 0:C * 128], ps[:, 4:4 + C // 4, :], ACT.Copy, scale=QSCALE[l]).then_inc(q_s, 1)
                act.wait_ge(k_ps, n + 1)
                if l < 2:
                    if not isinstance(n, int) or n > 0:
                        act.wait_ge(km_s, n)
                    act.activation(k_sb[:, :], ps[:, 6, 0:SK], ACT.Identity, bias=v1((BK0, BK1)[l])).then_inc(k_s, 1)
                else:
                    per = 4 if l == 2 else 2
                    act.wait_ge(kz, l - 1)
                    kv = km[:, 0:C * 2 * nk].rearrange("p (u c a s) -> p u c a s", u=2, a=2, s=nk)
                    pv = ps[:, 6:8, 0:per * nk].rearrange("p u (c s) -> p u c s", s=nk)
                    act.activation(kv[0:64, :, :, 0, :], pv[0:64], ACT.Copy)
                    act.activation(kv[64:128, :, :, 1, :], pv[64:128], ACT.Copy).then_inc(km_s, 1)
                act.wait_ge(v_ps, n + 1)
                settled(act)
                if l < 2:
                    act.activation(vb(b, 0, SK, 0, 128), ps[0:SK, 4, 0:128], ACT.Copy).then_inc(v_s, 1)
                elif l == 2:
                    act.activation(vb(b, 0, SK, 0, 1024), ps[0:SK, 4:6, :], ACT.Copy).then_inc(v_s, 1)
                else:
                    act.activation(vb(b, 0, SK, 0, 512), ps[0:SK, 4, :], ACT.Copy)
                    act.activation(vb(b, 0, 128, 512, 1024), ps[:, 5, :], ACT.Copy).then_inc(v_s, 1)

            def vb(b, p0, p1, c0, c1):
                if isinstance(b, int):
                    return v_all[p0:p1, b, c0:c1]
                return v_all[p0:p1, bass.ds(b, 1), c0:c1].rearrange("p a n -> p (a n)")

            def exps(l, n):
                W_ = HEADS[l] * KEYS[l]
                act.wait_ge(t_s, n + 1)
                if l:
                    act.activation(pr[:, 0:W_], sc[:, 0:W_], ACT.Exp).then_inc(e_s, 1)
                else:
                    act.activation(pr[:, 0:W_], sc[:, 0:W_], ACT.Square).then_inc(e_s, 1)
                    act.wait_ge(dev_s, n + 1)
                    act.activation(col[:, 5, :], col[:, 5, :], ACT.Sqrt).then_inc(dev2_s, 1)

            def turned(l, n):
                for g in range(4):
                    act.wait_ge(pt_ps, n * 4 + (g + 1))
                    if l < 3:
                        act.activation(pt[0:SK, g * 512:g * 512 + 512], ps[0:SK, 6 + g % 2, :], ACT.Copy).then_inc(pt_s, 1)
                    else:
                        act.activation(pt[0:SK, g * 512:g * 512 + 256], ps[0:SK, 6 + g % 2, 0:256], ACT.Copy)
                        act.activation(pt[:, g * 512 + 256:g * 512 + 512], ps[:, 6 + g % 2, 256:512], ACT.Copy).then_inc(pt_s, 1)

            def back(l, n, b):
                C = QC[l]
                act.wait_ge(pv_ps, n + 1)
                nb = max(1, C // 4)
                act.activation(o_sb[:, 0:C * 128], ps[:, 4:4 + nb, 0:C * 128 // nb], ACT.Copy).then_inc(o_s, 1)
                act.wait_ge(ot_ps, n + 1)
                if l < 2:
                    act.activation(ot_sb[:, 0:128], ps[:, 6, 0:128], ACT.Identity, bias=v1((BV0, BV1)[l])).then_inc(ot_s, 1)
                else:
                    act.activation(ot_sb[:, 0:C * 128], ps[:, 6:6 + nb, 0:C * 128 // nb], ACT.Copy).then_inc(ot_s, 1)
                act.wait_ge(out_ps, n + 1)
                settled(act)
                yb = y[:, b * S:b * S + S] if isinstance(b, int) else y[:, bass.ds(b * S, S)]
                if l < 3:
                    act.activation(yb, ps[:, 4, 0:128], ACT.Identity, bias=v1((BO0, BO1, BO2)[l])).then_inc(y_s, 1)
                else:
                    act.activation(yb, ps[:, 4, 0:128], ACT.Copy).then_inc(y_s, 1)

            def attention(l):
                n0 = B * l
                front(l, n0, 0)
                exps(l, n0)
                with act.Fori(0, B - 1) as b:
                    front(l, b + (n0 + 1), b + 1)
                    turned(l, b + n0)
                    exps(l, b + (n0 + 1))
                    back(l, b + n0, b)
                turned(l, n0 + B - 1)
                back(l, n0 + B - 1, B - 1)

            def experts(l):
                n = NC[l]
                act.wait_ge(rx_in, l + 1)
                act.activation(rt[:, 1], rt[:, 0], ACT.Exp, scale=-1.0 if l == 0 else 1.0).then_inc(rx_s, 1)
                act.wait_ge(ct_ps, l + 1)
                act.activation(cT[:], ps[0:E, 6:8, :], ACT.Copy).then_inc(ct_s, 1)
                for i in range(2 * E):
                    act.wait_ge(cb_ps, 2 * E * l + i + 1)
                    act.activation(cB[:, i // 2, i % 2 * HALF:i % 2 * HALF + HALF], ps[:, i % 4, :], ACT.Copy).then_inc(cb_s, 1)
                with act.Fori(0, E // 2) as j:
                    for i in range(4 * n):
                        u = j * (4 * n) + (U0[l] + i)
                        p, c = i // (2 * n), i % n
                        act.wait_ge(gu_ps, u + 1)
                        if l >= 2:
                            settled(act)
                        if l < 2:
                            act.activation(gs[:, i % 2, :], ps[:, i % 2, :], ACT.Silu).then_inc(g_s, 1)
                        else:
                            c0 = {2: GB2, 3: B13}[l] + p * n + c
                            bias = vec[:, bass.ds(j * (2 * n) + c0, 1)]
                            act.activation(gs[:, i % 2, :], ps[:, i % 2, :], ACT.Silu if l == 2 else ACT.Relu, bias=bias).then_inc(g_s, 1)

            act.wait_ge(ld_t, 16 * 7)
            act.wait_ge(init_v, 1)
            act.activation(tg[:], row[:], ACT.Tanh).then_inc(tanh_s, 1)
            layernorm(0)
            for l in range(4):
                layernorm(LN_A[l])
                if l in LN_A2:
                    layernorm(LN_A2[l])
                attention(l)
                if l == 3:
                    layernorm(LN_Y)
                layernorm(LN_F[l])
                experts(l)

        @block.gpsimd
        def _(g):
            g.sem_inc(dn_ps, 2)
            g.sem_inc(h_s, 2)
            g.sem_inc(y_s, 1)

            def stage(l, n, b):
                if not isinstance(n, int) or n > 0:
                    g.wait_ge(v_ps, n)
                settled(g)
                src = cxn if l == 3 else cx
                cb = src[:, b, :] if isinstance(b, int) else src[:, bass.ds(b, 1), :].rearrange("p a s -> p (a s)")
                xb = xn[:, b * S:b * S + S] if isinstance(b, int) else xn[:, bass.ds(b * S, S)]
                g.tensor_copy(st[:, 0:SK], cb)
                g.tensor_copy(st[:, SK:SK + S], xb).then_inc(stg, 1)
                if l < 2:
                    g.wait_ge(k_s, n + 1)
                    if not isinstance(n, int) or n > 0:
                        g.wait_ge(s_ps, n)
                    g.tensor_tensor(km[:, 0:1232].rearrange("p (h s) -> p h s", s=SK),
                                    k_sb[:, :].unsqueeze(1).to_broadcast([128, 16, SK]),
                                    hmask.unsqueeze(2).to_broadcast([128, 16, SK]), ALU.mult).then_inc(km_s, 1)

            g.wait_ge(ld_cx, 16)
            for l in range(4):
                if l >= 2:
                    g.wait_ge(s_ps, B * l)
                    g.memset(km[:], 0.0).then_inc(kz, 1)
                u = LN_A2.get(l, LN_A[l])
                ln_done(g, u)
                ln_done(g, u + 1)
                stage(l, B * l, 0)
                with g.Fori(1, B) as b:
                    stage(l, b + B * l, b)

        @block.vector
        def _(v):
            steps = [0]

            class Steps:

                def __init__(self, turn=0, per=0):
                    self.turn, self.per, self.k = turn, per, 0

                def __call__(self, ins):
                    self.k += 1
                    ins.then_inc(dch, 1)
                    v.wait_ge(dch, self.turn * self.per + (steps[0] + self.k))

                def mark(self):
                    return self.k

                def within(self, at, turn=0, per=0):
                    def step(ins, k=[0]):
                        k[0] += 1
                        ins.then_inc(dch, 1)
                        v.wait_ge(dch, self.turn * self.per + (steps[0] + at + k[0]) + turn * per)
                    return step

                def skip(self, k):
                    self.k += k

                def end(self, turns=1):
                    assert self.turn is 0 or self.k == self.per, self.k
                    steps[0] += self.k * turns

            def layernorm(u0):
                for u in (u0, u0 + 1):
                    _, dst, n, g, b = LN[u]
                    v.wait_ge(rs_s, u + 1)
                    v.tensor_tensor(dst, ps[:, u % 2, 0:n], rstd[:, u % 2, 0:n], ALU.mult).then_inc(xn_s, 1)
                    if g is not None:
                        v.wait_ge(xn_s, u + 1)
                        v.tensor_scalar(dst, dst, v1(g), v1(b), ALU.mult, ALU.add).then_inc(aff_s, 1)

            def heads(ap, l):
                h, nk = HEADS[l], KEYS[l]
                return ap.rearrange("p (u h s) -> p u h s", u=4, s=nk)

            def softmax(l, n, b, step):
                h, nk = HEADS[l], KEYS[l]
                W_ = h * nk
                hs = [128, 4, h // 4, nk]
                S4 = ps[:, 0:4, 0:W_ // 4].rearrange("p u (h s) -> p u h s", s=nk)
                T4 = heads(sc[:, 0:W_], l)
                P3 = pr[:, 0:W_].rearrange("p (h s) -> p h s", s=nk)
                c = [col[:, i, 0:h] for i in range(6)]
                c4 = [x_.rearrange("p (u h) -> p u h", u=4) for x_ in c]
                v.wait_ge(s_ps, n + 1)
                if l in (1, 3):
                    tab = bias1 if l == 1 else bias3
                    bb = tab[:, b, :] if isinstance(b, int) else tab[:, bass.ds(b, 1), :].rearrange("p a s -> p (a s)")
                    step(v.tensor_tensor(T4, S4, bb.unsqueeze(1).unsqueeze(1).to_broadcast(hs), ALU.add))
                    v.sem_inc(s_free, 1)
                    step(v.reduce_max(c4[0], T4, AX.X))
                    v.tensor_tensor(T4, T4, c4[0].unsqueeze(3).to_broadcast(hs), ALU.subtract).then_inc(t_s, 1)
                else:
                    step(v.reduce_max(c4[0], S4, AX.X))
                    step(v.tensor_tensor(T4, S4, c4[0].unsqueeze(3).to_broadcast(hs), ALU.subtract))
                    v.sem_inc(s_free, 1)
                    v.sem_inc(t_s, 1)
                v.wait_ge(e_s, n + 1)
                step(v.tensor_reduce(c[1], P3, AX.X, ALU.add))
                step(v.reciprocal(c[2], c[1]))
                v.tensor_tensor(P3, P3, c[2].unsqueeze(2).to_broadcast([128, h, nk]), ALU.mult).then_inc(p_s, 1)

            def sparsemax(n, step):
                hs = [128, 4, 4, SK]
                S4 = ps[:, 0:4, 0:308].rearrange("p u (h s) -> p u h s", s=SK)
                T4 = heads(sc[:, 0:1232], 0)
                T3 = sc[:, 0:1232].rearrange("p (h s) -> p h s", s=SK)
                P3 = pr[:, 0:1232].rearrange("p (h s) -> p h s", s=SK)
                I3 = ind[:].rearrange("p (h s) -> p h s", s=SK)
                top, avg, tau, f, cnt, dev = (col[:, i, :] for i in range(6))

                def newton(step):
                    step(v.tensor_tensor(P3, T3, tau.unsqueeze(2).to_broadcast([128, 16, SK]), ALU.subtract))
                    step(v.tensor_scalar(ind[:], pr[:, 0:1232], 0.0, None, ALU.is_gt))
                    step(v.tensor_scalar(pr[:, 0:1232], pr[:, 0:1232], 0.0, None, ALU.max))
                    step(v.tensor_reduce(f, P3, AX.X, ALU.add))
                    step(v.tensor_reduce(cnt, I3, AX.X, ALU.add))
                    step(v.reciprocal(cnt, cnt))
                    step(v.scalar_tensor_tensor(out=f, in0=f, scalar=-1.0, in1=cnt, op0=ALU.add, op1=ALU.mult))
                    step(v.tensor_tensor(tau, tau, f, ALU.add))

                def rows_sum(step):
                    step(v.tensor_tensor(P3, T3, tau.unsqueeze(2).to_broadcast([128, 16, SK]), ALU.subtract))
                    step(v.tensor_scalar(pr[:, 0:1232], pr[:, 0:1232], 0.0, None, ALU.max))

                v.wait_ge(s_ps, n + 1)
                step(v.reduce_max(top.rearrange("p (u h) -> p u h", u=4), S4, AX.X))
                step(v.tensor_tensor(T4, S4, top.rearrange("p (u h) -> p u h", u=4).unsqueeze(3).to_broadcast(hs), ALU.subtract))
                v.sem_inc(s_free, 1)
                v.sem_inc(t_s, 1)
                step(v.tensor_reduce(avg, T3, AX.X, ALU.add))
                step(v.tensor_scalar(avg, avg, 1.0 / SK, None, ALU.mult))
                step(v.tensor_tensor(f, avg, avg, ALU.mult))
                v.wait_ge(e_s, n + 1)
                step(v.tensor_reduce(dev, P3, AX.X, ALU.add))
                step(v.scalar_tensor_tensor(out=dev, in0=dev, scalar=1.0 / SK, in1=f, op0=ALU.mult, op1=ALU.subtract))
                step(v.tensor_scalar(dev, dev, 0.0, None, ALU.max))
                v.sem_inc(dev_s, 1)
                v.wait_ge(dev2_s, n + 1)
                step(v.tensor_scalar(dev, dev, GUESS[1], GUESS[0], ALU.mult, ALU.add))
                step(v.tensor_tensor(tau, dev, avg, ALU.add))
                step(v.tensor_scalar(tau, tau, -1.0 / SK, -1.0, ALU.min, ALU.max))
                for _ in range(SHORT):
                    newton(step)
                rows_sum(step)
                step(v.tensor_reduce(f, P3, AX.X, ALU.add))
                step(v.tensor_scalar(f, f, -1.0, None, ALU.add))
                step(v.tensor_tensor(f, f, f, ALU.mult))
                step(v.reduce_max(bad[:], f, AX.X))
                step(v.tensor_scalar(bad[:], bad[:], RESIDUAL ** 2, None, ALU.is_gt))
                v.sem_inc(bad_s, 1)
                v.wait_ge(bad_ps, n + 1)
                step(v.tensor_copy(bad_i[:], ps[0:1, 6, 0:1]))
                settled(v)
                left = v.value_load(bad_i[0:1, 0:1], min_val=0, max_val=128)
                at = step.mark()
                with v.If(left > 0):
                    again = step.within(at)
                    again(v.tensor_scalar(tau, avg, 0.0, -1.0, ALU.mult, ALU.add))
                    settled(v)
                    with v.Fori(0, LONG) as i:
                        turn = step.within(at + 1, i, 8)
                        newton(turn)
                    again = step.within(at + 1 + 8 * LONG)
                    rows_sum(again)
                    settled(v)
                with v.Else():
                    v.sem_inc(dch, 1 + 8 * LONG + 2)
                step.skip(1 + 8 * LONG + 2)
                v.sem_inc(p_s, 1)

            def attention(l):
                n0 = B * l
                per = {0: 11 + 8 * SHORT + 2 + 5 + 1 + 8 * LONG + 2 + 1, 2: 4}.get(l, 4)
                step = Steps()
                if l == 0:
                    sparsemax(n0, step)
                else:
                    softmax(l, n0, 0, step)
                step.end()
                with v.Fori(0, B - 1) as b:
                    step = Steps(b, per)
                    if l == 0:
                        sparsemax(b + (n0 + 1), step)
                    else:
                        softmax(l, b + (n0 + 1), b + 1, step)
                step.end(B - 1)

            def route(l):
                step = Steps()
                n = E - 1 if l == 0 else E
                L, X, Pb, oh1, oh2, w1, w2, val = (rt[:, i, :, 0:n] for i in range(8))
                res = rt[:, 9]
                m1, m2, s1, s2, r1 = (rc[:, i, :] for i in range(5))
                bc = [128, B, n]
                rv = rev[:, 0:n].unsqueeze(1).to_broadcast(bc)

                def spread(c):
                    return c.unsqueeze(2).to_broadcast(bc)

                def first_max(values, m, oh):
                    step(v.reduce_max(m, values, AX.X))
                    step(v.tensor_tensor(oh, values, spread(m), ALU.is_equal))
                    step(v.tensor_tensor(oh, oh, rv, ALU.mult))
                    step(v.reduce_max(s2, oh, AX.X))
                    step(v.tensor_tensor(oh, rv, spread(s2), ALU.is_equal))

                v.wait_ge(lg_ps, l + 1)
                logits = ps[:, 7, 0:B * E].rearrange("p (t e) -> p t e", e=E)
                if l in (0, 3):
                    rb = row[:, (RB0 if l == 0 else RB3):][:, 0:E].unsqueeze(1).to_broadcast([128, B, E])
                    step(v.tensor_tensor(rt[:, 0], logits, rb, ALU.add))
                    if l == 0:
                        v.sem_inc(rx_in, 1)
                        v.wait_ge(rx_s, 1)
                        step(v.tensor_scalar(w1, X, 1.0, None, ALU.add))
                        step(v.reciprocal(val, w1))
                    else:
                        step(v.tensor_copy(val, L))
                else:
                    step(v.tensor_copy(val, logits))
                first_max(val, m1, oh1)
                if l:
                    step(v.tensor_tensor(L, val, spread(m1), ALU.subtract))
                    v.sem_inc(rx_in, 1)
                if l != 1:
                    step(v.scalar_tensor_tensor(out=w2, in0=oh1, scalar=NEG, in1=val, op0=ALU.mult, op1=ALU.add))
                    first_max(w2, m2, oh2)
                    step(v.tensor_tensor(oh2, oh1, oh2, ALU.add))
                if l:
                    v.wait_ge(rx_s, l + 1)
                if l == 1:
                    step(v.tensor_reduce(s1, X, AX.X, ALU.add))
                    step(v.reciprocal(r1, s1))
                    step(v.scalar_tensor_tensor(out=res, in0=oh1, scalar=2.0, in1=spread(r1), op0=ALU.mult, op1=ALU.mult))
                    v.memset(res[:, :, E - 1:E], 1.0).then_inc(comb_s, 1)
                    step.end()
                    return
                src = val if l == 0 else X
                if l == 2:
                    step(v.tensor_reduce(s1, X, AX.X, ALU.add))
                    step(v.reciprocal(r1, s1))
                    step(v.tensor_tensor(Pb, X, spread(r1), ALU.mult))
                    src = Pb
                step(v.tensor_tensor(w1, src, oh2, ALU.mult))
                step(v.tensor_reduce(s1, w1, AX.X, ALU.add))
                if l == 2:
                    step(v.tensor_scalar(s1, s1, 1e-9, None, ALU.add))
                step(v.reciprocal(r1, s1))
                if l == 0:
                    step(v.memset(res[:, :, E - 1:E], 1.0))
                v.tensor_tensor(res[:, :, 0:n], w1, spread(r1), ALU.mult).then_inc(comb_s, 1)
                step.end()

            def experts(l):
                n = NC[l]
                route(l)
                v.wait_ge(cb_s, 2 * E * (l + 1))
                with v.Fori(0, E // 2) as j:
                    for i in range(4 * n):
                        u = j * (4 * n) + (U0[l] + i)
                        p, h, c = i // (2 * n), i // n % 2, i % n
                        coef = cB[:, bass.ds(2 * j + p, 1), h * HALF:h * HALF + HALF].rearrange("q a n -> q (a n)")
                        v.wait_ge(g_s, u + 1)
                        v.wait_ge(dn_ps, u + 1)
                        if l < 3:
                            if l == 2:
                                ub = vec[:, bass.ds(j * (2 * n) + (UB2 + p * n + c), 1)]
                                v.scalar_tensor_tensor(out=tu[:, i % 2, :], in0=ps[:, 2 + i % 2, :], scalar=ub, in1=gs[:, i % 2, :],
                                                       op0=ALU.add, op1=ALU.mult).then_inc(tu_s, 1)
                            else:
                                v.tensor_tensor(tu[:, i % 2, :], ps[:, 2 + i % 2, :], gs[:, i % 2, :], ALU.mult).then_inc(tu_s, 1)
                            v.wait_ge(tu_s, u + 1)
                            v.tensor_tensor(hb[:, i % 2, :], tu[:, i % 2, :], coef, ALU.mult).then_inc(h_s, 1)
                        else:
                            v.tensor_tensor(hb[:, i % 2, :], gs[:, i % 2, :], coef, ALU.mult).then_inc(h_s, 1)
                v.wait_ge(dn_ps, U0[l] + UNITS[l] + 2)
                for h in range(2):
                    xs = x[:, h * HALF:h * HALF + HALF]
                    v.scalar_tensor_tensor(out=xs, in0=ps[:, 4 + h, :], scalar=tg[:, GF + l:GF + l + 1], in1=xs,
                                           op0=ALU.mult, op1=ALU.add).then_inc(x_rdy, 1)

            def residual(l):
                if l < 3:
                    v.wait_ge(y_s, B * (l + 1) + 1)
                for h in range(2):
                    if l == 3:
                        ln_done(v, LN_Y + h)
                    xs, ys = x[:, h * HALF:h * HALF + HALF], y[:, h * HALF:h * HALF + HALF]
                    v.scalar_tensor_tensor(out=xs, in0=ys, scalar=tg[:, GX + l:GX + l + 1], in1=xs,
                                           op0=ALU.mult, op1=ALU.add).then_inc(x_rdy, 1)

            v.memset(eps[:], 1e-5).then_inc(init_v, 1)
            v.wait_ge(ld_t, 16 * 7)
            step = Steps()
            step(v.tensor_scalar(bias1[:], pad[:], NEG, None, ALU.mult))
            step(v.tensor_tensor(bias1[:], bias1[:], fside[:].unsqueeze(1).to_broadcast([128, B, SK]), ALU.add))
            step(v.tensor_scalar(bias3[:, :, 0:SK], keep[:], -1.0, -NEG, ALU.add, ALU.mult))
            step(v.memset(bias3[:, :, SK:SK + S], 0.0))
            v.wait_ge(tanh_s, 1)
            step(v.tensor_tensor(tg[:, GX + 2:GX + 3], tg[:, GX + 2:GX + 3], tg[:, GATE2:GATE2 + 1], ALU.mult))
            step.end()
            layernorm(0)
            for l in range(4):
                layernorm(LN_A[l])
                if l in LN_A2:
                    layernorm(LN_A2[l])
                attention(l)
                if l == 3:
                    layernorm(LN_Y)
                residual(l)
                layernorm(LN_F[l])
                experts(l)


def kernel(**inputs):
    import numpy as np
    import concourse.bacc as bacc
    from concourse.bass_utils import run_bass_kernel_spmd as run

    i = {k: np.asarray(v) for k, v in inputs.items()}
    f = np.float32

    def rows(v, n=None):
        v = v.reshape(1, -1)
        return np.broadcast_to(v, (128, v.shape[1]))

    const = np.zeros((128, NCONST), f)
    const[:, IDENT:IDENT + 128] = np.eye(128)
    const[:, CENTER:CENTER + 128] = np.eye(128) - 1.0 / D
    const[:, MEAN:MEAN + 128] = 1.0 / D
    const[np.arange(128), HMASK + np.arange(128) // 8] = 8 ** -0.5
    const[:, ONES] = 1.0
    const[:, REV:REV + E] = E - np.arange(E)

    vecs = [i[f"L{l}_xattn_{n}"] for l in (0, 1) for n in ("bq", "bk", "bv", "bo")]
    vecs += [i["L2_xattn_" + n] for n in ("ln_gamma", "ln_beta", "b_out")]
    vecs += [i["L3_xattn_" + n] for n in ("ln_x_g", "ln_x_b", "ln_l_g", "ln_l_b", "ln_o_g", "ln_o_b")]
    vec = np.concatenate([np.stack(vecs, 1), i["L2_ffn_gate_b"].reshape(-1, 128).T, i["L2_ffn_up_b"].reshape(-1, 128).T,
                          i["L3_ffn_b1"].reshape(-1, 128).T], 1)
    pad1 = np.zeros(1, f)
    row = rows(np.concatenate([i["g_xattn"], i["g_ffn"], i["L2_xattn_gate"], i["L0_ffn_routing_bias"], pad1, i["L3_ffn_b_router"]]))
    rw = np.stack([np.concatenate([i["L0_ffn_router_w"], np.zeros((D, 1), f)], 1), i["L1_ffn_router_w"], i["L2_ffn_router_w"].T,
                   i["L3_ffn_W_router"]], 1)
    zero = np.zeros((E, D), f)
    bd = np.stack([zero, zero, i["L2_ffn_down_b"], i["L3_ffn_b2"]], 1)

    def chunks(w):
        return w.reshape(-1, 128, D).transpose(1, 0, 2).reshape(128, -1)

    p = "L0_xattn_"
    wa0 = np.concatenate([i[p + "Wq"], i[p + "Wk"], i[p + "Wv"], i[p + "Wo"]], 1)
    p = "L1_xattn_"
    wa1 = np.concatenate([i[p + "Wq"].T, i[p + "Wk"].T, i[p + "Wv"].T, i[p + "Wo"].T], 1)
    p = "L2_xattn_"
    wa2 = np.concatenate([i[p + "w_q"], i[p + "w_kv"], chunks(i[p + "w_out"])], 1)
    p = "L3_xattn_"
    wa3 = np.concatenate([i[p + "Wq"], i[p + "Wkv"], chunks(i[p + "Wo"])], 1)

    def expert_w(ups, down):
        H = down.shape[1]
        HP = -(-H // 128) * 128
        ups = [np.pad(u, ((0, 0), (0, 0), (0, HP - H))) for u in ups]
        down = np.pad(down, ((0, 0), (0, HP - H), (0, 0))).reshape(E, -1, 128, D).transpose(0, 2, 1, 3).reshape(E, 128, -1)
        return np.concatenate(ups + [down], 2)

    def with_shared(r, s):
        return np.concatenate([r, s[None]], 0)

    w0 = expert_w([with_shared(i["L0_ffn_routed_gate"], i["L0_ffn_shared_gate"]), with_shared(i["L0_ffn_routed_up"], i["L0_ffn_shared_up"])],
                  with_shared(i["L0_ffn_routed_down"], i["L0_ffn_shared_down"]))
    w1 = expert_w([with_shared(i["L1_ffn_gate_w"], i["L1_ffn_shared_gate_w"]), with_shared(i["L1_ffn_up_w"], i["L1_ffn_shared_up_w"])],
                  with_shared(i["L1_ffn_down_w"], i["L1_ffn_shared_down_w"]))
    w2 = expert_w([i["L2_ffn_gate_w"], i["L2_ffn_up_w"]], i["L2_ffn_down_w"])
    w3 = expert_w([i["L3_ffn_W1"]], i["L3_ffn_W2"])

    arrays = {
        "x": i["x"].transpose(2, 0, 1).reshape(D, T), "cx": i["ctx_1024"].transpose(2, 0, 1), "const": const, "vec": vec, "row": row,
        "rw": rw, "bd": bd, "fside": i["fside_SxS2_0"],
        "pad": rows(i["mask_BxS2_bf0"]).reshape(128, B, SK),
        "keep": rows(i["mask_BxS2_bk1"]).reshape(128, B, SK),
        "wa0": wa0, "wa1": wa1, "wa2": wa2, "wa3": wa3, "w0": w0, "w1": w1, "w2": w2, "w3": w3,
    }
    nc = bacc.Bacc("TRN2", target_bir_lowering=False, num_devices=1)
    sent, aps = {}, {}
    for name, v in arrays.items():
        v = np.ascontiguousarray(v)
        sent["in_" + name] = v
        aps[name] = nc.dram_tensor("in_" + name, v.shape, mybir.dt.from_np(v.dtype), kind="ExternalInput").ap()
    out = nc.dram_tensor("out_0", (D, T), F32, kind="ExternalOutput").ap()
    build(nc, aps, out)
    r = run(nc, [sent], core_ids=[0])
    return r.results[0]["out_0"].reshape(D, B, S).transpose(1, 2, 0)
```

```python
from contextlib import ExitStack

import concourse.bass as bass
from concourse import mybir

F32 = mybir.dt.float32
BF16 = mybir.dt.bfloat16
U8 = mybir.dt.uint8
ACT = mybir.ActivationFunctionType
ALU = mybir.AluOpType
AX = mybir.AxisListType

B, S, D, SK = 8, 128, 128, 77
T = B * S
HALF = T // 2
E = 8
NEG = -1.0e30

HEADS = (16, 16, 16, 8)
HD = (8, 8, 64, 64)
KEYS = (SK, SK, SK, SK + S)
QSCALE = (1.0, 1.0, 64 ** -0.5, 1.0 / 64)
QC = tuple(max(1, h * d // D) for h, d in zip(HEADS, HD))
NC = (3, 4, 2, 4)
GATED = (True, True, True, False)

(BQ0, BK0, BV0, BO0, BQ1, BK1, BV1, BO1, G2, B2, BO2, XG3, XB3, LG3, LB3, OG3, OB3) = range(17)
GB2 = 17
UB2 = GB2 + E * NC[2]
B13 = UB2 + E * NC[2]
NVEC = B13 + E * NC[3]
GX, GF, GATE2, RB0, RB3 = 0, 4, 8, 9, 17
NROW = 25
IDENT, CENTER, MEAN, HMASK, REV = 0, 128, 256, 384, 400
ONES = 408
NCONST = 409
SHORT, LONG = 4, 20
RESIDUAL = 2.0e-6
GUESS = (-0.034, 1.02)


def build(nc, a, out):
    ctx = ExitStack()
    with ctx:
        def sb(name, shape, dt=F32):
            return ctx.enter_context(nc.sbuf_tensor(name, shape, dt))

        def sem(name):
            return ctx.enter_context(nc.semaphore(name))

        x = sb("x", [D, T])
        xn = sb("xn", [D, T])
        y = sb("y", [D, T])
        cx = sb("cx", [D, B, SK])
        cxn = sb("cxn", [D, B, SK])
        const = sb("const", [128, NCONST])
        vec = sb("vec", [128, NVEC])
        row = sb("row", [128, NROW])
        tg = sb("tg", [128, NROW])
        bad = sb("bad", [128, 1])
        bad_i = sb("bad_i", [1, 1], mybir.dt.int32)
        eps = sb("eps", [128, 1])
        rw = sb("rw", [D, 4, E])
        bd = sb("bd", [E, 4, D])
        fside = sb("fside", [S, SK])
        pad = sb("pad", [128, B, SK], U8)
        keep = sb("keep", [128, B, SK], U8)
        bias1 = sb("bias1", [128, B, KEYS[1]])
        bias3 = sb("bias3", [128, B, KEYS[3]])
        wa = [sb(f"wa{i}", [D, n]) for i, n in enumerate((512, 512, 4096, 2048))]
        sq = sb("sq", [128, 2, HALF])
        lnv = sb("lnv", [128, 2, HALF])
        rstd = sb("rstd", [128, 2, HALF])
        st = sb("st", [D, SK + S])
        q_sb = sb("q_sb", [128, 1024])
        k_sb = sb("k_sb", [128, SK])
        km = sb("km", [128, 1640])
        v_all = sb("v_all", [128, B, 1024])
        sc = sb("sc", [128, 1640])
        pr = sb("pr", [128, 1640])
        pt = sb("pt", [128, 2048])
        ind = sb("ind", [128, 16 * SK], BF16)
        col = sb("col", [128, 6, 16])
        o_sb = sb("o_sb", [128, 1024])
        ot_sb = sb("ot_sb", [128, 1024])
        W = [sb(f"W{i}", [128, 1536]) for i in range(2)]
        cT = sb("cT", [E, T])
        c3 = sb("c3", [128, B, 32], BF16)
        cT3 = sb("cT3", [128, T], BF16)
        sel = sb("sel", [128, E, 128], BF16)
        zeros = sb("zeros", [128, 128], BF16)
        identb = sb("identb", [128, 128], BF16)
        gs = sb("gs", [128, 2, HALF])
        tu = sb("tu", [128, 2, HALF])
        hb = sb("hb", [128, 4, HALF])
        rt = sb("rt", [128, 12, B, E])
        rc = sb("rc", [128, 6, B])

        ps = ctx.enter_context(nc.psum_tensor("ps", [128, 8, 512], F32))

        ident = const[:, IDENT:IDENT + 128]
        center = const[:, CENTER:CENTER + 128]
        mean = const[:, MEAN:MEAN + 128]
        ones = const[:, ONES:ONES + 1]
        hmask = const[:, HMASK:HMASK + 16]
        rev = const[:, REV:REV + E]

        def v1(i):
            return vec[:, i:i + 1]

        ld_x, ld_c, ld_cx, ld_t = sem("ld_x"), sem("ld_c"), sem("ld_cx"), sem("ld_t")
        ld_wa = [sem(f"ld_wa{i}") for i in range(4)]
        ld_w = [sem(f"ld_w{p}") for p in range(2)]
        init_v, init_g, tanh_s = sem("init_v"), sem("init_g"), sem("tanh_s")
        bias_s = sem("bias_s")
        x_rdy = sem("x_rdy")
        c_ps, sq_s, var_ps, ln_s, rs_s, xn_s, aff_s = (sem(n) for n in ("c_ps", "sq_s", "var_ps", "ln_s", "rs_s", "xn_s", "aff_s"))
        (stg, q_ps, q_s, k_ps, k_s, km_s, v_ps, v_s, s_ps, s_free, t_s, e_s, p_s, pt_ps, pt_s, pv_ps, o_s, ot_ps, ot_s, out_ps,
         y_s, kz) = (sem(n) for n in (
             "stg", "q_ps", "q_s", "k_ps", "k_s", "km_s", "v_ps", "v_s", "s_ps", "s_free", "t_s", "e_s", "p_s", "pt_ps", "pt_s",
             "pv_ps", "o_s", "ot_ps", "ot_s", "out_ps", "y_s", "kz"))
        dev_s, dev2_s, bad_s, bad_ps = sem("dev_s"), sem("dev2_s"), sem("bad_s"), sem("bad_ps")
        dch = sem("dch")
        lg_ps, rx_in, rx_s, comb_s, c3_s, ct_ps, ct_s, cb_ps, acc_ps, gu_ps, g_s, tu_s, h_s, dn_ps = (sem(n) for n in (
            "lg_ps", "rx_in", "rx_s", "comb_s", "c3_s", "ct_ps", "ct_s", "cb_ps", "acc_ps", "gu_ps", "g_s", "tu_s", "h_s", "dn_ps"))
        out_s = sem("out_s")
        passed = sem("passed")

        UNITS = [E * 2 * n for n in NC]
        U0 = [sum(UNITS[:i]) for i in range(4)]
        CT0 = (0, 1, 2, 4, 6)
        LN = []
        cxf, cxnf = cx[:].rearrange("p b s -> p (b s)"), cxn[:].rearrange("p b s -> p (b s)")
        CXH = B * SK // 2
        for i in range(2):
            LN.append((cxf[:, i * CXH:(i + 1) * CXH], cxnf[:, i * CXH:(i + 1) * CXH], CXH, XG3, XB3))

        def ln_pair(src, dst, g=None, b=None):
            at = len(LN)
            for i in range(2):
                LN.append((src[:, i * HALF:(i + 1) * HALF], dst[:, i * HALF:(i + 1) * HALF], HALF, g, b))
            return at

        LN_A, LN_A2, LN_F, LN_Y = [], {}, [], None
        for l in range(4):
            LN_A.append(ln_pair(x, xn))
            if l == 2:
                LN_A2[l] = ln_pair(xn, xn, G2, B2)
            if l == 3:
                LN_A2[l] = ln_pair(xn, xn, LG3, LB3)
                LN_Y = ln_pair(y, y, OG3, OB3)
            LN_F.append(ln_pair(x, xn))
        AFF = [sum(1 for u in LN[:i] if u[3] is not None) for i in range(len(LN) + 1)]

        def ln_done(eng, u):
            if LN[u][3] is None:
                eng.wait_ge(xn_s, u + 1)
            else:
                eng.wait_ge(aff_s, AFF[u + 1])

        def settled(eng):
            eng.sem_inc(passed, 1)

        block = ctx.enter_context(nc.Block())

        @block.sync
        def _(sp):
            sp.dma_start(const[:], a["const"]).then_inc(ld_c, 16)
            sp.dma_start(cx[:], a["cx"]).then_inc(ld_cx, 16)
            sp.dma_start(x[:], a["x"]).then_inc(ld_x, 16)
            for dst, name in ((vec, "vec"), (row, "row"), (rw, "rw"), (bd, "bd"), (fside, "fside"), (pad, "pad"), (keep, "keep"), (sel, "sel"), (identb, "identb")):
                sp.dma_start(dst[:], a[name]).then_inc(ld_t, 16)
            for l in range(4):
                sp.dma_start(wa[l][:], a[f"wa{l}"]).then_inc(ld_wa[l], 16)
            for l in range(4):
                w = a[f"w{l}"]
                n = w.shape[2]
                per = 2 * NC[l]
                if l:
                    sp.wait_ge(dn_ps, U0[l] + 4)
                for p in range(2):
                    sp.dma_start(W[p][:, 0:n], w[p]).then_inc(ld_w[p], 16)
                with sp.Fori(0, E // 2 - 1) as j:
                    for p in range(2):
                        sp.wait_ge(dn_ps, j * (2 * per) + (U0[l] + (p + 1) * per + 4))
                        sp.dma_start(W[p][:, 0:n], w[bass.ds(2 * j + (2 + p), 1)].rearrange("a p n -> (a p) n")).then_inc(ld_w[p], 16)
            for h in range(2):
                sp.wait_ge(x_rdy, 15 + h)
                sp.dma_start(out[:, h * HALF:(h + 1) * HALF], x[:, h * HALF:(h + 1) * HALF]).then_inc(out_s, 16)
            sp.wait_ge(out_s, 32)

        @block.tensor
        def _(pe):
            def layernorm(u0):
                for u in (u0, u0 + 1):
                    src, _, n, _, _ = LN[u]
                    pe.matmul(ps[:, u % 2, 0:n], center, src, start=True, stop=True).then_inc(c_ps, 1)
                for u in (u0, u0 + 1):
                    n = LN[u][2]
                    pe.wait_ge(sq_s, u + 1)
                    pe.matmul(ps[:, 2 + u % 2, 0:n], mean, sq[:, u % 2, 0:n], start=True, stop=True).then_inc(var_ps, 1)

            def keys(l, n):
                C, nk, w = QC[l], KEYS[l], wa[l]
                pe.wait_ge(stg, n + 1)
                if not isinstance(n, int) or n > 0:
                    pe.wait_ge(v_s, n)
                K0 = C * 128
                per = 4 if l == 2 else 2
                for c in range(C):
                    m = pe.matmul(ps[:, 6 + c // per, c % per * nk:c % per * nk + nk], w[:, K0 + c * 128:K0 + c * 128 + 128],
                                  st[:, 0:nk], start=True, stop=True)
                m.then_inc(k_ps, 1)

            def queries(l, n):
                C, w = QC[l], wa[l]
                pe.wait_ge(k_s if l < 2 else km_s, n + 1)
                for c in range(C):
                    m = pe.matmul(ps[:, 6 + c // 4, c % 4 * 128:c % 4 * 128 + 128], w[:, c * 128:c * 128 + 128],
                                  st[:, SK:SK + S], start=True, stop=True)
                m.then_inc(q_ps, 1)

            def values(l, n):
                w = wa[l]
                V0 = 2 * QC[l] * 128
                pe.wait_ge(q_s, n + 1)
                if l < 2:
                    m = pe.matmul(ps[0:SK, 6, 0:128], st[:, 0:SK], w[:, V0:V0 + 128], start=True, stop=True)
                elif l == 2:
                    for c in range(2):
                        m = pe.matmul(ps[0:SK, 6 + c, :], st[:, 0:SK], w[:, V0 + c * 512:V0 + c * 512 + 512], start=True, stop=True)
                else:
                    pe.matmul(ps[0:SK, 6, :], st[:, 0:SK], w[:, V0:V0 + 512], start=True, stop=True)
                    m = pe.matmul(ps[:, 7, :], st[:, SK:SK + S], w[:, V0:V0 + 512], start=True, stop=True)
                m.then_inc(v_ps, 1)

            def scores(l, n):
                pe.wait_ge(km_s, n + 1)
                if not isinstance(n, int) or n > 0:
                    pe.wait_ge(s_free, n)
                for t in range(4):
                    if l < 2:
                        m = pe.matmul(ps[:, t, 0:308], q_sb[:, 0:128], km[:, t * 308:t * 308 + 308], start=True, stop=True)
                    elif l == 2:
                        for c in (2 * t, 2 * t + 1):
                            m = pe.matmul(ps[:, t, c % 2 * 154:c % 2 * 154 + 154], q_sb[:, c * 128:c * 128 + 128],
                                          km[:, c * 154:c * 154 + 154], start=True, stop=True)
                    else:
                        m = pe.matmul(ps[:, t, 0:410], q_sb[:, t * 128:t * 128 + 128], km[:, t * 410:t * 410 + 410], start=True, stop=True)
                m.then_inc(s_ps, 1)

            def turn(l, n, last):
                pe.wait_ge(y_s, n + 1)
                if l == 0:
                    pe.wait_ge(bad_s, n + 1)
                    pe.matmul(ps[0:1, 4, 0:1], bad[:], ones[:, 0:1], start=True, stop=True).then_inc(bad_ps, 1)
                pe.wait_ge(p_s, n + 1)
                for g in range(4):
                    if g == 2:
                        pe.wait_ge(v_s, n + (1 if last else 2))
                    for i in range(4):
                        if l < 3:
                            h = 4 * g + i
                            m = pe.transpose(ps[0:SK, 4 + g, i * 128:i * 128 + 128], pr[:, h * SK:h * SK + SK], ident)
                        elif i < 2:
                            h = 2 * g + i
                            m = pe.transpose(ps[0:SK, 4 + g, i * 128:i * 128 + 128], pr[:, h * 205:h * 205 + SK], ident)
                        else:
                            h = 2 * g + i - 2
                            m = pe.transpose(ps[:, 4 + g, i * 128:i * 128 + 128], pr[:, h * 205 + SK:h * 205 + 205], ident)
                    m.then_inc(pt_ps, 1)
                pe.wait_ge(pt_s, n * 4 + 4)

            def weigh(l, n, b):
                for h in range(HEADS[l]):
                    d = HD[l]
                    o = ps[:, 4 + h * d // 512, h * d % 512:h * d % 512 + d]
                    if l < 3:
                        m = pe.matmul(o, pt[0:SK, h * 128:h * 128 + 128], v_at(b)[0:SK, h * d:h * d + d], start=True, stop=True)
                    else:
                        c0 = h // 2 * 512 + h % 2 * 128
                        pe.matmul(o, pt[0:SK, c0:c0 + 128], v_at(b)[0:SK, h * d:h * d + d], start=True, stop=False)
                        m = pe.matmul(o, pt[:, c0 + 256:c0 + 384], v_at(b)[:, 512 + h * d:512 + h * d + d], start=False, stop=True)
                m.then_inc(pv_ps, 1)

            def turn_out(l, n):
                pe.wait_ge(o_s, n + 1)
                for c in range(QC[l]):
                    m = pe.transpose(ps[:, 4 + c // 4, c % 4 * 128:c % 4 * 128 + 128], o_sb[:, c * 128:c * 128 + 128], ident)
                m.then_inc(ot_ps, 1)

            def project(l, n):
                C, w = QC[l], wa[l]
                pe.wait_ge(ot_s, n + 1)
                O0 = {0: 384, 1: 384, 2: 3072, 3: 1536}[l]
                for c in range(C):
                    m = pe.matmul(ps[:, 4, 0:128], w[:, O0 + c * 128:O0 + c * 128 + 128], ot_sb[:, c * 128:c * 128 + 128],
                                  start=(c == 0), stop=(c == C - 1))
                m.then_inc(out_ps, 1)

            def v_at(b):
                return v_all[:, b, :] if isinstance(b, int) else v_all[:, bass.ds(b, 1), :].rearrange("p a n -> p (a n)")

            def attention(l):
                pe.wait_ge(ld_wa[l], 16)
                n0 = B * l
                for n in (n0, n0 + 1):
                    keys(l, n)
                    queries(l, n)
                    values(l, n)
                    scores(l, n)
                with pe.Fori(0, B - 2) as b:
                    n = b + n0
                    turn(l, n, False)
                    keys(l, b + (n0 + 2))
                    weigh(l, n, b)
                    queries(l, b + (n0 + 2))
                    turn_out(l, n)
                    values(l, b + (n0 + 2))
                    project(l, n)
                    scores(l, b + (n0 + 2))
                for b in (B - 2, B - 1):
                    turn(l, n0 + b, b == B - 1)
                    weigh(l, n0 + b, b)
                    turn_out(l, n0 + b)
                    project(l, n0 + b)

            def experts(l):
                n, H = NC[l], NC[l] * 128
                up, down = H, (2 * H if GATED[l] else H)
                ln_done(pe, LN_F[l] + 1)
                NU = 4 * n

                def place(i):
                    return i // (2 * n), i // n % 2, i % n

                def spread(j, i):
                    p, h, _ = place(i)
                    e = 2 * j + p
                    w = sel[:, e, :] if isinstance(e, int) else sel[:, bass.ds(e, 1), :].rearrange("p a n -> p (a n)")
                    return pe.matmul(ps[:, 6 + h, :], w, cT3[:, h * HALF:h * HALF + HALF], start=True, stop=True)

                def gate_up(u, i):
                    p, h, c = place(i)
                    if GATED[l]:
                        pe.wait_ge(tu_s, u + 1)
                    else:
                        pe.wait_ge(g_s, u - 1)
                    xs = xn[:, h * HALF:h * HALF + HALF]
                    m = pe.matmul(ps[:, i % 2, :], W[p][:, c * 128:c * 128 + 128], xs, start=True, stop=True)
                    if GATED[l]:
                        m = pe.matmul(ps[:, 2 + i % 2, :], W[p][:, up + c * 128:up + c * 128 + 128], xs, start=True, stop=True)
                    m.then_inc(gu_ps, 1)

                def down_(u, i):
                    p, h, c = place(i)
                    pe.wait_ge(h_s, u + 3)
                    pe.matmul(ps[:, 4 + h, :], W[p][:, down + c * 128:down + c * 128 + 128], hb[:, i % 4, :],
                              start=False, stop=False, skip_group_check=True).then_inc(dn_ps, 1)

                def pair(j, last):
                    for i in range(NU):
                        k = i + 2
                        if k < NU:
                            if k == 2 * n:
                                pe.wait_ge(ld_w[1], (j + (4 * l + 1)) * 16)
                            if k % n == 0 and k > 0:
                                spread(j, k)
                            gate_up(j * NU + (U0[l] + k), k)
                        elif not last:
                            if k == NU:
                                pe.wait_ge(ld_w[0], (j + (4 * l + 2)) * 16)
                                spread(j + 1, 0)
                            if k - NU == n:
                                spread(j + 1, k - NU)
                            gate_up(j * NU + (U0[l] + k), k - NU)
                        down_(j * NU + (U0[l] + i), i)

                for t in range(B):
                    m = pe.matmul(ps[:, 7, t * E:t * E + E], xn[:, t * S:t * S + S], rw[:, l, :], start=True, stop=True)
                m.then_inc(lg_ps, 1)
                pe.wait_ge(ld_w[0], 16 * (4 * l + 1))
                gate_up(U0[l], 0)
                gate_up(U0[l] + 1, 1)
                pe.wait_ge(c3_s, l + 1)
                c3b = ps[:, 5, :].bitcast(BF16)
                for t in range(B):
                    m = pe.transpose(c3b[0:32, t * 128:t * 128 + 128], c3[:, t, :], identb[:])
                m.then_inc(ct_ps, 1)
                if l >= 2:
                    for t in range(B):
                        m = pe.transpose(ps[0:E, 6 + t // 4, t % 4 * 128:t % 4 * 128 + 128], rt[:, 9, t, :], ident)
                    m.then_inc(ct_ps, 1)
                pe.wait_ge(ct_s, CT0[l] + (2 if l >= 2 else 1))
                spread(0, 0).then_inc(cb_ps, 1)
                for h in range(2):
                    pe.matmul(ps[:, 4 + h, :], zeros[:], cT3[:, 0:HALF], start=True, stop=False, skip_group_check=True)
                with pe.Fori(0, E // 2 - 1) as j:
                    pair(j, False)
                pair(E // 2 - 1, True)
                for h in range(2):
                    if l >= 2:
                        m = pe.matmul(ps[:, 4 + h, :], bd[:, l, :], cT[:, h * HALF:h * HALF + HALF], start=False, stop=True,
                                      skip_group_check=True)
                    else:
                        m = pe.matmul(ps[:, 4 + h, :], zeros[:], cT3[:, 0:HALF], start=False, stop=True, skip_group_check=True)
                    m.then_inc(acc_ps, 1)

            pe.wait_ge(ld_c, 16)
            pe.wait_ge(ld_cx, 16)
            layernorm(0)
            pe.wait_ge(ld_x, 16)
            pe.wait_ge(ld_t, 16 * 9)
            ln_done(pe, 1)
            for l in range(4):
                if l:
                    pe.wait_ge(x_rdy, 4 * l)
                layernorm(LN_A[l])
                if l in LN_A2:
                    ln_done(pe, LN_A[l])
                    ln_done(pe, LN_A[l] + 1)
                    layernorm(LN_A2[l])
                    ln_done(pe, LN_A2[l] + 1)
                else:
                    ln_done(pe, LN_A[l] + 1)
                attention(l)
                if l == 3:
                    pe.wait_ge(y_s, B * 4 + 1)
                    layernorm(LN_Y)
                pe.wait_ge(x_rdy, 4 * l + 2)
                layernorm(LN_F[l])
                experts(l)

        @block.scalar
        def _(act):
            def layernorm(u0):
                for u in (u0, u0 + 1):
                    n = LN[u][2]
                    act.wait_ge(c_ps, u + 1)
                    act.activation(sq[:, u % 2, 0:n], ps[:, u % 2, 0:n], ACT.Square).then_inc(sq_s, 1)
                for u in (u0, u0 + 1):
                    n = LN[u][2]
                    act.wait_ge(var_ps, u + 1)
                    act.activation(lnv[:, u % 2, 0:n], ps[:, 2 + u % 2, 0:n], ACT.Ln, bias=eps[:, 0:1]).then_inc(ln_s, 1)
                for u in (u0, u0 + 1):
                    n = LN[u][2]
                    act.wait_ge(ln_s, u + 1)
                    act.activation(rstd[:, u % 2, 0:n], lnv[:, u % 2, 0:n], ACT.Exp, scale=-0.5).then_inc(rs_s, 1)

            def keys(l, n):
                C, nk = QC[l], KEYS[l]
                act.wait_ge(k_ps, n + 1)
                if not isinstance(n, int) or n > 0:
                    act.wait_ge(s_ps, n)
                if l < 2:
                    if not isinstance(n, int) or n > 0:
                        act.wait_ge(km_s, n)
                    act.activation(k_sb[:, :], ps[:, 6, 0:SK], ACT.Identity, bias=v1((BK0, BK1)[l])).then_inc(k_s, 1)
                else:
                    per = 4 if l == 2 else 2
                    act.wait_ge(kz, l - 1)
                    kv = km[:, 0:C * 2 * nk].rearrange("p (u c a s) -> p u c a s", u=2, a=2, s=nk)
                    pv = ps[:, 6:8, 0:per * nk].rearrange("p u (c s) -> p u c s", s=nk)
                    act.activation(kv[0:64, :, :, 0, :], pv[0:64], ACT.Copy)
                    act.activation(kv[64:128, :, :, 1, :], pv[64:128], ACT.Copy).then_inc(km_s, 1)

            def queries(l, n):
                C = QC[l]
                act.wait_ge(q_ps, n + 1)
                if l < 2:
                    act.activation(q_sb[:, 0:128], ps[:, 6, 0:128], ACT.Identity, bias=v1((BQ0, BQ1)[l])).then_inc(q_s, 1)
                else:
                    act.activation(q_sb[:, 0:C * 128], ps[:, 6:6 + C // 4, :], ACT.Copy, scale=QSCALE[l]).then_inc(q_s, 1)

            def values(l, n, b):
                act.wait_ge(v_ps, n + 1)
                settled(act)
                if l < 2:
                    act.activation(vb(b, 0, SK, 0, 128), ps[0:SK, 6, 0:128], ACT.Copy).then_inc(v_s, 1)
                elif l == 2:
                    act.activation(vb(b, 0, SK, 0, 1024), ps[0:SK, 6:8, :], ACT.Copy).then_inc(v_s, 1)
                else:
                    act.activation(vb(b, 0, SK, 0, 512), ps[0:SK, 6, :], ACT.Copy)
                    act.activation(vb(b, 0, 128, 512, 1024), ps[:, 7, :], ACT.Copy).then_inc(v_s, 1)

            def vb(b, p0, p1, c0, c1):
                if isinstance(b, int):
                    return v_all[p0:p1, b, c0:c1]
                return v_all[p0:p1, bass.ds(b, 1), c0:c1].rearrange("p a n -> p (a n)")

            def exps(l, n):
                W_ = HEADS[l] * KEYS[l]
                act.wait_ge(t_s, n + 1)
                if l:
                    act.activation(pr[:, 0:W_], sc[:, 0:W_], ACT.Exp).then_inc(e_s, 1)
                else:
                    act.activation(pr[:, 0:W_], sc[:, 0:W_], ACT.Square).then_inc(e_s, 1)
                    act.wait_ge(dev_s, n + 1)
                    act.activation(col[:, 5, :], col[:, 5, :], ACT.Sqrt).then_inc(dev2_s, 1)

            def turned(l, n):
                for g in range(4):
                    act.wait_ge(pt_ps, n * 4 + (g + 1))
                    if l < 3:
                        act.activation(pt[0:SK, g * 512:g * 512 + 512], ps[0:SK, 4 + g, :], ACT.Copy).then_inc(pt_s, 1)
                    else:
                        act.activation(pt[0:SK, g * 512:g * 512 + 256], ps[0:SK, 4 + g, 0:256], ACT.Copy)
                        act.activation(pt[:, g * 512 + 256:g * 512 + 512], ps[:, 4 + g, 256:512], ACT.Copy).then_inc(pt_s, 1)

            def outs(l, n):
                C = QC[l]
                nb = max(1, C // 4)
                act.wait_ge(pv_ps, n + 1)
                act.activation(o_sb[:, 0:C * 128], ps[:, 4:4 + nb, 0:C * 128 // nb], ACT.Copy).then_inc(o_s, 1)

            def turned_outs(l, n):
                C = QC[l]
                nb = max(1, C // 4)
                act.wait_ge(ot_ps, n + 1)
                if l < 2:
                    act.activation(ot_sb[:, 0:128], ps[:, 4, 0:128], ACT.Identity, bias=v1((BV0, BV1)[l])).then_inc(ot_s, 1)
                else:
                    act.activation(ot_sb[:, 0:C * 128], ps[:, 4:4 + nb, 0:C * 128 // nb], ACT.Copy).then_inc(ot_s, 1)

            def projected(l, n, b):
                act.wait_ge(out_ps, n + 1)
                settled(act)
                yb = y[:, b * S:b * S + S] if isinstance(b, int) else y[:, bass.ds(b * S, S)]
                if l < 3:
                    act.activation(yb, ps[:, 4, 0:128], ACT.Identity, bias=v1((BO0, BO1, BO2)[l])).then_inc(y_s, 1)
                else:
                    act.activation(yb, ps[:, 4, 0:128], ACT.Copy).then_inc(y_s, 1)

            def attention(l):
                n0 = B * l
                for b in (0, 1):
                    keys(l, n0 + b)
                    queries(l, n0 + b)
                    values(l, n0 + b, b)
                    if b == 0:
                        exps(l, n0)
                with act.Fori(0, B - 2) as b:
                    turned(l, b + n0)
                    keys(l, b + (n0 + 2))
                    exps(l, b + (n0 + 1))
                    outs(l, b + n0)
                    queries(l, b + (n0 + 2))
                    turned_outs(l, b + n0)
                    values(l, b + (n0 + 2), b + 2)
                    projected(l, b + n0, b)
                for b in (B - 2, B - 1):
                    turned(l, n0 + b)
                    if b == B - 2:
                        exps(l, n0 + B - 1)
                    outs(l, n0 + b)
                    turned_outs(l, n0 + b)
                    projected(l, n0 + b, b)

            def experts(l):
                n = NC[l]
                act.wait_ge(rx_in, l + 1)
                act.activation(rt[:, 1], rt[:, 0], ACT.Exp, scale=-1.0 if l == 0 else 1.0).then_inc(rx_s, 1)
                with act.Fori(0, E // 2) as j:
                    for i in range(4 * n):
                        u = j * (4 * n) + (U0[l] + i)
                        p, c = i // (2 * n), i % n
                        act.wait_ge(gu_ps, u + 1)
                        if not GATED[l]:
                            act.wait_ge(h_s, u + 1)
                        if l >= 2:
                            settled(act)
                        if l < 2:
                            act.activation(gs[:, i % 2, :], ps[:, i % 2, :], ACT.Silu).then_inc(g_s, 1)
                        else:
                            c0 = {2: GB2, 3: B13}[l] + p * n + c
                            bias = vec[:, bass.ds(j * (2 * n) + c0, 1)]
                            act.activation(gs[:, i % 2, :], ps[:, i % 2, :], ACT.Silu if l == 2 else ACT.Relu, bias=bias).then_inc(g_s, 1)

            act.wait_ge(ld_t, 16 * 9)
            act.wait_ge(init_v, 4)
            act.activation(tg[:], row[:], ACT.Tanh).then_inc(tanh_s, 1)
            layernorm(0)
            for l in range(4):
                layernorm(LN_A[l])
                if l in LN_A2:
                    layernorm(LN_A2[l])
                attention(l)
                if l == 3:
                    layernorm(LN_Y)
                layernorm(LN_F[l])
                experts(l)

        @block.gpsimd
        def _(g):
            g.sem_inc(dn_ps, 4)
            g.sem_inc(h_s, 2)
            g.sem_inc(tu_s, 2)
            g.sem_inc(y_s, 1)

            def stage(l, n, b):
                if not isinstance(n, int) or n > 0:
                    g.wait_ge(v_ps, n)
                settled(g)
                src = cxn if l == 3 else cx
                cb = src[:, b, :] if isinstance(b, int) else src[:, bass.ds(b, 1), :].rearrange("p a s -> p (a s)")
                xb = xn[:, b * S:b * S + S] if isinstance(b, int) else xn[:, bass.ds(b * S, S)]
                g.tensor_copy(st[:, 0:SK], cb)
                g.tensor_copy(st[:, SK:SK + S], xb).then_inc(stg, 1)
                if l < 2:
                    g.wait_ge(k_s, n + 1)
                    if not isinstance(n, int) or n > 0:
                        g.wait_ge(s_ps, n)
                    g.tensor_tensor(km[:, 0:1232].rearrange("p (h s) -> p h s", s=SK),
                                    k_sb[:, :].unsqueeze(1).to_broadcast([128, 16, SK]),
                                    hmask.unsqueeze(2).to_broadcast([128, 16, SK]), ALU.mult).then_inc(km_s, 1)

            g.wait_ge(ld_cx, 16)
            for l in range(4):
                if l >= 2:
                    g.wait_ge(s_ps, B * l)
                    g.memset(km[:], 0.0).then_inc(kz, 1)
                u = LN_A2.get(l, LN_A[l])
                ln_done(g, u)
                ln_done(g, u + 1)
                stage(l, B * l, 0)
                with g.Fori(1, B) as b:
                    stage(l, b + B * l, b)

        @block.vector
        def _(v):
            steps = [0]

            class Steps:

                def __init__(self, turn=0, per=0):
                    self.turn, self.per, self.k = turn, per, 0

                def __call__(self, ins):
                    self.k += 1
                    ins.then_inc(dch, 1)
                    v.wait_ge(dch, self.turn * self.per + (steps[0] + self.k))

                def mark(self):
                    return self.k

                def within(self, at, turn=0, per=0):
                    def step(ins, k=[0]):
                        k[0] += 1
                        ins.then_inc(dch, 1)
                        v.wait_ge(dch, self.turn * self.per + (steps[0] + at + k[0]) + turn * per)
                    return step

                def skip(self, k):
                    self.k += k

                def end(self, turns=1):
                    assert self.turn is 0 or self.k == self.per, self.k
                    steps[0] += self.k * turns

            def layernorm(u0):
                for u in (u0, u0 + 1):
                    _, dst, n, g, b = LN[u]
                    v.wait_ge(rs_s, u + 1)
                    v.tensor_tensor(dst, ps[:, u % 2, 0:n], rstd[:, u % 2, 0:n], ALU.mult).then_inc(xn_s, 1)
                    if g is not None:
                        v.wait_ge(xn_s, u + 1)
                        v.tensor_scalar(dst, dst, v1(g), v1(b), ALU.mult, ALU.add).then_inc(aff_s, 1)

            def heads(ap, l):
                h, nk = HEADS[l], KEYS[l]
                return ap.rearrange("p (u h s) -> p u h s", u=4, s=nk)

            def softmax(l, n, b, step):
                h, nk = HEADS[l], KEYS[l]
                W_ = h * nk
                hs = [128, 4, h // 4, nk]
                S4 = ps[:, 0:4, 0:W_ // 4].rearrange("p u (h s) -> p u h s", s=nk)
                T4 = heads(sc[:, 0:W_], l)
                P3 = pr[:, 0:W_].rearrange("p (h s) -> p h s", s=nk)
                c = [col[:, i, 0:h] for i in range(6)]
                c4 = [x_.rearrange("p (u h) -> p u h", u=4) for x_ in c]
                v.wait_ge(s_ps, n + 1)
                if l in (1, 3):
                    tab = bias1 if l == 1 else bias3
                    bb = tab[:, b, :] if isinstance(b, int) else tab[:, bass.ds(b, 1), :].rearrange("p a s -> p (a s)")
                    step(v.tensor_tensor(T4, S4, bb.unsqueeze(1).unsqueeze(1).to_broadcast(hs), ALU.add))
                    v.sem_inc(s_free, 1)
                    step(v.reduce_max(c4[0], T4, AX.X))
                    v.tensor_tensor(T4, T4, c4[0].unsqueeze(3).to_broadcast(hs), ALU.subtract).then_inc(t_s, 1)
                else:
                    step(v.reduce_max(c4[0], S4, AX.X))
                    step(v.tensor_tensor(T4, S4, c4[0].unsqueeze(3).to_broadcast(hs), ALU.subtract))
                    v.sem_inc(s_free, 1)
                    v.sem_inc(t_s, 1)
                v.wait_ge(e_s, n + 1)
                step(v.tensor_reduce(c[1], P3, AX.X, ALU.add))
                step(v.reciprocal(c[2], c[1]))
                v.tensor_tensor(P3, P3, c[2].unsqueeze(2).to_broadcast([128, h, nk]), ALU.mult).then_inc(p_s, 1)

            def sparsemax(n, step):
                hs = [128, 4, 4, SK]
                S4 = ps[:, 0:4, 0:308].rearrange("p u (h s) -> p u h s", s=SK)
                T4 = heads(sc[:, 0:1232], 0)
                T3 = sc[:, 0:1232].rearrange("p (h s) -> p h s", s=SK)
                P3 = pr[:, 0:1232].rearrange("p (h s) -> p h s", s=SK)
                I3 = ind[:].rearrange("p (h s) -> p h s", s=SK)
                top, avg, tau, f, cnt, dev = (col[:, i, :] for i in range(6))

                def newton(step):
                    step(v.tensor_tensor(P3, T3, tau.unsqueeze(2).to_broadcast([128, 16, SK]), ALU.subtract))
                    step(v.tensor_scalar(ind[:], pr[:, 0:1232], 0.0, None, ALU.is_gt))
                    step(v.tensor_scalar(pr[:, 0:1232], pr[:, 0:1232], 0.0, None, ALU.max))
                    step(v.tensor_reduce(f, P3, AX.X, ALU.add))
                    step(v.tensor_reduce(cnt, I3, AX.X, ALU.add))
                    step(v.reciprocal(cnt, cnt))
                    step(v.scalar_tensor_tensor(out=f, in0=f, scalar=-1.0, in1=cnt, op0=ALU.add, op1=ALU.mult))
                    step(v.tensor_tensor(tau, tau, f, ALU.add))

                def rows_sum(step):
                    step(v.tensor_tensor(P3, T3, tau.unsqueeze(2).to_broadcast([128, 16, SK]), ALU.subtract))
                    step(v.tensor_scalar(pr[:, 0:1232], pr[:, 0:1232], 0.0, None, ALU.max))

                v.wait_ge(s_ps, n + 1)
                step(v.reduce_max(top.rearrange("p (u h) -> p u h", u=4), S4, AX.X))
                step(v.tensor_tensor(T4, S4, top.rearrange("p (u h) -> p u h", u=4).unsqueeze(3).to_broadcast(hs), ALU.subtract))
                v.sem_inc(s_free, 1)
                v.sem_inc(t_s, 1)
                step(v.tensor_reduce(avg, T3, AX.X, ALU.add))
                step(v.tensor_scalar(avg, avg, 1.0 / SK, None, ALU.mult))
                step(v.tensor_tensor(f, avg, avg, ALU.mult))
                v.wait_ge(e_s, n + 1)
                step(v.tensor_reduce(dev, P3, AX.X, ALU.add))
                step(v.scalar_tensor_tensor(out=dev, in0=dev, scalar=1.0 / SK, in1=f, op0=ALU.mult, op1=ALU.subtract))
                step(v.tensor_scalar(dev, dev, 0.0, None, ALU.max))
                v.sem_inc(dev_s, 1)
                v.wait_ge(dev2_s, n + 1)
                step(v.tensor_scalar(dev, dev, GUESS[1], GUESS[0], ALU.mult, ALU.add))
                step(v.tensor_tensor(tau, dev, avg, ALU.add))
                step(v.tensor_scalar(tau, tau, -1.0 / SK, -1.0, ALU.min, ALU.max))
                for _ in range(SHORT):
                    newton(step)
                rows_sum(step)
                step(v.tensor_reduce(f, P3, AX.X, ALU.add))
                step(v.tensor_scalar(f, f, -1.0, None, ALU.add))
                step(v.tensor_tensor(f, f, f, ALU.mult))
                step(v.reduce_max(bad[:], f, AX.X))
                step(v.tensor_scalar(bad[:], bad[:], RESIDUAL ** 2, None, ALU.is_gt))
                v.sem_inc(bad_s, 1)
                v.wait_ge(bad_ps, n + 1)
                step(v.tensor_copy(bad_i[:], ps[0:1, 4, 0:1]))
                settled(v)
                left = v.value_load(bad_i[0:1, 0:1], min_val=0, max_val=128)
                at = step.mark()
                with v.If(left > 0):
                    again = step.within(at)
                    again(v.tensor_scalar(tau, avg, 0.0, -1.0, ALU.mult, ALU.add))
                    settled(v)
                    with v.Fori(0, LONG) as i:
                        turn = step.within(at + 1, i, 8)
                        newton(turn)
                    again = step.within(at + 1 + 8 * LONG)
                    rows_sum(again)
                    settled(v)
                with v.Else():
                    v.sem_inc(dch, 1 + 8 * LONG + 2)
                step.skip(1 + 8 * LONG + 2)
                v.sem_inc(p_s, 1)

            def attention(l):
                n0 = B * l
                per = {0: 11 + 8 * SHORT + 2 + 5 + 1 + 8 * LONG + 2 + 1, 2: 4}.get(l, 4)
                step = Steps()
                if l == 0:
                    sparsemax(n0, step)
                else:
                    softmax(l, n0, 0, step)
                step.end()
                with v.Fori(0, B - 1) as b:
                    step = Steps(b, per)
                    if l == 0:
                        sparsemax(b + (n0 + 1), step)
                    else:
                        softmax(l, b + (n0 + 1), b + 1, step)
                step.end(B - 1)

            def route(l):
                step = Steps()
                n = E - 1 if l == 0 else E
                L, X, Pb, oh1, oh2, w1, w2, val = (rt[:, i, :, 0:n] for i in range(8))
                res = rt[:, 9]
                m1, m2, s1, s2, r1 = (rc[:, i, :] for i in range(5))
                bc = [128, B, n]
                rv = rev[:, 0:n].unsqueeze(1).to_broadcast(bc)

                def spread(c):
                    return c.unsqueeze(2).to_broadcast(bc)

                def first_max(values, m, oh):
                    step(v.reduce_max(m, values, AX.X))
                    step(v.tensor_tensor(oh, values, spread(m), ALU.is_equal))
                    step(v.tensor_tensor(oh, oh, rv, ALU.mult))
                    step(v.reduce_max(s2, oh, AX.X))
                    step(v.tensor_tensor(oh, rv, spread(s2), ALU.is_equal))

                v.wait_ge(lg_ps, l + 1)
                logits = ps[:, 7, 0:B * E].rearrange("p (t e) -> p t e", e=E)
                if l in (0, 3):
                    rb = row[:, (RB0 if l == 0 else RB3):][:, 0:E].unsqueeze(1).to_broadcast([128, B, E])
                    step(v.tensor_tensor(rt[:, 0], logits, rb, ALU.add))
                    if l == 0:
                        v.sem_inc(rx_in, 1)
                        v.wait_ge(rx_s, 1)
                        step(v.tensor_scalar(w1, X, 1.0, None, ALU.add))
                        step(v.reciprocal(val, w1))
                    else:
                        step(v.tensor_copy(val, L))
                else:
                    step(v.tensor_copy(val, logits))
                first_max(val, m1, oh1)
                if l:
                    step(v.tensor_tensor(L, val, spread(m1), ALU.subtract))
                    v.sem_inc(rx_in, 1)
                if l != 1:
                    step(v.scalar_tensor_tensor(out=w2, in0=oh1, scalar=NEG, in1=val, op0=ALU.mult, op1=ALU.add))
                    first_max(w2, m2, oh2)
                    step(v.tensor_tensor(oh2, oh1, oh2, ALU.add))
                if l:
                    v.wait_ge(rx_s, l + 1)
                if l == 1:
                    step(v.tensor_reduce(s1, X, AX.X, ALU.add))
                    step(v.reciprocal(r1, s1))
                    step(v.scalar_tensor_tensor(out=res, in0=oh1, scalar=2.0, in1=spread(r1), op0=ALU.mult, op1=ALU.mult))
                    step(v.memset(res[:, :, E - 1:E], 1.0))
                    parts(l, step)
                    return
                src = val if l == 0 else X
                if l == 2:
                    step(v.tensor_reduce(s1, X, AX.X, ALU.add))
                    step(v.reciprocal(r1, s1))
                    step(v.tensor_tensor(Pb, X, spread(r1), ALU.mult))
                    src = Pb
                step(v.tensor_tensor(w1, src, oh2, ALU.mult))
                step(v.tensor_reduce(s1, w1, AX.X, ALU.add))
                if l == 2:
                    step(v.tensor_scalar(s1, s1, 1e-9, None, ALU.add))
                step(v.reciprocal(r1, s1))
                if l == 0:
                    step(v.memset(res[:, :, E - 1:E], 1.0))
                step(v.tensor_tensor(res[:, :, 0:n], w1, spread(r1), ALU.mult))
                parts(l, step)

            def parts(l, step):
                c, r1, r2 = rt[:, 9], rt[:, 10], rt[:, 11]
                step(v.tensor_copy(c3[:, :, 0:E], c))
                step(v.tensor_tensor(r1, c, c3[:, :, 0:E], ALU.subtract))
                step(v.tensor_copy(c3[:, :, E:2 * E], r1))
                step(v.tensor_tensor(r2, r1, c3[:, :, E:2 * E], ALU.subtract))
                step(v.tensor_copy(c3[:, :, 2 * E:3 * E], r2))
                v.sem_inc(c3_s, 1)
                v.wait_ge(ct_ps, CT0[l] + 1)
                v.tensor_copy(cT3[0:32, :], ps[0:32, 5, :].bitcast(BF16)).then_inc(ct_s, 1)
                if l >= 2:
                    v.wait_ge(ct_ps, CT0[l] + 2)
                    v.tensor_copy(cT[:].rearrange("e (u n) -> e u n", u=2), ps[0:E, 6:8, :]).then_inc(ct_s, 1)
                step.end()

            def experts(l):
                n = NC[l]
                route(l)
                v.wait_ge(cb_ps, l + 1)
                with v.Fori(0, E // 2) as j:
                    for i in range(4 * n):
                        u = j * (4 * n) + (U0[l] + i)
                        p, h, c = i // (2 * n), i // n % 2, i % n
                        coef = ps[:, 6 + h, :]
                        v.wait_ge(g_s, u + 1)
                        if l < 3:
                            v.wait_ge(h_s, u + 1)
                            if l == 2:
                                ub = vec[:, bass.ds(j * (2 * n) + (UB2 + p * n + c), 1)]
                                v.scalar_tensor_tensor(out=tu[:, i % 2, :], in0=ps[:, 2 + i % 2, :], scalar=ub, in1=gs[:, i % 2, :],
                                                       op0=ALU.add, op1=ALU.mult).then_inc(tu_s, 1)
                            else:
                                v.tensor_tensor(tu[:, i % 2, :], ps[:, 2 + i % 2, :], gs[:, i % 2, :], ALU.mult).then_inc(tu_s, 1)
                            v.wait_ge(dn_ps, u + 1)
                            v.wait_ge(tu_s, u + 3)
                            v.tensor_tensor(hb[:, i % 4, :], tu[:, i % 2, :], coef, ALU.mult).then_inc(h_s, 1)
                        else:
                            v.wait_ge(dn_ps, u + 1)
                            v.tensor_tensor(hb[:, i % 4, :], gs[:, i % 2, :], coef, ALU.mult).then_inc(h_s, 1)
                for h in range(2):
                    v.wait_ge(acc_ps, 2 * l + h + 1)
                    xs = x[:, h * HALF:h * HALF + HALF]
                    v.scalar_tensor_tensor(out=xs, in0=ps[:, 4 + h, :], scalar=tg[:, GF + l:GF + l + 1], in1=xs,
                                           op0=ALU.mult, op1=ALU.add).then_inc(x_rdy, 1)

            def residual(l):
                if l < 3:
                    v.wait_ge(y_s, B * (l + 1) + 1)
                for h in range(2):
                    if l == 3:
                        ln_done(v, LN_Y + h)
                    xs, ys = x[:, h * HALF:h * HALF + HALF], y[:, h * HALF:h * HALF + HALF]
                    v.scalar_tensor_tensor(out=xs, in0=ys, scalar=tg[:, GX + l:GX + l + 1], in1=xs,
                                           op0=ALU.mult, op1=ALU.add).then_inc(x_rdy, 1)

            v.memset(c3[:], 0.0).then_inc(init_v, 1)
            v.memset(cT3[:], 0.0).then_inc(init_v, 1)
            v.memset(zeros[:], 0.0).then_inc(init_v, 1)
            v.memset(eps[:], 1e-5).then_inc(init_v, 1)
            v.wait_ge(init_v, 4)
            v.wait_ge(ld_t, 16 * 9)
            step = Steps()
            step(v.tensor_scalar(bias1[:], pad[:], NEG, None, ALU.mult))
            step(v.tensor_tensor(bias1[:], bias1[:], fside[:].unsqueeze(1).to_broadcast([128, B, SK]), ALU.add))
            step(v.tensor_scalar(bias3[:, :, 0:SK], keep[:], -1.0, -NEG, ALU.add, ALU.mult))
            step(v.memset(bias3[:, :, SK:SK + S], 0.0))
            v.wait_ge(tanh_s, 1)
            step(v.tensor_tensor(tg[:, GX + 2:GX + 3], tg[:, GX + 2:GX + 3], tg[:, GATE2:GATE2 + 1], ALU.mult))
            step.end()
            layernorm(0)
            for l in range(4):
                layernorm(LN_A[l])
                if l in LN_A2:
                    layernorm(LN_A2[l])
                attention(l)
                if l == 3:
                    layernorm(LN_Y)
                residual(l)
                layernorm(LN_F[l])
                experts(l)


def kernel(**inputs):
    import numpy as np
    import concourse.bacc as bacc
    from concourse.bass_utils import run_bass_kernel_spmd as run

    i = {k: np.asarray(v) for k, v in inputs.items()}
    f = np.float32

    def rows(v, n=None):
        v = v.reshape(1, -1)
        return np.broadcast_to(v, (128, v.shape[1]))

    const = np.zeros((128, NCONST), f)
    const[:, IDENT:IDENT + 128] = np.eye(128)
    const[:, CENTER:CENTER + 128] = np.eye(128) - 1.0 / D
    const[:, MEAN:MEAN + 128] = 1.0 / D
    const[np.arange(128), HMASK + np.arange(128) // 8] = 8 ** -0.5
    const[:, ONES] = 1.0
    const[:, REV:REV + E] = E - np.arange(E)

    import ml_dtypes
    sel = np.zeros((128, E, 128), ml_dtypes.bfloat16)
    for e in range(E):
        sel[[e, E + e, 2 * E + e], e] = 1
    identb = np.eye(128).astype(ml_dtypes.bfloat16)

    vecs = [i[f"L{l}_xattn_{n}"] for l in (0, 1) for n in ("bq", "bk", "bv", "bo")]
    vecs += [i["L2_xattn_" + n] for n in ("ln_gamma", "ln_beta", "b_out")]
    vecs += [i["L3_xattn_" + n] for n in ("ln_x_g", "ln_x_b", "ln_l_g", "ln_l_b", "ln_o_g", "ln_o_b")]
    vec = np.concatenate([np.stack(vecs, 1), i["L2_ffn_gate_b"].reshape(-1, 128).T, i["L2_ffn_up_b"].reshape(-1, 128).T,
                          i["L3_ffn_b1"].reshape(-1, 128).T], 1)
    pad1 = np.zeros(1, f)
    row = rows(np.concatenate([i["g_xattn"], i["g_ffn"], i["L2_xattn_gate"], i["L0_ffn_routing_bias"], pad1, i["L3_ffn_b_router"]]))
    rw = np.stack([np.concatenate([i["L0_ffn_router_w"], np.zeros((D, 1), f)], 1), i["L1_ffn_router_w"], i["L2_ffn_router_w"].T,
                   i["L3_ffn_W_router"]], 1)
    zero = np.zeros((E, D), f)
    bd = np.stack([zero, zero, i["L2_ffn_down_b"], i["L3_ffn_b2"]], 1)

    def chunks(w):
        return w.reshape(-1, 128, D).transpose(1, 0, 2).reshape(128, -1)

    p = "L0_xattn_"
    wa0 = np.concatenate([i[p + "Wq"], i[p + "Wk"], i[p + "Wv"], i[p + "Wo"]], 1)
    p = "L1_xattn_"
    wa1 = np.concatenate([i[p + "Wq"].T, i[p + "Wk"].T, i[p + "Wv"].T, i[p + "Wo"].T], 1)
    p = "L2_xattn_"
    wa2 = np.concatenate([i[p + "w_q"], i[p + "w_kv"], chunks(i[p + "w_out"])], 1)
    p = "L3_xattn_"
    wa3 = np.concatenate([i[p + "Wq"], i[p + "Wkv"], chunks(i[p + "Wo"])], 1)

    def expert_w(ups, down):
        H = down.shape[1]
        HP = -(-H // 128) * 128
        ups = [np.pad(u, ((0, 0), (0, 0), (0, HP - H))) for u in ups]
        down = np.pad(down, ((0, 0), (0, HP - H), (0, 0))).reshape(E, -1, 128, D).transpose(0, 2, 1, 3).reshape(E, 128, -1)
        return np.concatenate(ups + [down], 2)

    def with_shared(r, s):
        return np.concatenate([r, s[None]], 0)

    w0 = expert_w([with_shared(i["L0_ffn_routed_gate"], i["L0_ffn_shared_gate"]), with_shared(i["L0_ffn_routed_up"], i["L0_ffn_shared_up"])],
                  with_shared(i["L0_ffn_routed_down"], i["L0_ffn_shared_down"]))
    w1 = expert_w([with_shared(i["L1_ffn_gate_w"], i["L1_ffn_shared_gate_w"]), with_shared(i["L1_ffn_up_w"], i["L1_ffn_shared_up_w"])],
                  with_shared(i["L1_ffn_down_w"], i["L1_ffn_shared_down_w"]))
    w2 = expert_w([i["L2_ffn_gate_w"], i["L2_ffn_up_w"]], i["L2_ffn_down_w"])
    w3 = expert_w([i["L3_ffn_W1"]], i["L3_ffn_W2"])

    arrays = {
        "x": i["x"].transpose(2, 0, 1).reshape(D, T), "cx": i["ctx_1024"].transpose(2, 0, 1), "sel": sel, "identb": identb, "const": const, "vec": vec, "row": row,
        "rw": rw, "bd": bd, "fside": i["fside_SxS2_0"],
        "pad": rows(i["mask_BxS2_bf0"]).reshape(128, B, SK),
        "keep": rows(i["mask_BxS2_bk1"]).reshape(128, B, SK),
        "wa0": wa0, "wa1": wa1, "wa2": wa2, "wa3": wa3, "w0": w0, "w1": w1, "w2": w2, "w3": w3,
    }
    nc = bacc.Bacc("TRN2", target_bir_lowering=False, num_devices=1)
    sent, aps = {}, {}
    for name, v in arrays.items():
        v = np.ascontiguousarray(v)
        sent["in_" + name] = v
        aps[name] = nc.dram_tensor("in_" + name, v.shape, mybir.dt.from_np(v.dtype), kind="ExternalInput").ap()
    out = nc.dram_tensor("out_0", (D, T), F32, kind="ExternalOutput").ap()
    build(nc, aps, out)
    r = run(nc, [sent], core_ids=[0])
    return r.results[0]["out_0"].reshape(D, B, S).transpose(1, 2, 0)
```

```python
from contextlib import ExitStack

import concourse.bass as bass
from concourse import mybir

F32 = mybir.dt.float32
BF16 = mybir.dt.bfloat16
F32R = mybir.dt.float32r
U8 = mybir.dt.uint8
ACT = mybir.ActivationFunctionType
ALU = mybir.AluOpType
AX = mybir.AxisListType

B, S, D, SK = 8, 128, 128, 77
T = B * S
HALF = T // 2
E = 8
NEG = -1.0e30

HEADS = (16, 16, 16, 8)
HD = (8, 8, 64, 64)
KEYS = (SK, SK, SK, SK + S)
QSCALE = (1.0, 1.0, 64 ** -0.5, 1.0 / 64)
QC = tuple(max(1, h * d // D) for h, d in zip(HEADS, HD))
NC = (3, 4, 2, 4)
GATED = (True, True, True, False)

LN_EXP = "natural_log_exp_and_others"

(BQ0, BK0, BV0, BO0, BQ1, BK1, BV1, BO1, G2, B2, BO2, XG3, XB3, LG3, LB3, OG3, OB3) = range(17)
GB2 = 17
UB2 = GB2 + E * NC[2]
B13 = UB2 + E * NC[2]
NVEC = B13 + E * NC[3]
GX, GF, GATE2, RB0, RB3 = 0, 4, 8, 9, 17
NROW = 25
IDENT, CENTER, MEAN, HMASK, REV = 0, 128, 256, 384, 400
ONES = 408
NCONST = 409
SHORT, LONG = 3, 20
RESIDUAL = 3.0e-5
VH = 12
GUESS = (-0.034, 1.02)


def build(nc, a, out):
    ctx = ExitStack()
    with ctx:
        def sb(name, shape, dt=F32):
            return ctx.enter_context(nc.sbuf_tensor(name, shape, dt))

        def sem(name):
            return ctx.enter_context(nc.semaphore(name))

        x = sb("x", [D, T])
        xn = sb("xn", [D, T])
        y = sb("y", [D, T])
        cx = sb("cx", [D, B, SK])
        cxn = sb("cxn", [D, B, SK])
        const = sb("const", [128, NCONST])
        vec = sb("vec", [128, NVEC])
        row = sb("row", [128, NROW])
        tg = sb("tg", [128, NROW])
        bad = sb("bad", [128, 1])
        bad_i = sb("bad_i", [1, 1], mybir.dt.int32)
        eps = sb("eps", [128, 1])
        rw = sb("rw", [D, 4, E])
        bd = sb("bd", [E, 4, D])
        fside = sb("fside", [S, SK])
        pad = sb("pad", [128, B, SK], U8)
        keep = sb("keep", [128, B, SK], U8)
        bias1 = sb("bias1", [128, B, KEYS[1]])
        bias3 = sb("bias3", [128, B, KEYS[3]])
        wa = [sb(f"wa{i}", [D, n]) for i, n in enumerate((512, 512, 4096, 2048))]
        sq = sb("sq", [128, 2, HALF])
        lnv = sb("lnv", [128, 2, HALF])
        rstd = sb("rstd", [128, 2, HALF])
        st = sb("st", [D, SK + S])
        q_sb = sb("q_sb", [128, 1024])
        k_sb = sb("k_sb", [128, SK])
        pr = sb("pr", [128, 1640])
        ind = sb("ind", [128, 16 * SK], BF16)
        col = sb("col", [128, 6, 16])
        tot = sb("tot", [128, 16])
        num = sb("num", [128, 16])
        ksum = sb("ksum", [128, 1])
        stat = sb("stat", [128, 5, 16])
        o_sb = sb("o_sb", [128, 128])
        ot_sb = sb("ot_sb", [128, 1024])
        W = [sb(f"W{i}", [128, 1536]) for i in range(2)]
        cT = sb("cT", [E, T])
        c3 = sb("c3", [128, B, 32], BF16)
        cT3 = sb("cT3", [128, T], BF16)
        sel = sb("sel", [128, E, 128], BF16)
        zeros = sb("zeros", [128, 128], BF16)
        identb = sb("identb", [128, 128], BF16)
        with ExitStack() as attn:
            def sb_attn(name, shape):
                return attn.enter_context(nc.sbuf_tensor(name, shape, F32))

            v_sb = sb_attn("v_sb", [128, 2, 1024])
            km = sb_attn("km", [128, 1640])
            sc = sb_attn("sc", [128, 1640])
            pt = sb_attn("pt", [128, 2048])
        Wh, Wl = ([sb(f"{k}{p}", [128, 1536], F32R) for p in range(2)] for k in ("Wh", "Wl"))
        hh, hl = (sb(k, [128, 4, HALF], F32R) for k in ("hh", "hl"))
        xh, xl = (sb(k, [D, T], F32R) for k in ("xh", "xl"))
        gs = sb("gs", [128, 2, HALF])
        tu = sb("tu", [128, 2, HALF])
        hb = sb("hb", [128, 4, HALF])
        rt = sb("rt", [128, 12, B, E])
        rc = sb("rc", [128, 6, B])

        ps = ctx.enter_context(nc.psum_tensor("ps", [128, 8, 512], F32))

        ident = const[:, IDENT:IDENT + 128]
        center = const[:, CENTER:CENTER + 128]
        mean = const[:, MEAN:MEAN + 128]
        ones = const[:, ONES:ONES + 1]
        hmask = const[:, HMASK:HMASK + 16]
        rev = const[:, REV:REV + E]

        squares = hb[:].rearrange("p u n -> p (u n)")[:, 0:16 * SK]

        def v1(i):
            return vec[:, i:i + 1]

        ld_vec, ld_x, ld_c, ld_cx, ld_t = sem("ld_vec"), sem("ld_x"), sem("ld_c"), sem("ld_cx"), sem("ld_t")
        ld_wa = [sem(f"ld_wa{i}") for i in range(4)]
        ld_w = [sem(f"ld_w{p}") for p in range(2)]
        init_v, tanh_s = sem("init_v"), sem("tanh_s")
        xh_s, xl_s = sem("xh_s"), sem("xl_s")
        wh_s = sem("wh_s")
        wl_s, wd_s = sem("wl_s"), sem("wd_s")
        hh_s, hl_s = sem("hh_s"), sem("hl_s")
        x_rdy = sem("x_rdy")
        c_ps, sq_s, var_ps, ln_s, rs_s, xn_s, aff_s = (sem(n) for n in ("c_ps", "sq_s", "var_ps", "ln_s", "rs_s", "xn_s", "aff_s"))
        (stg, q_ps, q_s, k_ps, k_s, km_s, v_ps, v_s, s_ps, s_free, t_s, e_s, p_s, pt_ps, pt_s, pv_ps, o_s, ot_ps, ot_s, out_ps,
         y_s, kz) = (sem(n) for n in (
             "stg", "q_ps", "q_s", "k_ps", "k_s", "km_s", "v_ps", "v_s", "s_ps", "s_free", "t_s", "e_s", "p_s", "pt_ps", "pt_s",
             "pv_ps", "o_s", "ot_ps", "ot_s", "out_ps", "y_s", "kz"))
        tau_s, relu_s, above_s, ind_s = sem("tau_s"), sem("relu_s"), sem("above_s"), sem("ind_s")
        stat_s, guess_s, gch = sem("stat_s"), sem("guess_s"), sem("gch")
        dev_s, dev2_s, bad_s, bad_ps = sem("dev_s"), sem("dev2_s"), sem("bad_s"), sem("bad_ps")
        dch = sem("dch")
        lg_ps, rx_in, rx_s, c3_s, ct_ps, ct_s, cb_ps, acc_ps, gu_ps, g_s, tu_s, h_s, dn_ps = (sem(n) for n in (
            "lg_ps", "rx_in", "rx_s", "c3_s", "ct_ps", "ct_s", "cb_ps", "acc_ps", "gu_ps", "g_s", "tu_s", "h_s", "dn_ps"))
        out_s = sem("out_s")
        passed = sem("passed")

        UNITS = [E * 2 * n for n in NC]
        U0 = [sum(UNITS[:i]) for i in range(4)]
        CT0 = (0, 1, 2, 4, 6)
        LN = []
        cxf, cxnf = cx[:].rearrange("p b s -> p (b s)"), cxn[:].rearrange("p b s -> p (b s)")
        CXH = B * SK // 2
        LN_C = 2

        def context():
            for i in range(2):
                LN.append((cxf[:, i * CXH:(i + 1) * CXH], cxnf[:, i * CXH:(i + 1) * CXH], CXH, XG3, XB3))

        def ln_pair(src, dst, g=None, b=None):
            at = len(LN)
            for i in range(2):
                LN.append((src[:, i * HALF:(i + 1) * HALF], dst[:, i * HALF:(i + 1) * HALF], HALF, g, b))
            return at

        LN_A, LN_A2, LN_F, LN_Y = [], {}, [], None
        for l in range(4):
            LN_A.append(ln_pair(x, xn))
            if l == 0:
                context()
            if l == 2:
                LN_A2[l] = ln_pair(xn, xn, G2, B2)
            if l == 3:
                LN_A2[l] = ln_pair(xn, xn, LG3, LB3)
                LN_Y = ln_pair(y, y, OG3, OB3)
            LN_F.append(ln_pair(x, xn))
        AFF = [sum(1 for u in LN[:i] if u[3] is not None) for i in range(len(LN) + 1)]

        def ln_banks(u):
            return (4 + u % 2, 6 + u % 2) if u in (LN_C, LN_C + 1) else (u % 2, 2 + u % 2)

        def ln_done(eng, u):
            if LN[u][3] is None:
                eng.wait_ge(xn_s, u + 1)
            else:
                eng.wait_ge(aff_s, AFF[u + 1])

        TABLES = ((row, "row"), (rw, "rw"), (bd, "bd"), (fside, "fside"), (pad, "pad"), (keep, "keep"), (sel, "sel"), (identb, "identb"))

        def settled(eng):
            eng.sem_inc(passed, 1)

        block = ctx.enter_context(nc.Block())

        @block.sync
        def _(sp):
            sp.dma_start(const[:], a["const"]).then_inc(ld_c, 16)
            sp.dma_start(x[:], a["x"]).then_inc(ld_x, 16)
            sp.dma_start(cx[:], a["cx"]).then_inc(ld_cx, 16)
            sp.dma_start(vec[:], a["vec"]).then_inc(ld_vec, 16)
            sp.dma_start(wa[0][:], a["wa0"]).then_inc(ld_wa[0], 16)
            for dst, name in TABLES:
                sp.dma_start(dst[:], a[name]).then_inc(ld_t, 16)
            for l in range(1, 4):
                sp.dma_start(wa[l][:], a[f"wa{l}"]).then_inc(ld_wa[l], 16)
            for l in range(4):
                w = a[f"w{l}"]
                n = w.shape[2]
                if l:
                    sp.wait_ge(wd_s, E * l)
                for p in range(2):
                    sp.dma_start(W[p][:, 0:n], w[p]).then_inc(ld_w[p], 16)
                with sp.Fori(0, E // 2 - 1) as j:
                    for p in range(2):
                        sp.wait_ge(wd_s, 2 * j + (E * l + p + 1))
                        sp.dma_start(W[p][:, 0:n], w[bass.ds(2 * j + (2 + p), 1)].rearrange("a p n -> (a p) n")).then_inc(ld_w[p], 16)
            for h in range(2):
                sp.wait_ge(x_rdy, 15 + h)
                sp.dma_start(out[:, h * HALF:(h + 1) * HALF], x[:, h * HALF:(h + 1) * HALF]).then_inc(out_s, 16)
            sp.wait_ge(out_s, 32)

        @block.tensor
        def _(pe):
            def layernorm(u0, ready=lambda i: None):
                for u in (u0, u0 + 1):
                    src, _, n, _, _ = LN[u]
                    ready(u - u0)
                    pe.matmul(ps[:, ln_banks(u)[0], 0:n], center, src, start=True, stop=True).then_inc(c_ps, 1)
                for u in (u0, u0 + 1):
                    n = LN[u][2]
                    pe.wait_ge(sq_s, u + 1)
                    pe.matmul(ps[:, ln_banks(u)[1], 0:n], mean, sq[:, u % 2, 0:n], start=True, stop=True).then_inc(var_ps, 1)

            def keys(l, n):
                C, nk, w = QC[l], KEYS[l], wa[l]
                pe.wait_ge(stg, n + 1)
                if not isinstance(n, int) or n > 0:
                    pe.wait_ge(v_s, n)
                K0 = C * 128
                per = 4 if l == 2 else 2
                for c in range(C):
                    m = pe.matmul(ps[:, 6 + c // per, c % per * nk:c % per * nk + nk], w[:, K0 + c * 128:K0 + c * 128 + 128],
                                  st[:, 0:nk], start=True, stop=True)
                m.then_inc(k_ps, 1)

            def queries(l, n):
                C, w = QC[l], wa[l]
                pe.wait_ge(k_s if l < 2 else km_s, n + 1)
                for c in range(C):
                    m = pe.matmul(ps[:, 6 + c // 4, c % 4 * 128:c % 4 * 128 + 128], w[:, c * 128:c * 128 + 128],
                                  st[:, SK:SK + S], start=True, stop=True)
                m.then_inc(q_ps, 1)

            def values(l, n):
                w = wa[l]
                V0 = 2 * QC[l] * 128
                pe.wait_ge(q_s, n + 1)
                if l < 2:
                    m = pe.matmul(ps[0:SK, 6, 0:128], st[:, 0:SK], w[:, V0:V0 + 128], start=True, stop=True)
                elif l == 2:
                    for c in range(2):
                        m = pe.matmul(ps[0:SK, 6 + c, :], st[:, 0:SK], w[:, V0 + c * 512:V0 + c * 512 + 512], start=True, stop=True)
                else:
                    pe.matmul(ps[0:SK, 6, :], st[:, 0:SK], w[:, V0:V0 + 512], start=True, stop=True)
                    m = pe.matmul(ps[:, 7, :], st[:, SK:SK + S], w[:, V0:V0 + 512], start=True, stop=True)
                m.then_inc(v_ps, 1)

            def scores(l, n):
                pe.wait_ge(km_s, n + 1)
                if not isinstance(n, int) or n > 0:
                    pe.wait_ge(s_free, n)
                for t in range(4):
                    if l < 2:
                        m = pe.matmul(ps[:, t, 0:308], q_sb[:, 0:128], km[:, t * 308:t * 308 + 308], start=True, stop=True)
                    elif l == 2:
                        for c in (2 * t, 2 * t + 1):
                            m = pe.matmul(ps[:, t, c % 2 * 154:c % 2 * 154 + 154], q_sb[:, c * 128:c * 128 + 128],
                                          km[:, c * 154:c * 154 + 154], start=True, stop=True)
                    else:
                        m = pe.matmul(ps[:, t, 0:410], q_sb[:, t * 128:t * 128 + 128], km[:, t * 410:t * 410 + 410], start=True, stop=True)
                if l == 0:
                    m = pe.matmul(ps[:, 3, 308:324], q_sb[:, 0:128], km[:, 1232:1248], start=True, stop=True)
                m.then_inc(s_ps, 1)

            def turn(l, n, last):
                pe.wait_ge(y_s, n + 1)
                if l == 0:
                    pe.wait_ge(bad_s, n + 1)
                    pe.matmul(ps[0:1, 4, 0:1], bad[:], ones[:, 0:1], start=True, stop=True).then_inc(bad_ps, 1)
                pe.wait_ge(p_s, n + 1)
                for g in range(4):
                    if g == 2:
                        pe.wait_ge(v_s, n + (1 if last else 2))
                    for i in range(4):
                        if l < 3:
                            h = 4 * g + i
                            m = pe.transpose(ps[0:SK, 4 + g, i * 128:i * 128 + 128], pr[:, h * SK:h * SK + SK], ident)
                        elif i < 2:
                            h = 2 * g + i
                            m = pe.transpose(ps[0:SK, 4 + g, i * 128:i * 128 + 128], pr[:, h * 205:h * 205 + SK], ident)
                        else:
                            h = 2 * g + i - 2
                            m = pe.transpose(ps[:, 4 + g, i * 128:i * 128 + 128], pr[:, h * 205 + SK:h * 205 + 205], ident)
                    m.then_inc(pt_ps, 1)

            def weigh(l, n, b):
                for h in range(HEADS[l]):
                    d = HD[l]
                    group = HEADS[l] // 4
                    if h % group == 0:
                        pe.wait_ge(pt_s, n * 4 + (h // group + 1))
                    if l < 2:
                        m = pe.matmul(ps[:, 4, h * d:h * d + d], pt[0:SK, h * 128:h * 128 + 128], v_sb[0:SK, b, h * d:h * d + d],
                                      start=True, stop=True)
                        continue
                    o = ps[h % 2 * d:h % 2 * d + d, 4 + h // 8, h % 8 // 2 * 128:h % 8 // 2 * 128 + 128]
                    if l == 2:
                        m = pe.matmul(o, v_sb[0:SK, b, h * d:h * d + d], pt[0:SK, h * 128:h * 128 + 128], start=True, stop=True)
                    else:
                        c0 = h // 2 * 512 + h % 2 * 128
                        pe.matmul(o, v_sb[0:SK, b, h * d:h * d + d], pt[0:SK, c0:c0 + 128], start=True, stop=False)
                        m = pe.matmul(o, v_sb[:, b, 512 + h * d:512 + h * d + d], pt[:, c0 + 256:c0 + 384], start=False, stop=True)
                m.then_inc(pv_ps, 1)

            def turn_out(l, n):
                if l >= 2:
                    return
                pe.wait_ge(o_s, n + 1)
                for c in range(QC[l]):
                    m = pe.transpose(ps[:, 4 + c // 4, c % 4 * 128:c % 4 * 128 + 128], o_sb[:, c * 128:c * 128 + 128], ident)
                m.then_inc(ot_ps, 1)

            def project(l, n):
                C, w = QC[l], wa[l]
                pe.wait_ge(ot_s, n + 1)
                O0 = {0: 384, 1: 384, 2: 3072, 3: 1536}[l]
                for c in range(C):
                    m = pe.matmul(ps[:, 4, 0:128], w[:, O0 + c * 128:O0 + c * 128 + 128], ot_sb[:, c * 128:c * 128 + 128],
                                  start=(c == 0), stop=(c == C - 1))
                m.then_inc(out_ps, 1)

            def attention(l):
                pe.wait_ge(ld_wa[l], 16)
                n0 = B * l
                for n in (n0, n0 + 1):
                    keys(l, n)
                    queries(l, n)
                    values(l, n)
                    if n == n0:
                        ln_done(pe, LN_A2.get(l, LN_A[l]) + 1)
                    scores(l, n)
                if l == 0:
                    pe.wait_ge(v_s, 2)
                    layernorm(LN_C)
                    ln_done(pe, LN_C + 1)
                with pe.Fori(0, B // 2 - 1) as j:
                    for i in range(2):
                        n, n2 = 2 * j + (n0 + i), 2 * j + (n0 + i + 2)
                        turn(l, n, False)
                        if l < 2:
                            weigh(l, n, i)
                        else:
                            pe.wait_ge(pt_s, n * 4 + 4)
                        keys(l, n2)
                        if l >= 2:
                            weigh(l, n, i)
                        queries(l, n2)
                        turn_out(l, n)
                        if l >= 2:
                            project(l, n)
                        values(l, n2)
                        if l < 2:
                            project(l, n)
                        scores(l, n2)
                for b in (B - 2, B - 1):
                    turn(l, n0 + b, b == B - 1)
                    weigh(l, n0 + b, b % 2)
                    turn_out(l, n0 + b)
                    project(l, n0 + b)

            def experts(l):
                n, H = NC[l], NC[l] * 128
                up, down = H, (2 * H if GATED[l] else H)
                ln_done(pe, LN_F[l])
                NU = 4 * n

                def place(i):
                    return i // (2 * n), i // n % 2, i % n

                def spread(j, i):
                    p, h, _ = place(i)
                    if not isinstance(j, int) or (j, i) > (0, 0):
                        pe.wait_ge(h_s, j * NU + (U0[l] + i - n + 2))
                    e = 2 * j + p
                    w = sel[:, e, :] if isinstance(e, int) else sel[:, bass.ds(e, 1), :].rearrange("p a n -> p (a n)")
                    return pe.matmul(ps[:, 6 + h, :], w, cT3[:, h * HALF:h * HALF + HALF], start=True, stop=True)

                def gate_up(u, i):
                    p, h, c = place(i)
                    if GATED[l]:
                        pe.wait_ge(tu_s, u + 1)
                    else:
                        pe.wait_ge(g_s, u - 1)
                    hs = slice(h * HALF, h * HALF + HALF)
                    for k in range(2 if GATED[l] else 1):
                        ws = slice(k * up + c * 128, k * up + c * 128 + 128)
                        o = ps[:, 2 * k + i % 2, :]
                        pe.matmul(o, Wh[p][:, ws], xh[:, hs], start=True, stop=False)
                        pe.matmul(o, Wh[p][:, ws], xl[:, hs], start=False, stop=False)
                        m = pe.matmul(o, Wl[p][:, ws], xh[:, hs], start=False, stop=True)
                    m.then_inc(gu_ps, 1)

                def down_(u, i):
                    p, h, c = place(i)
                    ws = slice(down + c * 128, down + c * 128 + 128)
                    o = ps[:, 4 + h, :]
                    pe.wait_ge(hl_s, u + 5)
                    pe.matmul(o, Wh[p][:, ws], hh[:, i % 4, :], start=False, stop=False, skip_group_check=True)
                    pe.matmul(o, Wh[p][:, ws], hl[:, i % 4, :], start=False, stop=False, skip_group_check=True)
                    pe.matmul(o, Wl[p][:, ws], hh[:, i % 4, :], start=False, stop=False, skip_group_check=True).then_inc(dn_ps, 1)

                def pair(j, last):
                    for i in range(NU):
                        k = i + 3
                        if k < NU:
                            if k == 2 * n:
                                pe.wait_ge(wl_s, 2 * j + (E * l + 2))
                            if k % n == 0:
                                spread(j, k)
                            gate_up(j * NU + (U0[l] + k), k)
                        elif not last:
                            if k == NU:
                                pe.wait_ge(wl_s, 2 * j + (E * l + 3))
                            if k % n == 0:
                                spread(j + 1, k - NU)
                            gate_up(j * NU + (U0[l] + k), k - NU)
                        if i % (2 * n) == 0:
                            pe.wait_ge(wd_s, 2 * j + (E * l + 1 + i // (2 * n)))
                        down_(j * NU + (U0[l] + i), i)
                        if last and i % n == n - 1 and i >= 2 * n:
                            close(place(i)[1])

                def close(h):
                    w, c = (bd[:, l, :], cT[:, h * HALF:h * HALF + HALF]) if l >= 2 else (zeros[:], cT3[:, 0:HALF])
                    pe.matmul(ps[:, 4 + h, :], w, c, start=False, stop=True, skip_group_check=True).then_inc(acc_ps, 1)

                if l == 0:
                    pe.wait_ge(ld_t, 16 * len(TABLES))
                for t in range(B):
                    if t == B // 2:
                        ln_done(pe, LN_F[l] + 1)
                    m = pe.matmul(ps[:, 7, t * E:t * E + E], xn[:, t * S:t * S + S], rw[:, l, :], start=True, stop=True)
                m.then_inc(lg_ps, 1)
                pe.wait_ge(xl_s, 2 * l + 2)
                pe.wait_ge(wl_s, E * l + 1)
                gate_up(U0[l], 0)
                gate_up(U0[l] + 1, 1)
                pe.wait_ge(c3_s, l + 1)
                c3b = ps[:, 5, :].bitcast(BF16)
                for t in range(B):
                    m = pe.transpose(c3b[0:32, t * 128:t * 128 + 128], c3[:, t, :], identb[:])
                m.then_inc(ct_ps, 1)
                if l >= 2:
                    for t in range(B):
                        m = pe.transpose(ps[0:E, 6 + t // 4, t % 4 * 128:t % 4 * 128 + 128], rt[:, 9, t, :], ident)
                    m.then_inc(ct_ps, 1)
                pe.wait_ge(ct_s, CT0[l] + (2 if l >= 2 else 1))
                spread(0, 0).then_inc(cb_ps, 1)
                for h in range(2):
                    pe.matmul(ps[:, 4 + h, :], zeros[:], cT3[:, 0:HALF], start=True, stop=False, skip_group_check=True)
                if n == 2:
                    spread(0, 2)
                gate_up(U0[l] + 2, 2)
                with pe.Fori(0, E // 2 - 1) as j:
                    pair(j, False)
                pair(E // 2 - 1, True)

            pe.wait_ge(ld_c, 16)
            pe.wait_ge(ld_x, 16)
            for l in range(4):
                layernorm(LN_A[l], lambda i: pe.wait_ge(x_rdy, 4 * l - 1 + i) if l else None)
                if l in LN_A2:
                    layernorm(LN_A2[l], lambda i: ln_done(pe, LN_A[l] + i))
                attention(l)
                if l == 3:
                    layernorm(LN_Y, lambda i: pe.wait_ge(y_s, B * 3 + (i + 1) * B // 2 + 1))
                layernorm(LN_F[l], lambda i: pe.wait_ge(x_rdy, 4 * l + 1 + i))
                experts(l)

        @block.scalar
        def _(act):
            def layernorm(u0):
                for u in (u0, u0 + 1):
                    n = LN[u][2]
                    act.wait_ge(c_ps, u + 1)
                    act.activation(sq[:, u % 2, 0:n], ps[:, ln_banks(u)[0], 0:n], ACT.Square).then_inc(sq_s, 1)
                for u in (u0, u0 + 1):
                    n = LN[u][2]
                    act.wait_ge(var_ps, u + 1)
                    act.activation(lnv[:, u % 2, 0:n], ps[:, ln_banks(u)[1], 0:n], ACT.Ln, bias=eps[:, 0:1]).then_inc(ln_s, 1)
                    act.wait_ge(ln_s, u + 1)
                    act.activation(rstd[:, u % 2, 0:n], lnv[:, u % 2, 0:n], ACT.Exp, scale=-0.5).then_inc(rs_s, 1)

            def keys(l, n):
                C, nk = QC[l], KEYS[l]
                act.wait_ge(k_ps, n + 1)
                if not isinstance(n, int) or n > 0:
                    act.wait_ge(s_ps, n)
                if l < 2:
                    if not isinstance(n, int) or n > 0:
                        act.wait_ge(km_s, n)
                    act.activation(k_sb[:, :], ps[:, 6, 0:SK], ACT.Identity, bias=v1((BK0, BK1)[l]),
                                   accum_out=ksum[:, 0:1]).then_inc(k_s, 1)
                else:
                    per = 4 if l == 2 else 2
                    act.wait_ge(kz, l - 1)
                    kv = km[:, 0:C * 2 * nk].rearrange("p (u c a s) -> p u c a s", u=2, a=2, s=nk)
                    pv = ps[:, 6:8, 0:per * nk].rearrange("p u (c s) -> p u c s", s=nk)
                    act.activation(kv[0:64, :, :, 0, :], pv[0:64], ACT.Copy)
                    act.activation(kv[64:128, :, :, 1, :], pv[64:128], ACT.Copy).then_inc(km_s, 1)

            def queries(l, n):
                C = QC[l]
                act.wait_ge(q_ps, n + 1)
                if l < 2:
                    act.activation(q_sb[:, 0:128], ps[:, 6, 0:128], ACT.Identity, bias=v1((BQ0, BQ1)[l])).then_inc(q_s, 1)
                else:
                    act.activation(q_sb[:, 0:C * 128], ps[:, 6:6 + C // 4, :], ACT.Copy, scale=QSCALE[l]).then_inc(q_s, 1)

            def values(l, n, b):
                act.wait_ge(v_ps, n + 1)
                if l < 2:
                    act.activation(v_sb[0:SK, b, 0:128], ps[0:SK, 6, 0:128], ACT.Copy).then_inc(v_s, 1)
                elif l == 2:
                    act.activation(v_sb[0:SK, b, :], ps[0:SK, 6:8, :], ACT.Copy).then_inc(v_s, 1)
                else:
                    act.activation(v_sb[0:SK, b, 0:512], ps[0:SK, 6, :], ACT.Copy)
                    act.activation(v_sb[:, b, 512:1024], ps[:, 7, :], ACT.Copy).then_inc(v_s, 1)

            def exps(l, n):
                W_ = HEADS[l] * KEYS[l]
                act.wait_ge(t_s, n + (1 - B))
                act.activation(pr[:, 0:W_], sc[:, 0:W_], ACT.Exp).then_inc(e_s, 1)

            def deviation(n):
                act.wait_ge(s_ps, n + 1)
                act.activation(stat[:, 1, :], ps[:, 3, 308:324], ACT.Copy, scale=1.0 / SK)
                for h in range(16):
                    act.activation(squares[:, h * SK:h * SK + SK], ps[:, h // 4, h % 4 * SK:h % 4 * SK + SK], ACT.Square,
                                   accum_out=stat[:, 0, h:h + 1]).then_inc(stat_s, 1)
                act.wait_ge(dev_s, n + 1)
                act.activation(stat[:, 3, :], stat[:, 0, :], ACT.Sqrt).then_inc(dev2_s, 1)

            def newton(n, k):
                act.wait_ge(tau_s, n * (SHORT + 1) + (k + 1))
                for h in range(VH, 16):
                    hs = slice(h * SK, h * SK + SK)
                    m = act.activation(pr[:, hs], sc[:, hs], ACT.Relu, bias=col[:, 2, h:h + 1], accum_out=tot[:, h:h + 1])
                m.then_inc(relu_s, 1)
                if k == SHORT:
                    return
                act.wait_ge(relu_s, n * (SHORT + 1) + (k + 1))
                for h in range(VH, 16):
                    hs = slice(h * SK, h * SK + SK)
                    act.activation(ind[:, hs], pr[:, hs], ACT.Sign, accum_out=num[:, h:h + 1])
                act.wait_ge(above_s, n * SHORT + (k + 1))
                act.activation(ind[:, 0:VH * SK], pr[:, 0:VH * SK], ACT.Sign).then_inc(ind_s, 1)

            def turned(l, n):
                for g in range(4):
                    act.wait_ge(pt_ps, n * 4 + (g + 1))
                    if l < 3:
                        act.activation(pt[0:SK, g * 512:g * 512 + 512], ps[0:SK, 4 + g, :], ACT.Copy).then_inc(pt_s, 1)
                    else:
                        act.activation(pt[0:SK, g * 512:g * 512 + 256], ps[0:SK, 4 + g, 0:256], ACT.Copy)
                        act.activation(pt[:, g * 512 + 256:g * 512 + 512], ps[:, 4 + g, 256:512], ACT.Copy).then_inc(pt_s, 1)

            def outs(l, n):
                C = QC[l]
                if l >= 2:
                    return
                act.wait_ge(pv_ps, n + 1)
                act.activation(o_sb[:, 0:128], ps[:, 4, 0:128], ACT.Copy).then_inc(o_s, 1)

            def turned_outs(l, n):
                if l >= 2:
                    return
                act.wait_ge(ot_ps, n + 1)
                act.activation(ot_sb[:, 0:128], ps[:, 4, 0:128], ACT.Identity, bias=v1((BV0, BV1)[l])).then_inc(ot_s, 1)

            def projected(l, n, b):
                act.wait_ge(out_ps, n + 1)
                settled(act)
                yb = y[:, b * S:b * S + S] if isinstance(b, int) else y[:, bass.ds(b * S, S)]
                if l < 3:
                    act.activation(yb, ps[:, 4, 0:128], ACT.Identity, bias=v1((BO0, BO1, BO2)[l])).then_inc(y_s, 1)
                else:
                    act.activation(yb, ps[:, 4, 0:128], ACT.Copy).then_inc(y_s, 1)

            def attention_sparse():
                for b in (0, 1):
                    keys(0, b)
                    queries(0, b)
                    values(0, b, b)
                    if b == 0:
                        deviation(0)
                newton(0, 0)
                act.wait_ge(ld_t, 16 * len(TABLES))
                act.activation(tg[:], row[:], ACT.Tanh).then_inc(tanh_s, 1)
                act.preload_act_table_set(LN_EXP)
                layernorm(LN_C)
                act.preload_act_table(ACT.Sqrt)
                for k in range(1, SHORT + 1):
                    newton(0, k)
                deviation(1)
                with act.Fori(0, B // 2 - 1) as j:
                    for i in range(2):
                        n, n1, n2 = (2 * j + (i + k) for k in range(3))
                        turned(0, n)
                        newton(n1, 0)
                        keys(0, n2)
                        outs(0, n)
                        newton(n1, 1)
                        queries(0, n2)
                        turned_outs(0, n)
                        newton(n1, 2)
                        values(0, n2, i)
                        newton(n1, 3)
                        projected(0, n, n)
                        deviation(n2)
                turned(0, B - 2)
                newton(B - 1, 0)
                outs(0, B - 2)
                newton(B - 1, 1)
                turned_outs(0, B - 2)
                newton(B - 1, 2)
                projected(0, B - 2, B - 2)
                newton(B - 1, 3)
                turned(0, B - 1)
                outs(0, B - 1)
                turned_outs(0, B - 1)
                projected(0, B - 1, B - 1)

            def attention(l):
                if l == 0:
                    attention_sparse()
                    return
                n0 = B * l
                for b in (0, 1):
                    keys(l, n0 + b)
                    queries(l, n0 + b)
                    values(l, n0 + b, b)
                    if b == 0:
                        exps(l, n0)
                with act.Fori(0, B // 2 - 1) as j:
                    for i in range(2):
                        n, n1, n2 = (2 * j + (n0 + i + k) for k in range(3))
                        turned(l, n)
                        keys(l, n2)
                        exps(l, n1)
                        outs(l, n)
                        queries(l, n2)
                        turned_outs(l, n)
                        if l >= 2:
                            projected(l, n, 2 * j + i)
                        values(l, n2, i)
                        if l < 2:
                            projected(l, n, 2 * j + i)
                for b in (B - 2, B - 1):
                    turned(l, n0 + b)
                    if b == B - 2:
                        exps(l, n0 + B - 1)
                    outs(l, n0 + b)
                    turned_outs(l, n0 + b)
                    projected(l, n0 + b, b)

            def experts(l):
                n = NC[l]
                for h in range(2):
                    hs = slice(h * HALF, h * HALF + HALF)
                    ln_done(act, LN_F[l] + h)
                    act.activation(xh[:, hs], xn[:, hs], ACT.Copy).then_inc(xh_s, 1)
                act.wait_ge(rx_in, l + 1)
                act.activation(rt[:, 1], rt[:, 0], ACT.Exp, scale=-1.0 if l == 0 else 1.0).then_inc(rx_s, 1)
                if l < 3:
                    act.preload_act_table(ACT.Silu)
                NU = 4 * n

                def gate(j, i):
                    if i == NU:
                        j, i = j + 1, 0
                    u = j * NU + (U0[l] + i)
                    p, c = i // (2 * n), i % n
                    act.wait_ge(gu_ps, u + 1)
                    if not GATED[l]:
                        act.wait_ge(h_s, u + 1)
                    if l < 2:
                        act.activation(gs[:, i % 2, :], ps[:, i % 2, :], ACT.Silu).then_inc(g_s, 1)
                        return
                    c0 = {2: GB2, 3: B13}[l] + p * n + c
                    if isinstance(j, int):
                        bias = v1(j * (2 * n) + c0)
                    else:
                        settled(act)
                        bias = vec[:, bass.ds(j * (2 * n) + c0, 1)]
                    act.activation(gs[:, i % 2, :], ps[:, i % 2, :], ACT.Silu if l == 2 else ACT.Relu, bias=bias).then_inc(g_s, 1)

                def high(j, i):
                    u = j * NU + (U0[l] + i)
                    act.wait_ge(dn_ps, u + 1)
                    act.wait_ge(h_s, u + 3)
                    act.activation(hh[:, i % 4, :], hb[:, i % 4, :], ACT.Copy).then_inc(hh_s, 1)

                def pair(j, last):
                    for i in range(NU):
                        if i + 1 < NU or not last:
                            gate(j, i + 1)
                        high(j, i)

                gate(0, 0)
                with act.Fori(0, E // 2 - 1) as j:
                    pair(j, False)
                pair(E // 2 - 1, True)

            act.wait_ge(init_v, 4)
            for l in range(4):
                act.preload_act_table_set(LN_EXP)
                layernorm(LN_A[l])
                if l in LN_A2:
                    layernorm(LN_A2[l])
                if l == 0:
                    act.preload_act_table(ACT.Sqrt)
                    act.wait_ge(ld_vec, 16)
                attention(l)
                if l == 0:
                    act.preload_act_table_set(LN_EXP)
                if l == 3:
                    layernorm(LN_Y)
                layernorm(LN_F[l])
                experts(l)

        @block.gpsimd
        def _(g):
            g.sem_inc(dn_ps, 4)
            g.sem_inc(h_s, 2)
            g.sem_inc(hl_s, 4)
            g.sem_inc(tu_s, 2)
            g.sem_inc(y_s, 1)

            def stage(l, n, b):
                if not isinstance(n, int) or n > 0:
                    g.wait_ge(v_ps, n)
                settled(g)
                src = cxn if l == 3 else cx
                cb = src[:, b, :] if isinstance(b, int) else src[:, bass.ds(b, 1), :].rearrange("p a s -> p (a s)")
                xb = xn[:, b * S:b * S + S] if isinstance(b, int) else xn[:, bass.ds(b * S, S)]
                g.tensor_copy(st[:, 0:SK], cb)
                g.tensor_copy(st[:, SK:SK + S], xb).then_inc(stg, 1)
                if l < 2:
                    g.wait_ge(k_s, n + 1)
                    if not isinstance(n, int) or n > 0:
                        g.wait_ge(s_ps, n)
                    settled(g)
                    if l == 0:
                        g.tensor_scalar(km[:, 1232:1248], hmask, ksum[:, 0:1], None, ALU.mult)
                    g.tensor_tensor(km[:, 0:1232].rearrange("p (h s) -> p h s", s=SK),
                                    k_sb[:, :].unsqueeze(1).to_broadcast([128, 16, SK]),
                                    hmask.unsqueeze(2).to_broadcast([128, 16, SK]), ALU.mult).then_inc(km_s, 1)
                if l == 0:
                    guess(n)

            def guess(n):
                sums, avg, sqr, dev, out_ = (stat[:, i, :] for i in range(5))

                def step(k, ins):
                    ins.then_inc(gch, 1)
                    g.wait_ge(gch, n * 4 + (k + 1))
                    settled(g)

                g.wait_ge(stat_s, n * 16 + 16)
                settled(g)
                step(0, g.tensor_tensor(sqr, avg, avg, ALU.mult))
                step(1, g.tensor_scalar(sums, sums, 1.0 / SK, None, ALU.mult))
                step(2, g.tensor_tensor(sums, sums, sqr, ALU.subtract))
                g.tensor_scalar(sums, sums, 0.0, None, ALU.max).then_inc(dev_s, 1)
                g.wait_ge(dev2_s, n + 1)
                settled(g)
                step(3, g.tensor_scalar(dev, dev, GUESS[1], GUESS[0], ALU.mult, ALU.add))
                g.tensor_tensor(out_, dev, avg, ALU.add).then_inc(guess_s, 1)

            def split_weights(l, p, j):
                n = NC[l]
                up = (2 if GATED[l] else 1) * n * 128
                g.wait_ge(ld_w[p], (j + (4 * l + 1)) * 16)
                for k, (c0, c1, done) in enumerate(((0, up, wl_s), (up, up + n * 128, wd_s))):
                    if not isinstance(j, int):
                        if k == 0:
                            g.wait_ge(gu_ps, j * (4 * n) + (U0[l] + (p - 1) * 2 * n))
                        else:
                            g.wait_ge(dn_ps, j * (4 * n) + (U0[l] + (p - 1) * 2 * n + 4))
                    settled(g)
                    g.tensor_copy(Wh[p][:, c0:c1], W[p][:, c0:c1]).then_inc(wh_s, 1)
                    g.wait_ge(wh_s, 4 * j + (2 * E * l + 2 * p + k + 1))
                    g.tensor_tensor(Wl[p][:, c0:c1], W[p][:, c0:c1], Wh[p][:, c0:c1].bitcast(F32), ALU.subtract).then_inc(done, 1)

            g.wait_ge(ld_cx, 16)
            for l in range(4):
                if l >= 2:
                    g.wait_ge(dn_ps, U0[l] + 4)
                    g.memset(km[:], 0.0).then_inc(kz, 1)
                u = LN_A2.get(l, LN_A[l])
                ln_done(g, u)
                stage(l, B * l, 0)
                with g.Fori(1, B // 2) as b:
                    stage(l, b + B * l, b)
                ln_done(g, u + 1)
                with g.Fori(B // 2, B) as b:
                    stage(l, b + B * l, b)
                g.wait_ge(y_s, B * (l + 1) + 1)
                for p in range(2):
                    split_weights(l, p, 0)
                with g.Fori(1, E // 2) as j:
                    for p in range(2):
                        split_weights(l, p, j)

        @block.vector
        def _(v):
            steps = [0]

            class Steps:

                def __init__(self, turn=0, per=0):
                    self.turn, self.per, self.k = turn, per, 0

                def __call__(self, ins):
                    self.k += 1
                    ins.then_inc(dch, 1)
                    v.wait_ge(dch, self.turn * self.per + (steps[0] + self.k))

                def mark(self):
                    return self.k

                def within(self, at, turn=0, per=0):
                    def step(ins, k=[0]):
                        k[0] += 1
                        ins.then_inc(dch, 1)
                        v.wait_ge(dch, self.turn * self.per + (steps[0] + at + k[0]) + turn * per)
                    return step

                def skip(self, k):
                    self.k += k

                def end(self, turns=1):
                    assert isinstance(self.turn, int) or self.k == self.per, self.k
                    steps[0] += self.k * turns

            def ln_unit(u):
                _, dst, n, g, b = LN[u]
                v.wait_ge(rs_s, u + 1)
                v.tensor_tensor(dst, ps[:, ln_banks(u)[0], 0:n], rstd[:, u % 2, 0:n], ALU.mult).then_inc(xn_s, 1)
                if g is not None:
                    v.wait_ge(xn_s, u + 1)
                    v.tensor_scalar(dst, dst, v1(g), v1(b), ALU.mult, ALU.add).then_inc(aff_s, 1)

            def layernorm(u0):
                ln_unit(u0)
                ln_unit(u0 + 1)

            def heads(ap, l):
                h, nk = HEADS[l], KEYS[l]
                return ap.rearrange("p (u h s) -> p u h s", u=4, s=nk)

            def softmax(l, n, b, step):
                h, nk = HEADS[l], KEYS[l]
                W_ = h * nk
                hs = [128, 4, h // 4, nk]
                S4 = ps[:, 0:4, 0:W_ // 4].rearrange("p u (h s) -> p u h s", s=nk)
                T4 = heads(sc[:, 0:W_], l)
                P3 = pr[:, 0:W_].rearrange("p (h s) -> p h s", s=nk)
                c = [col[:, i, 0:h] for i in range(6)]
                c4 = [x_.rearrange("p (u h) -> p u h", u=4) for x_ in c]
                v.wait_ge(s_ps, n + 1)
                if l in (1, 3):
                    tab = bias1 if l == 1 else bias3
                    bb = tab[:, b, :] if isinstance(b, int) else tab[:, bass.ds(b, 1), :].rearrange("p a s -> p (a s)")
                    step(v.tensor_tensor(T4, S4, bb.unsqueeze(1).unsqueeze(1).to_broadcast(hs), ALU.add))
                    v.sem_inc(s_free, 1)
                    step(v.reduce_max(c4[0], T4, AX.X))
                    v.tensor_tensor(T4, T4, c4[0].unsqueeze(3).to_broadcast(hs), ALU.subtract).then_inc(t_s, 1)
                else:
                    step(v.reduce_max(c4[0], S4, AX.X))
                    step(v.tensor_tensor(T4, S4, c4[0].unsqueeze(3).to_broadcast(hs), ALU.subtract))
                    v.sem_inc(s_free, 1)
                    v.sem_inc(t_s, 1)
                if l >= 2 and not isinstance(b, int):
                    turned_outs(l, n - 1)
                v.wait_ge(e_s, n + (1 - B))
                step(v.tensor_reduce(c[1], P3, AX.X, ALU.add))
                step(v.reciprocal(c[2], c[1]))
                v.tensor_tensor(P3, P3, c[2].unsqueeze(2).to_broadcast([128, h, nk]), ALU.mult).then_inc(p_s, 1)

            def sparsemax(n, step):
                hs = [128, 4, 4, SK]
                S4 = ps[:, 0:4, 0:308].rearrange("p u (h s) -> p u h s", s=SK)
                T4 = heads(sc[:, 0:1232], 0)
                T3 = sc[:, 0:1232].rearrange("p (h s) -> p h s", s=SK)
                P3 = pr[:, 0:1232].rearrange("p (h s) -> p h s", s=SK)
                I3 = ind[:].rearrange("p (h s) -> p h s", s=SK)
                top, avg, ntau, f, cnt = (col[:, i, :] for i in range(5))

                def above(step, heads):
                    step(v.tensor_tensor(P3[:, 0:heads], T3[:, 0:heads], ntau[:, 0:heads].unsqueeze(2).to_broadcast([128, heads, SK]),
                                         ALU.add))
                    step(v.tensor_scalar(pr[:, 0:heads * SK], pr[:, 0:heads * SK], 0.0, None, ALU.max))

                def move(step):
                    step(v.reciprocal(cnt, num[:]))
                    step(v.scalar_tensor_tensor(out=f, in0=tot[:], scalar=-1.0, in1=cnt, op0=ALU.add, op1=ALU.mult))
                    step(v.tensor_tensor(ntau, ntau, f, ALU.subtract))

                def newton(step, k):
                    above(step, VH)
                    v.sem_inc(above_s, 1)
                    step(v.tensor_reduce(tot[:, 0:VH], P3[:, 0:VH], AX.X, ALU.add))
                    v.wait_ge(ind_s, n * SHORT + (k + 1))
                    step(v.tensor_reduce(num[:, 0:VH], I3[:, 0:VH], AX.X, ALU.add))
                    move(step)
                    v.sem_inc(tau_s, 1)

                def newton_alone(step):
                    above(step, 16)
                    step(v.tensor_scalar(ind[:], pr[:, 0:1232], 0.0, None, ALU.is_gt))
                    step(v.tensor_reduce(tot[:], P3, AX.X, ALU.add))
                    step(v.tensor_reduce(num[:], I3, AX.X, ALU.add))
                    move(step)

                v.wait_ge(guess_s, n + 1)
                step(v.reduce_max(top.rearrange("p (u h) -> p u h", u=4), S4, AX.X))
                step(v.tensor_tensor(ntau, top, stat[:, 4, :], ALU.subtract))
                step(v.tensor_scalar(ntau, ntau, 1.0 / SK, 1.0, ALU.max, ALU.min))
                step(v.tensor_tensor(T4, S4, top.rearrange("p (u h) -> p u h", u=4).unsqueeze(3).to_broadcast(hs), ALU.subtract))
                v.sem_inc(s_free, 1)
                v.sem_inc(tau_s, 1)
                if not isinstance(n, int) or n > 0:
                    v.wait_ge(pt_ps, n * 4)
                for i in range(SHORT):
                    newton(step, i)
                    if i == 0 and isinstance(n, int):
                        v.wait_ge(ld_vec, 16)
                        layernorm(LN_C)
                above(step, VH)
                step(v.tensor_reduce(tot[:, 0:VH], P3[:, 0:VH], AX.X, ALU.add))
                v.wait_ge(relu_s, n * (SHORT + 1) + (SHORT + 1))
                step(v.tensor_scalar(f, tot[:], -1.0, None, ALU.add))
                step(v.tensor_tensor(avg, f, cnt, ALU.mult))
                step(v.tensor_tensor(f, f, f, ALU.mult))
                step(v.reduce_max(bad[:], f, AX.X))
                step(v.tensor_scalar(bad[:], bad[:], RESIDUAL ** 2, None, ALU.is_gt))
                v.sem_inc(bad_s, 1)
                step(v.tensor_tensor(P3, P3, avg.unsqueeze(2).to_broadcast([128, 16, SK]), ALU.subtract))
                step(v.tensor_scalar(pr[:, 0:1232], pr[:, 0:1232], 0.0, None, ALU.max))
                v.wait_ge(bad_ps, n + 1)
                step(v.tensor_copy(bad_i[:], ps[0:1, 4, 0:1]))
                settled(v)
                left = v.value_load(bad_i[0:1, 0:1], min_val=0, max_val=128)
                at = step.mark()
                with v.If(left > 0):
                    again = step.within(at)
                    again(v.memset(ntau, 1.0))
                    settled(v)
                    with v.Fori(0, LONG) as i:
                        turn = step.within(at + 1, i, 8)
                        newton_alone(turn)
                    again = step.within(at + 1 + 8 * LONG)
                    above(again, 16)
                    settled(v)
                with v.Else():
                    v.sem_inc(dch, 1 + 8 * LONG + 2)
                step.skip(1 + 8 * LONG + 2)
                v.sem_inc(p_s, 1)

            def tables():
                v.wait_ge(ld_t, 16 * len(TABLES))
                step = Steps()
                step(v.tensor_scalar(bias1[:], pad[:], NEG, None, ALU.mult))
                step(v.tensor_tensor(bias1[:], bias1[:], fside[:].unsqueeze(1).to_broadcast([128, B, SK]), ALU.add))
                step(v.tensor_scalar(bias3[:, :, 0:SK], keep[:], -1.0, -NEG, ALU.add, ALU.mult))
                step(v.memset(bias3[:, :, SK:SK + S], 0.0))
                v.wait_ge(tanh_s, 1)
                step(v.tensor_tensor(tg[:, GX + 2:GX + 3], tg[:, GX + 2:GX + 3], tg[:, GATE2:GATE2 + 1], ALU.mult))
                step.end()

            def turned_outs(l, n):
                C = QC[l]
                v.wait_ge(pv_ps, n + 1)
                v.tensor_copy(ot_sb[:, 0:C * 128], ps[:, 4:4 + C // 4, :]).then_inc(ot_s, 1)

            def attention(l):
                n0 = B * l
                per = {0: 4 + 7 * SHORT + 2 + 8 + 1 + 8 * LONG + 2 + 1, 2: 4}.get(l, 4)
                step = Steps()
                if l == 0:
                    sparsemax(n0, step)
                else:
                    softmax(l, n0, 0, step)
                step.end()
                if l == 0:
                    tables()
                with v.Fori(0, B - 1) as b:
                    step = Steps(b, per)
                    if l == 0:
                        sparsemax(b + (n0 + 1), step)
                    else:
                        softmax(l, b + (n0 + 1), b + 1, step)
                if l >= 2:
                    turned_outs(l, n0 + B - 1)
                step.end(B - 1)

            def route(l):
                step = Steps()
                n = E - 1 if l == 0 else E
                L, X, Pb, oh1, oh2, w1, w2, val = (rt[:, i, :, 0:n] for i in range(8))
                res = rt[:, 9]
                m1, m2, s1, s2, r1 = (rc[:, i, :] for i in range(5))
                bc = [128, B, n]
                rv = rev[:, 0:n].unsqueeze(1).to_broadcast(bc)

                def spread(c):
                    return c.unsqueeze(2).to_broadcast(bc)

                def first_max(values, m, oh):
                    step(v.reduce_max(m, values, AX.X))
                    step(v.tensor_tensor(oh, values, spread(m), ALU.is_equal))
                    step(v.tensor_tensor(oh, oh, rv, ALU.mult))
                    step(v.reduce_max(s2, oh, AX.X))
                    step(v.tensor_tensor(oh, rv, spread(s2), ALU.is_equal))

                v.wait_ge(lg_ps, l + 1)
                logits = ps[:, 7, 0:B * E].rearrange("p (t e) -> p t e", e=E)
                if l in (0, 3):
                    rb = row[:, (RB0 if l == 0 else RB3):][:, 0:E].unsqueeze(1).to_broadcast([128, B, E])
                    step(v.tensor_tensor(rt[:, 0], logits, rb, ALU.add))
                    if l == 0:
                        v.sem_inc(rx_in, 1)
                        v.wait_ge(rx_s, 1)
                        step(v.tensor_scalar(w1, X, 1.0, None, ALU.add))
                        step(v.reciprocal(val, w1))
                    else:
                        step(v.tensor_copy(val, L))
                else:
                    step(v.tensor_copy(val, logits))
                first_max(val, m1, oh1)
                if l:
                    step(v.tensor_tensor(L, val, spread(m1), ALU.subtract))
                    v.sem_inc(rx_in, 1)
                if l != 1:
                    step(v.scalar_tensor_tensor(out=w2, in0=oh1, scalar=NEG, in1=val, op0=ALU.mult, op1=ALU.add))
                    first_max(w2, m2, oh2)
                    step(v.tensor_tensor(oh2, oh1, oh2, ALU.add))
                if l:
                    v.wait_ge(rx_s, l + 1)
                if l == 1:
                    step(v.tensor_reduce(s1, X, AX.X, ALU.add))
                    step(v.reciprocal(r1, s1))
                    step(v.scalar_tensor_tensor(out=res, in0=oh1, scalar=2.0, in1=spread(r1), op0=ALU.mult, op1=ALU.mult))
                    step(v.memset(res[:, :, E - 1:E], 1.0))
                    parts(l, step)
                    return
                src = val if l == 0 else X
                if l == 2:
                    step(v.tensor_reduce(s1, X, AX.X, ALU.add))
                    step(v.reciprocal(r1, s1))
                    step(v.tensor_tensor(Pb, X, spread(r1), ALU.mult))
                    src = Pb
                step(v.tensor_tensor(w1, src, oh2, ALU.mult))
                step(v.tensor_reduce(s1, w1, AX.X, ALU.add))
                if l == 2:
                    step(v.tensor_scalar(s1, s1, 1e-9, None, ALU.add))
                step(v.reciprocal(r1, s1))
                if l == 0:
                    step(v.memset(res[:, :, E - 1:E], 1.0))
                step(v.tensor_tensor(res[:, :, 0:n], w1, spread(r1), ALU.mult))
                parts(l, step)

            def parts(l, step):
                c, r1, r2 = rt[:, 9], rt[:, 10], rt[:, 11]
                step(v.tensor_copy(c3[:, :, 0:E], c))
                step(v.tensor_tensor(r1, c, c3[:, :, 0:E], ALU.subtract))
                step(v.tensor_copy(c3[:, :, E:2 * E], r1))
                step(v.tensor_tensor(r2, r1, c3[:, :, E:2 * E], ALU.subtract))
                step(v.tensor_copy(c3[:, :, 2 * E:3 * E], r2))
                v.sem_inc(c3_s, 1)
                v.wait_ge(ct_ps, CT0[l] + 1)
                v.tensor_copy(cT3[0:32, :], ps[0:32, 5, :].bitcast(BF16)).then_inc(ct_s, 1)
                if l >= 2:
                    v.wait_ge(ct_ps, CT0[l] + 2)
                    v.tensor_copy(cT[:].rearrange("e (u n) -> e u n", u=2), ps[0:E, 6:8, :]).then_inc(ct_s, 1)
                step.end()

            def experts(l):
                n = NC[l]
                for h in range(2):
                    hs = slice(h * HALF, h * HALF + HALF)
                    v.wait_ge(xh_s, 2 * l + h + 1)
                    v.tensor_tensor(xl[:, hs], xn[:, hs], xh[:, hs].bitcast(F32), ALU.subtract).then_inc(xl_s, 1)
                route(l)
                v.wait_ge(cb_ps, l + 1)
                NU = 4 * n

                def hidden(j, i):
                    if i == NU:
                        j, i = j + 1, 0
                    u = j * NU + (U0[l] + i)
                    p, h, c = i // (2 * n), i // n % 2, i % n
                    act_ = gs[:, i % 2, :]
                    v.wait_ge(g_s, u + 1)
                    if GATED[l]:
                        act_ = tu[:, i % 2, :]
                        v.wait_ge(h_s, u + 1)
                        up = ps[:, 2 + i % 2, :]
                        if l == 2:
                            if not isinstance(j, int):
                                settled(v)
                            c0 = UB2 + p * n + c
                            ub = v1(j * (2 * n) + c0) if isinstance(j, int) else vec[:, bass.ds(j * (2 * n) + c0, 1)]
                            v.scalar_tensor_tensor(out=act_, in0=up, scalar=ub, in1=gs[:, i % 2, :],
                                                   op0=ALU.add, op1=ALU.mult).then_inc(tu_s, 1)
                        else:
                            v.tensor_tensor(act_, up, gs[:, i % 2, :], ALU.mult).then_inc(tu_s, 1)
                        v.wait_ge(tu_s, u + 3)
                    v.wait_ge(hl_s, u + 1)
                    v.tensor_tensor(hb[:, i % 4, :], act_, ps[:, 6 + h, :], ALU.mult).then_inc(h_s, 1)

                def low(j, i):
                    u = j * NU + (U0[l] + i)
                    v.wait_ge(hh_s, u + 1)
                    v.tensor_tensor(hl[:, i % 4, :], hb[:, i % 4, :], hh[:, i % 4, :].bitcast(F32), ALU.subtract).then_inc(hl_s, 1)

                def update(h):
                    v.wait_ge(acc_ps, 2 * l + h + 1)
                    xs = x[:, h * HALF:h * HALF + HALF]
                    v.scalar_tensor_tensor(out=xs, in0=ps[:, 4 + h, :], scalar=tg[:, GF + l:GF + l + 1], in1=xs,
                                           op0=ALU.mult, op1=ALU.add).then_inc(x_rdy, 1)

                def pair(j, last):
                    for i in range(NU):
                        if i + 1 < NU or not last:
                            hidden(j, i + 1)
                        low(j, i)
                        if last and i == 3 * n + 1:
                            update(0)
                    if last:
                        update(1)

                hidden(0, 0)
                with v.Fori(0, E // 2 - 1) as j:
                    pair(j, False)
                pair(E // 2 - 1, True)

            def residual(l, h):
                if l < 3:
                    v.wait_ge(y_s, B * l + (h + 1) * B // 2 + 1)
                else:
                    ln_done(v, LN_Y + h)
                xs, ys = x[:, h * HALF:h * HALF + HALF], y[:, h * HALF:h * HALF + HALF]
                v.scalar_tensor_tensor(out=xs, in0=ys, scalar=tg[:, GX + l:GX + l + 1], in1=xs,
                                       op0=ALU.mult, op1=ALU.add).then_inc(x_rdy, 1)

            v.memset(c3[:], 0.0).then_inc(init_v, 1)
            v.memset(cT3[:], 0.0).then_inc(init_v, 1)
            v.memset(zeros[:], 0.0).then_inc(init_v, 1)
            v.memset(eps[:], 1e-5).then_inc(init_v, 1)
            v.wait_ge(init_v, 4)
            for l in range(4):
                layernorm(LN_A[l])
                if l in LN_A2:
                    layernorm(LN_A2[l])
                attention(l)
                for h in range(2):
                    if l == 3:
                        ln_unit(LN_Y + h)
                    residual(l, h)
                layernorm(LN_F[l])
                experts(l)


def kernel(**inputs):
    import numpy as np
    import concourse.bacc as bacc
    from concourse.bass_utils import run_bass_kernel_spmd as run

    i = {k: np.asarray(v) for k, v in inputs.items()}
    f = np.float32

    def rows(v, n=None):
        v = v.reshape(1, -1)
        return np.broadcast_to(v, (128, v.shape[1]))

    const = np.zeros((128, NCONST), f)
    const[:, IDENT:IDENT + 128] = np.eye(128)
    const[:, CENTER:CENTER + 128] = np.eye(128) - 1.0 / D
    const[:, MEAN:MEAN + 128] = 1.0 / D
    const[np.arange(128), HMASK + np.arange(128) // 8] = 8 ** -0.5
    const[:, ONES] = 1.0
    const[:, REV:REV + E] = E - np.arange(E)

    import ml_dtypes
    sel = np.zeros((128, E, 128), ml_dtypes.bfloat16)
    for e in range(E):
        sel[[e, E + e, 2 * E + e], e] = 1
    identb = np.eye(128).astype(ml_dtypes.bfloat16)

    vecs = [i[f"L{l}_xattn_{n}"] for l in (0, 1) for n in ("bq", "bk", "bv", "bo")]
    vecs += [i["L2_xattn_" + n] for n in ("ln_gamma", "ln_beta", "b_out")]
    vecs += [i["L3_xattn_" + n] for n in ("ln_x_g", "ln_x_b", "ln_l_g", "ln_l_b", "ln_o_g", "ln_o_b")]
    vec = np.concatenate([np.stack(vecs, 1), i["L2_ffn_gate_b"].reshape(-1, 128).T, i["L2_ffn_up_b"].reshape(-1, 128).T,
                          i["L3_ffn_b1"].reshape(-1, 128).T], 1)
    pad1 = np.zeros(1, f)
    row = rows(np.concatenate([i["g_xattn"], i["g_ffn"], i["L2_xattn_gate"], i["L0_ffn_routing_bias"], pad1, i["L3_ffn_b_router"]]))
    rw = np.stack([np.concatenate([i["L0_ffn_router_w"], np.zeros((D, 1), f)], 1), i["L1_ffn_router_w"], i["L2_ffn_router_w"].T,
                   i["L3_ffn_W_router"]], 1)
    zero = np.zeros((E, D), f)
    bd = np.stack([zero, zero, i["L2_ffn_down_b"], i["L3_ffn_b2"]], 1)

    def chunks(w):
        return w.reshape(-1, 128, D).transpose(1, 0, 2).reshape(128, -1)

    p = "L0_xattn_"
    wa0 = np.concatenate([i[p + "Wq"], i[p + "Wk"], i[p + "Wv"], i[p + "Wo"]], 1)
    p = "L1_xattn_"
    wa1 = np.concatenate([i[p + "Wq"].T, i[p + "Wk"].T, i[p + "Wv"].T, i[p + "Wo"].T], 1)
    p = "L2_xattn_"
    wa2 = np.concatenate([i[p + "w_q"], i[p + "w_kv"], chunks(i[p + "w_out"])], 1)
    p = "L3_xattn_"
    wa3 = np.concatenate([i[p + "Wq"], i[p + "Wkv"], chunks(i[p + "Wo"])], 1)

    def expert_w(ups, down):
        H = down.shape[1]
        HP = -(-H // 128) * 128
        ups = [np.pad(u, ((0, 0), (0, 0), (0, HP - H))) for u in ups]
        down = np.pad(down, ((0, 0), (0, HP - H), (0, 0))).reshape(E, -1, 128, D).transpose(0, 2, 1, 3).reshape(E, 128, -1)
        return np.concatenate(ups + [down], 2)

    def with_shared(r, s):
        return np.concatenate([r, s[None]], 0)

    w0 = expert_w([with_shared(i["L0_ffn_routed_gate"], i["L0_ffn_shared_gate"]), with_shared(i["L0_ffn_routed_up"], i["L0_ffn_shared_up"])],
                  with_shared(i["L0_ffn_routed_down"], i["L0_ffn_shared_down"]))
    w1 = expert_w([with_shared(i["L1_ffn_gate_w"], i["L1_ffn_shared_gate_w"]), with_shared(i["L1_ffn_up_w"], i["L1_ffn_shared_up_w"])],
                  with_shared(i["L1_ffn_down_w"], i["L1_ffn_shared_down_w"]))
    w2 = expert_w([i["L2_ffn_gate_w"], i["L2_ffn_up_w"]], i["L2_ffn_down_w"])
    w3 = expert_w([i["L3_ffn_W1"]], i["L3_ffn_W2"])

    arrays = {
        "x": i["x"].transpose(2, 0, 1).reshape(D, T), "cx": i["ctx_1024"].transpose(2, 0, 1), "sel": sel, "identb": identb, "const": const, "vec": vec, "row": row,
        "rw": rw, "bd": bd, "fside": i["fside_SxS2_0"],
        "pad": rows(i["mask_BxS2_bf0"]).reshape(128, B, SK),
        "keep": rows(i["mask_BxS2_bk1"]).reshape(128, B, SK),
        "wa0": wa0, "wa1": wa1, "wa2": wa2, "wa3": wa3, "w0": w0, "w1": w1, "w2": w2, "w3": w3,
    }
    nc = bacc.Bacc("TRN2", target_bir_lowering=False, num_devices=1)
    sent, aps = {}, {}
    for name, v in arrays.items():
        v = np.ascontiguousarray(v)
        sent["in_" + name] = v
        aps[name] = nc.dram_tensor("in_" + name, v.shape, mybir.dt.from_np(v.dtype), kind="ExternalInput").ap()
    out = nc.dram_tensor("out_0", (D, T), F32, kind="ExternalOutput").ap()
    build(nc, aps, out)
    r = run(nc, [sent], core_ids=[0])
    return r.results[0]["out_0"].reshape(D, B, S).transpose(1, 2, 0)
```
